# Optimizing a Trainium2 kernel written in Bass

```python
import numpy as np
import jax
import jax.numpy as jnp

def _softmax(x, axis=-1):
    return jax.nn.softmax(x, axis=axis)

def _gelu(x):
    return jax.nn.gelu(x, approximate=True)

def _silu(x):
    return jax.nn.silu(x)

def _sigmoid(x):
    return jax.nn.sigmoid(x)

def _layernorm(x, axis=-1, eps=1e-05):
    m = jnp.mean(x, axis=axis, keepdims=True)
    v = jnp.var(x, axis=axis, keepdims=True)
    return (x - m) / jnp.sqrt(v + eps)

def _scatter_add(tgt, idx, src, axis=0):
    return tgt.at[idx].add(src)

def _segment_sum(src, seg, n):
    return jax.ops.segment_sum(src, seg, n)
kernel_name = 'mk_xattn_seq_d4_seqx_r4_0947b1'

def setup_inputs(seed: int=0):
    np.random.seed(seed)
    _w = jnp.asarray

    def _rec_inputs():
        import jax
        import jax.numpy as jnp
        _rk = jax.random.key(seed)
        x = -0.0002928 + 1 * jax.random.normal(jax.random.fold_in(_rk, 1), (4, 512, 256), jnp.float32)
        _lenS = 512 - jax.random.randint(jax.random.fold_in(_rk, 7), (4,), 0, max(1, 512 // 4) + 1, jnp.int32)
        _lenS2 = 512 - jax.random.randint(jax.random.fold_in(_rk, 8), (4,), 0, max(1, 512 // 4) + 1, jnp.int32)
        _ctx_1024P = jax.random.normal(jax.random.fold_in(_rk, 11), (4, 16, 256), jnp.float32)
        _ctx_1024c = jax.random.dirichlet(jax.random.fold_in(_rk, 511), 0.3 * jnp.ones((16,), jnp.float32), (4, 512))
        _ctx_1024t = jnp.einsum('bsk,bkd->bsd', _ctx_1024c, _ctx_1024P)
        _ctx_1024t = _ctx_1024t * jax.lax.rsqrt(jnp.mean(jnp.square(_ctx_1024t)) + 1e-12) * 0.953939
        ctx_1024 = -1.39393e-06 + 0.999914 * (_ctx_1024t + 0.3 * jax.random.normal(jax.random.fold_in(_rk, 611), (4, 512, 256), jnp.float32))
        _validS = jnp.arange(512)[None, :] < _lenS[:, None]
        _validS2 = jnp.arange(512)[None, :] < _lenS2[:, None]
        _causal = jnp.tril(jnp.ones((512, 512), dtype=bool))
        mask_BxSxS_ik0 = jnp.where(jnp.broadcast_to(_validS[:, None, :], (4, 512, 512)), 0, 1).astype(jnp.int32)
        mask_BxSxS2_if1 = jnp.where(jnp.ones((4, 512, 512), dtype=bool), 1, 0).astype(jnp.int32)
        mask_BxSxS2_ik0 = jnp.where(jnp.broadcast_to(_validS2[:, None, :], (4, 512, 512)), 0, 1).astype(jnp.int32)
        return (x, ctx_1024, mask_BxSxS_ik0, mask_BxSxS2_if1, mask_BxSxS2_ik0)
    x, ctx_1024, mask_BxSxS_ik0, mask_BxSxS2_if1, mask_BxSxS2_ik0 = _rec_inputs()

    def _L0_xattn_setup():
        import jax, jax.numpy as jnp
        import numpy as np
        EPS = 1e-05

        def _layernorm(x, g, b):
            m = jnp.mean(x, axis=-1, keepdims=True)
            v = jnp.mean((x - m) ** 2, axis=-1, keepdims=True)
            return (x - m) / jnp.sqrt(v + EPS) * g + b

        def _mha(x, kv, Wq, Wk, Wv, mask, causal):
            m = mask[:, None]
            Q = jnp.einsum('bsd,hdk->bhsk', x, Wq) * m
            K = jnp.einsum('bsd,hdk->bhsk', kv, Wk) * m
            V = jnp.einsum('bsd,hdk->bhsk', kv, Wv) * m
            energy = jnp.einsum('bhsk,bhtk->bhst', Q, K)
            S = energy.shape[-1]
            lengths = jnp.sum(energy[:, :, 0, :] != 0, axis=-1)
            cols = jnp.arange(S)
            energy = jnp.where(cols[None, None, None, :] >= lengths[:, :, None, None], -jnp.inf, energy)
            if causal:
                energy = jnp.where(cols[None, :] > cols[:, None], -jnp.inf, energy)
            dk = Wq.shape[-1]
            score = jax.nn.softmax(energy / jnp.sqrt(jnp.asarray(dk, energy.dtype)), axis=-1)
            out = jnp.einsum('bhst,bhtk->bhsk', score, V) * m
            B, H, Sx, dkk = out.shape
            return out.transpose(0, 2, 1, 3).reshape(B, Sx, H * dkk)
        key = jax.random.key(seed)
        ks = jax.random.split(key, 20)
        B, S, D, H = (2, 512, 256, 16)
        dk = D // H
        sd = 0.02
        inp = {'x': jax.random.normal(ks[0], (B, S, D), jnp.float32), 'context': jax.random.normal(ks[1], (B, S, D), jnp.float32), 'Wq1': jax.random.normal(ks[2], (H, D, dk), jnp.float32) * sd, 'Wk1': jax.random.normal(ks[3], (H, D, dk), jnp.float32) * sd, 'Wv1': jax.random.normal(ks[4], (H, D, dk), jnp.float32) * sd, 'Wq2': jax.random.normal(ks[5], (H, D, dk), jnp.float32) * sd, 'Wk2': jax.random.normal(ks[6], (H, D, dk), jnp.float32) * sd, 'Wv2': jax.random.normal(ks[7], (H, D, dk), jnp.float32) * sd, 'ln1_g': jnp.ones((D,), jnp.float32), 'ln1_b': jnp.zeros((D,), jnp.float32), 'ln2_g': jnp.ones((D,), jnp.float32), 'ln2_b': jnp.zeros((D,), jnp.float32), 'ln3_g': jnp.ones((D,), jnp.float32), 'ln3_b': jnp.zeros((D,), jnp.float32), 'fc1_w': jax.random.normal(ks[8], (D, D), jnp.float32) * sd, 'fc1_b': jnp.zeros((D,), jnp.float32), 'fc2_w': jax.random.normal(ks[9], (D, D), jnp.float32) * sd, 'fc2_b': jnp.zeros((D,), jnp.float32)}
        return inp
    _L0_xattn_all = _L0_xattn_setup()
    _L0_xattn_in = {k: v for k, v in _L0_xattn_all.items() if k in ('Wq1', 'Wk1', 'Wv1', 'Wq2', 'Wk2', 'Wv2', 'ln1_g', 'ln1_b', 'ln2_g', 'ln2_b', 'ln3_g', 'ln3_b', 'fc1_w', 'fc1_b', 'fc2_w', 'fc2_b')}
    del _L0_xattn_all

    def _L1_xattn_setup():
        import jax, jax.numpy as jnp
        import numpy as np
        B, T, S_ENC, D, H, E, K = (4, 256, 64, 256, 16, 8, 2)
        DK = D // H
        HID = 4 * D
        NEG = -65504.0
        EPS = 1e-05

        def rmsnorm(x, w):
            return w * (x * jax.lax.rsqrt(jnp.mean(x * x, axis=-1, keepdims=True) + EPS))

        def mha(xq, xk, xv, mask, wq, wk, wv, wo):
            q = jnp.einsum('bsd,ed->bse', xq, wq).reshape(xq.shape[0], -1, H, DK).transpose(0, 2, 1, 3)
            k = jnp.einsum('bsd,ed->bse', xk, wk).reshape(xk.shape[0], -1, H, DK).transpose(0, 2, 1, 3)
            v = jnp.einsum('bsd,ed->bse', xv, wv).reshape(xv.shape[0], -1, H, DK).transpose(0, 2, 1, 3)
            scores = jnp.einsum('bhqd,bhkd->bhqk', q, k) / jnp.sqrt(jnp.float32(DK))
            scores = jnp.where(mask[:, None, :, :] == 0, NEG, scores)
            attn = jax.nn.softmax(scores, axis=-1)
            out = jnp.einsum('bhqk,bhkd->bhqd', attn, v)
            out = out.transpose(0, 2, 1, 3).reshape(xq.shape[0], -1, D)
            return jnp.einsum('bsd,ed->bse', out, wo)

        def moe_ffn(x, gate_w, exp_w1, exp_w2, sh_w1, sh_w2):
            b, s, d = x.shape
            xf = x.reshape(-1, d)
            sh = jnp.einsum('nd,hd->nh', xf, sh_w1)
            sh = jax.nn.silu(sh)
            sh = jnp.einsum('nh,dh->nd', sh, sh_w2)
            logits = jnp.einsum('nd,ed->ne', xf, gate_w)
            topk_vals, topk_idx = jax.lax.top_k(logits, K)
            topk_gates = jax.nn.softmax(topk_vals, axis=-1)
            n = xf.shape[0]
            gates = jnp.zeros((n, E), dtype=xf.dtype).at[jnp.arange(n)[:, None], topk_idx].set(topk_gates)
            h = jnp.einsum('nd,ehd->neh', xf, exp_w1)
            h = jax.nn.silu(h)
            eo = jnp.einsum('neh,edh->ned', h, exp_w2)
            sel = jnp.einsum('ned,ne->nd', eo, gates)
            return (sh + sel).reshape(b, s, d)
        key = jax.random.key(seed)
        ks = jax.random.split(key, 16)
        sd = 1.0 / np.sqrt(D)
        inp = {'x': jax.random.normal(ks[0], (B, T, D), jnp.float32), 'encoder_output': jax.random.normal(ks[1], (B, S_ENC, D), jnp.float32), 'tgt_mask': jnp.tril(jnp.ones((T, T), jnp.int32))[None].repeat(B, 0), 'src_mask': jnp.ones((B, T, S_ENC), jnp.int32), 'norm1_w': jnp.ones((D,), jnp.float32), 'norm2_w': jnp.ones((D,), jnp.float32), 'norm3_w': jnp.ones((D,), jnp.float32), 'sa_wq': jax.random.normal(ks[2], (D, D), jnp.float32) * sd, 'sa_wk': jax.random.normal(ks[3], (D, D), jnp.float32) * sd, 'sa_wv': jax.random.normal(ks[4], (D, D), jnp.float32) * sd, 'sa_wo': jax.random.normal(ks[5], (D, D), jnp.float32) * sd, 'ca_wq': jax.random.normal(ks[6], (D, D), jnp.float32) * sd, 'ca_wk': jax.random.normal(ks[7], (D, D), jnp.float32) * sd, 'ca_wv': jax.random.normal(ks[8], (D, D), jnp.float32) * sd, 'ca_wo': jax.random.normal(ks[9], (D, D), jnp.float32) * sd, 'gate_w': jax.random.normal(ks[10], (E, D), jnp.float32) * 0.02, 'exp_w1': jax.random.normal(ks[11], (E, HID, D), jnp.float32) * sd, 'exp_w2': jax.random.normal(ks[12], (E, D, HID), jnp.float32) / np.sqrt(HID), 'sh_w1': jax.random.normal(ks[13], (HID, D), jnp.float32) * sd, 'sh_w2': jax.random.normal(ks[14], (D, HID), jnp.float32) / np.sqrt(HID)}
        return inp
    _L1_xattn_all = _L1_xattn_setup()
    _L1_xattn_in = {k: v for k, v in _L1_xattn_all.items() if k in ('norm1_w', 'norm2_w', 'norm3_w', 'sa_wq', 'sa_wk', 'sa_wv', 'sa_wo', 'ca_wq', 'ca_wk', 'ca_wv', 'ca_wo', 'gate_w', 'exp_w1', 'exp_w2', 'sh_w1', 'sh_w2')}
    del _L1_xattn_all

    def _L2_xattn_setup():
        import jax, jax.numpy as jnp
        import numpy as np
        B, S, D, H, DFF = (2, 512, 256, 16, 1024)
        DK = D // H
        LN_EPS = 1e-05

        def _mha(q, k, v, mask, wq, bq, wk, bk, wv, bv, wo, bo):
            b, sq, _ = q.shape
            sk = k.shape[1]
            Q = (q @ wq + bq).reshape(b, sq, H, DK).transpose(0, 2, 1, 3)
            K = (k @ wk + bk).reshape(b, sk, H, DK).transpose(0, 2, 1, 3)
            V = (v @ wv + bv).reshape(b, sk, H, DK).transpose(0, 2, 1, 3)
            scores = jnp.einsum('bhqd,bhkd->bhqk', Q, K) / np.float32(np.sqrt(DK))
            if mask is not None:
                scores = jnp.where(mask[:, None, :, :] == 0, jnp.float32(-1e+20), scores)
            A = jax.nn.softmax(scores, axis=-1)
            out = jnp.einsum('bhqk,bhkd->bhqd', A, V).transpose(0, 2, 1, 3).reshape(b, sq, D)
            return out @ wo + bo

        def _ln(x, g, b):
            m = jnp.mean(x, axis=-1, keepdims=True)
            v = jnp.var(x, axis=-1, keepdims=True)
            return (x - m) * jax.lax.rsqrt(v + LN_EPS) * g + b
        key = jax.random.key(seed)
        ks = jax.random.split(key, 32)
        ki = iter(range(32))

        def w(shape, scale=0.02):
            return (jax.random.normal(ks[next(ki)], shape, jnp.float32) * scale).astype(jnp.float32)
        inp = {}
        inp['x'] = jax.random.normal(ks[next(ki)], (B, S, D), jnp.float32)
        inp['enc_output'] = jax.random.normal(ks[next(ki)], (B, S, D), jnp.float32)
        causal = jnp.tril(jnp.ones((S, S), jnp.int32))
        inp['tgt_mask'] = jnp.broadcast_to(causal, (B, S, S))
        inp['memory_mask'] = jnp.ones((B, S, S), jnp.int32)
        for p in ('sa', 'ca'):
            for n in ('q', 'k', 'v', 'o'):
                inp[f'{p}_w{n}'] = w((D, D))
                inp[f'{p}_b{n}'] = jnp.zeros((D,), jnp.float32)
        inp['ff_w1'] = w((D, DFF))
        inp['ff_b1'] = jnp.zeros((DFF,), jnp.float32)
        inp['ff_w2'] = w((DFF, D))
        inp['ff_b2'] = jnp.zeros((D,), jnp.float32)
        for i in (1, 2, 3):
            inp[f'ln{i}_g'] = jnp.ones((D,), jnp.float32)
            inp[f'ln{i}_b'] = jnp.zeros((D,), jnp.float32)
        return inp
    _L2_xattn_all = _L2_xattn_setup()
    _L2_xattn_in = {k: v for k, v in _L2_xattn_all.items() if k in ('sa_wq', 'sa_bq', 'sa_wk', 'sa_bk', 'sa_wv', 'sa_bv', 'sa_wo', 'sa_bo', 'ca_wq', 'ca_bq', 'ca_wk', 'ca_bk', 'ca_wv', 'ca_bv', 'ca_wo', 'ca_bo', 'ff_w1', 'ff_b1', 'ff_w2', 'ff_b2', 'ln1_g', 'ln1_b', 'ln2_g', 'ln2_b', 'ln3_g', 'ln3_b')}
    del _L2_xattn_all

    def _L3_xattn_setup():
        import jax, jax.numpy as jnp
        import numpy as np
        D_MODEL = 256
        NUM_HEADS = 8
        D_K = D_MODEL // NUM_HEADS
        NEG_INF = -1000000000.0
        EPS = 1e-06

        def _split_heads(x, B, S):
            return x.reshape(B, S, NUM_HEADS, D_K).transpose(0, 2, 1, 3)
        key = jax.random.key(seed)
        ks = jax.random.split(key, 10)
        B, S = (4, 512)
        scale = 1.0 / np.sqrt(D_MODEL)
        return {'queries': jax.random.normal(ks[0], (B, S, D_MODEL), jnp.float32), 'keys': jax.random.normal(ks[1], (B, S, D_MODEL), jnp.float32), 'values': jax.random.normal(ks[2], (B, S, D_MODEL), jnp.float32), 'Wq': jax.random.normal(ks[3], (D_MODEL, D_MODEL), jnp.float32) * scale, 'bq': jnp.zeros((D_MODEL,), jnp.float32), 'Wk': jax.random.normal(ks[4], (D_MODEL, D_MODEL), jnp.float32) * scale, 'bk': jnp.zeros((D_MODEL,), jnp.float32), 'Wv': jax.random.normal(ks[5], (D_MODEL, D_MODEL), jnp.float32) * scale, 'bv': jnp.zeros((D_MODEL,), jnp.float32), 'gamma': jnp.ones((D_MODEL,), jnp.float32), 'beta': jnp.zeros((D_MODEL,), jnp.float32)}
    _L3_xattn_all = _L3_xattn_setup()
    _L3_xattn_in = {k: v for k, v in _L3_xattn_all.items() if k in ('Wq', 'bq', 'Wk', 'bk', 'Wv', 'bv', 'gamma', 'beta')}
    del _L3_xattn_all
    return {'x': x, 'ctx_1024': ctx_1024, 'mask_BxSxS_ik0': mask_BxSxS_ik0, 'mask_BxSxS2_if1': mask_BxSxS2_if1, 'mask_BxSxS2_ik0': mask_BxSxS2_ik0, 'L0_xattn_Wq1': _L0_xattn_in['Wq1'], 'L0_xattn_Wk1': _L0_xattn_in['Wk1'], 'L0_xattn_Wv1': _L0_xattn_in['Wv1'], 'L0_xattn_Wq2': _L0_xattn_in['Wq2'], 'L0_xattn_Wk2': _L0_xattn_in['Wk2'], 'L0_xattn_Wv2': _L0_xattn_in['Wv2'], 'L0_xattn_ln1_g': _L0_xattn_in['ln1_g'], 'L0_xattn_ln1_b': _L0_xattn_in['ln1_b'], 'L0_xattn_ln2_g': _L0_xattn_in['ln2_g'], 'L0_xattn_ln2_b': _L0_xattn_in['ln2_b'], 'L0_xattn_ln3_g': _L0_xattn_in['ln3_g'], 'L0_xattn_ln3_b': _L0_xattn_in['ln3_b'], 'L0_xattn_fc1_w': _L0_xattn_in['fc1_w'], 'L0_xattn_fc1_b': _L0_xattn_in['fc1_b'], 'L0_xattn_fc2_w': _L0_xattn_in['fc2_w'], 'L0_xattn_fc2_b': _L0_xattn_in['fc2_b'], 'L1_xattn_norm1_w': _L1_xattn_in['norm1_w'], 'L1_xattn_norm2_w': _L1_xattn_in['norm2_w'], 'L1_xattn_norm3_w': _L1_xattn_in['norm3_w'], 'L1_xattn_sa_wq': _L1_xattn_in['sa_wq'], 'L1_xattn_sa_wk': _L1_xattn_in['sa_wk'], 'L1_xattn_sa_wv': _L1_xattn_in['sa_wv'], 'L1_xattn_sa_wo': _L1_xattn_in['sa_wo'], 'L1_xattn_ca_wq': _L1_xattn_in['ca_wq'], 'L1_xattn_ca_wk': _L1_xattn_in['ca_wk'], 'L1_xattn_ca_wv': _L1_xattn_in['ca_wv'], 'L1_xattn_ca_wo': _L1_xattn_in['ca_wo'], 'L1_xattn_gate_w': _L1_xattn_in['gate_w'], 'L1_xattn_exp_w1': _L1_xattn_in['exp_w1'], 'L1_xattn_exp_w2': _L1_xattn_in['exp_w2'], 'L1_xattn_sh_w1': _L1_xattn_in['sh_w1'], 'L1_xattn_sh_w2': _L1_xattn_in['sh_w2'], 'L2_xattn_sa_wq': _L2_xattn_in['sa_wq'], 'L2_xattn_sa_bq': _L2_xattn_in['sa_bq'], 'L2_xattn_sa_wk': _L2_xattn_in['sa_wk'], 'L2_xattn_sa_bk': _L2_xattn_in['sa_bk'], 'L2_xattn_sa_wv': _L2_xattn_in['sa_wv'], 'L2_xattn_sa_bv': _L2_xattn_in['sa_bv'], 'L2_xattn_sa_wo': _L2_xattn_in['sa_wo'], 'L2_xattn_sa_bo': _L2_xattn_in['sa_bo'], 'L2_xattn_ca_wq': _L2_xattn_in['ca_wq'], 'L2_xattn_ca_bq': _L2_xattn_in['ca_bq'], 'L2_xattn_ca_wk': _L2_xattn_in['ca_wk'], 'L2_xattn_ca_bk': _L2_xattn_in['ca_bk'], 'L2_xattn_ca_wv': _L2_xattn_in['ca_wv'], 'L2_xattn_ca_bv': _L2_xattn_in['ca_bv'], 'L2_xattn_ca_wo': _L2_xattn_in['ca_wo'], 'L2_xattn_ca_bo': _L2_xattn_in['ca_bo'], 'L2_xattn_ff_w1': _L2_xattn_in['ff_w1'], 'L2_xattn_ff_b1': _L2_xattn_in['ff_b1'], 'L2_xattn_ff_w2': _L2_xattn_in['ff_w2'], 'L2_xattn_ff_b2': _L2_xattn_in['ff_b2'], 'L2_xattn_ln1_g': _L2_xattn_in['ln1_g'], 'L2_xattn_ln1_b': _L2_xattn_in['ln1_b'], 'L2_xattn_ln2_g': _L2_xattn_in['ln2_g'], 'L2_xattn_ln2_b': _L2_xattn_in['ln2_b'], 'L2_xattn_ln3_g': _L2_xattn_in['ln3_g'], 'L2_xattn_ln3_b': _L2_xattn_in['ln3_b'], 'L3_xattn_Wq': _L3_xattn_in['Wq'], 'L3_xattn_bq': _L3_xattn_in['bq'], 'L3_xattn_Wk': _L3_xattn_in['Wk'], 'L3_xattn_bk': _L3_xattn_in['bk'], 'L3_xattn_Wv': _L3_xattn_in['Wv'], 'L3_xattn_bv': _L3_xattn_in['bv'], 'L3_xattn_gamma': _L3_xattn_in['gamma'], 'L3_xattn_beta': _L3_xattn_in['beta']}

def reference(x, ctx_1024, mask_BxSxS_ik0, mask_BxSxS2_if1, mask_BxSxS2_ik0, L0_xattn_Wq1, L0_xattn_Wk1, L0_xattn_Wv1, L0_xattn_Wq2, L0_xattn_Wk2, L0_xattn_Wv2, L0_xattn_ln1_g, L0_xattn_ln1_b, L0_xattn_ln2_g, L0_xattn_ln2_b, L0_xattn_ln3_g, L0_xattn_ln3_b, L0_xattn_fc1_w, L0_xattn_fc1_b, L0_xattn_fc2_w, L0_xattn_fc2_b, L1_xattn_norm1_w, L1_xattn_norm2_w, L1_xattn_norm3_w, L1_xattn_sa_wq, L1_xattn_sa_wk, L1_xattn_sa_wv, L1_xattn_sa_wo, L1_xattn_ca_wq, L1_xattn_ca_wk, L1_xattn_ca_wv, L1_xattn_ca_wo, L1_xattn_gate_w, L1_xattn_exp_w1, L1_xattn_exp_w2, L1_xattn_sh_w1, L1_xattn_sh_w2, L2_xattn_sa_wq, L2_xattn_sa_bq, L2_xattn_sa_wk, L2_xattn_sa_bk, L2_xattn_sa_wv, L2_xattn_sa_bv, L2_xattn_sa_wo, L2_xattn_sa_bo, L2_xattn_ca_wq, L2_xattn_ca_bq, L2_xattn_ca_wk, L2_xattn_ca_bk, L2_xattn_ca_wv, L2_xattn_ca_bv, L2_xattn_ca_wo, L2_xattn_ca_bo, L2_xattn_ff_w1, L2_xattn_ff_b1, L2_xattn_ff_w2, L2_xattn_ff_b2, L2_xattn_ln1_g, L2_xattn_ln1_b, L2_xattn_ln2_g, L2_xattn_ln2_b, L2_xattn_ln3_g, L2_xattn_ln3_b, L3_xattn_Wq, L3_xattn_bq, L3_xattn_Wk, L3_xattn_bk, L3_xattn_Wv, L3_xattn_bv, L3_xattn_gamma, L3_xattn_beta):
    import jax
    import jax.numpy as jnp

    def _L0_xattn_ref(x, context, Wq1, Wk1, Wv1, Wq2, Wk2, Wv2, ln1_g, ln1_b, ln2_g, ln2_b, ln3_g, ln3_b, fc1_w, fc1_b, fc2_w, fc2_b):
        import jax, jax.numpy as jnp
        import numpy as np
        EPS = 1e-05

        def _layernorm(x, g, b):
            m = jnp.mean(x, axis=-1, keepdims=True)
            v = jnp.mean((x - m) ** 2, axis=-1, keepdims=True)
            return (x - m) / jnp.sqrt(v + EPS) * g + b

        def _mha(x, kv, Wq, Wk, Wv, mask, causal):
            m = mask[:, None]
            Q = jnp.einsum('bsd,hdk->bhsk', x, Wq) * m
            K = jnp.einsum('bsd,hdk->bhsk', kv, Wk) * m
            V = jnp.einsum('bsd,hdk->bhsk', kv, Wv) * m
            energy = jnp.einsum('bhsk,bhtk->bhst', Q, K)
            S = energy.shape[-1]
            lengths = jnp.sum(energy[:, :, 0, :] != 0, axis=-1)
            cols = jnp.arange(S)
            energy = jnp.where(cols[None, None, None, :] >= lengths[:, :, None, None], -jnp.inf, energy)
            if causal:
                energy = jnp.where(cols[None, :] > cols[:, None], -jnp.inf, energy)
            dk = Wq.shape[-1]
            score = jax.nn.softmax(energy / jnp.sqrt(jnp.asarray(dk, energy.dtype)), axis=-1)
            out = jnp.einsum('bhst,bhtk->bhsk', score, V) * m
            B, H, Sx, dkk = out.shape
            return out.transpose(0, 2, 1, 3).reshape(B, Sx, H * dkk)
        mask0 = 1.0 - jnp.all(x == 0, axis=2, keepdims=True).astype(x.dtype)
        z = _mha(x, x, Wq1, Wk1, Wv1, mask0, causal=True)
        x1 = _layernorm(x + z, ln1_g, ln1_b)
        mask1 = 1.0 - jnp.all(x1 == 0, axis=2, keepdims=True).astype(x1.dtype)
        z = _mha(x1, context, Wq2, Wk2, Wv2, mask1, causal=False)
        x2 = _layernorm(x1 + z, ln2_g, ln2_b)
        z = jnp.maximum(x2 @ fc1_w.T + fc1_b, 0.0) * mask0
        z = (z @ fc2_w.T + fc2_b) * mask0
        return _layernorm(x2 + z, ln3_g, ln3_b)

    def _L1_xattn_ref(x, encoder_output, tgt_mask, src_mask, norm1_w, norm2_w, norm3_w, sa_wq, sa_wk, sa_wv, sa_wo, ca_wq, ca_wk, ca_wv, ca_wo, gate_w, exp_w1, exp_w2, sh_w1, sh_w2):
        import jax, jax.numpy as jnp
        import numpy as np
        B, T, S_ENC, D, H, E, K = (4, 256, 64, 256, 16, 8, 2)
        DK = D // H
        HID = 4 * D
        NEG = -65504.0
        EPS = 1e-05

        def rmsnorm(x, w):
            return w * (x * jax.lax.rsqrt(jnp.mean(x * x, axis=-1, keepdims=True) + EPS))

        def mha(xq, xk, xv, mask, wq, wk, wv, wo):
            q = jnp.einsum('bsd,ed->bse', xq, wq).reshape(xq.shape[0], -1, H, DK).transpose(0, 2, 1, 3)
            k = jnp.einsum('bsd,ed->bse', xk, wk).reshape(xk.shape[0], -1, H, DK).transpose(0, 2, 1, 3)
            v = jnp.einsum('bsd,ed->bse', xv, wv).reshape(xv.shape[0], -1, H, DK).transpose(0, 2, 1, 3)
            scores = jnp.einsum('bhqd,bhkd->bhqk', q, k) / jnp.sqrt(jnp.float32(DK))
            scores = jnp.where(mask[:, None, :, :] == 0, NEG, scores)
            attn = jax.nn.softmax(scores, axis=-1)
            out = jnp.einsum('bhqk,bhkd->bhqd', attn, v)
            out = out.transpose(0, 2, 1, 3).reshape(xq.shape[0], -1, D)
            return jnp.einsum('bsd,ed->bse', out, wo)

        def moe_ffn(x, gate_w, exp_w1, exp_w2, sh_w1, sh_w2):
            b, s, d = x.shape
            xf = x.reshape(-1, d)
            sh = jnp.einsum('nd,hd->nh', xf, sh_w1)
            sh = jax.nn.silu(sh)
            sh = jnp.einsum('nh,dh->nd', sh, sh_w2)
            logits = jnp.einsum('nd,ed->ne', xf, gate_w)
            topk_vals, topk_idx = jax.lax.top_k(logits, K)
            topk_gates = jax.nn.softmax(topk_vals, axis=-1)
            n = xf.shape[0]
            gates = jnp.zeros((n, E), dtype=xf.dtype).at[jnp.arange(n)[:, None], topk_idx].set(topk_gates)
            h = jnp.einsum('nd,ehd->neh', xf, exp_w1)
            h = jax.nn.silu(h)
            eo = jnp.einsum('neh,edh->ned', h, exp_w2)
            sel = jnp.einsum('ned,ne->nd', eo, gates)
            return (sh + sel).reshape(b, s, d)
        xn = rmsnorm(x, norm1_w)
        h = x + mha(xn, xn, xn, tgt_mask, sa_wq, sa_wk, sa_wv, sa_wo)
        hn = rmsnorm(h, norm2_w)
        h = h + mha(hn, encoder_output, encoder_output, src_mask, ca_wq, ca_wk, ca_wv, ca_wo)
        hn = rmsnorm(h, norm3_w)
        return h + moe_ffn(hn, gate_w, exp_w1, exp_w2, sh_w1, sh_w2)

    def _L2_xattn_ref(x, enc_output, tgt_mask, memory_mask, sa_wq, sa_bq, sa_wk, sa_bk, sa_wv, sa_bv, sa_wo, sa_bo, ca_wq, ca_bq, ca_wk, ca_bk, ca_wv, ca_bv, ca_wo, ca_bo, ff_w1, ff_b1, ff_w2, ff_b2, ln1_g, ln1_b, ln2_g, ln2_b, ln3_g, ln3_b):
        import jax, jax.numpy as jnp
        import numpy as np
        B, S, D, H, DFF = (2, 512, 256, 16, 1024)
        DK = D // H
        LN_EPS = 1e-05

        def _mha(q, k, v, mask, wq, bq, wk, bk, wv, bv, wo, bo):
            b, sq, _ = q.shape
            sk = k.shape[1]
            Q = (q @ wq + bq).reshape(b, sq, H, DK).transpose(0, 2, 1, 3)
            K = (k @ wk + bk).reshape(b, sk, H, DK).transpose(0, 2, 1, 3)
            V = (v @ wv + bv).reshape(b, sk, H, DK).transpose(0, 2, 1, 3)
            scores = jnp.einsum('bhqd,bhkd->bhqk', Q, K) / np.float32(np.sqrt(DK))
            if mask is not None:
                scores = jnp.where(mask[:, None, :, :] == 0, jnp.float32(-1e+20), scores)
            A = jax.nn.softmax(scores, axis=-1)
            out = jnp.einsum('bhqk,bhkd->bhqd', A, V).transpose(0, 2, 1, 3).reshape(b, sq, D)
            return out @ wo + bo

        def _ln(x, g, b):
            m = jnp.mean(x, axis=-1, keepdims=True)
            v = jnp.var(x, axis=-1, keepdims=True)
            return (x - m) * jax.lax.rsqrt(v + LN_EPS) * g + b
        sa = _mha(x, x, x, tgt_mask, sa_wq, sa_bq, sa_wk, sa_bk, sa_wv, sa_bv, sa_wo, sa_bo)
        x = _ln(x + sa, ln1_g, ln1_b)
        ca = _mha(x, enc_output, enc_output, memory_mask, ca_wq, ca_bq, ca_wk, ca_bk, ca_wv, ca_bv, ca_wo, ca_bo)
        x = _ln(x + ca, ln2_g, ln2_b)
        ff = jax.nn.relu(x @ ff_w1 + ff_b1) @ ff_w2 + ff_b2
        x = _ln(x + ff, ln3_g, ln3_b)
        return x

    def _L3_xattn_ref(queries, keys, values, Wq, bq, Wk, bk, Wv, bv, gamma, beta):
        import jax, jax.numpy as jnp
        import numpy as np
        D_MODEL = 256
        NUM_HEADS = 8
        D_K = D_MODEL // NUM_HEADS
        NEG_INF = -1000000000.0
        EPS = 1e-06

        def _split_heads(x, B, S):
            return x.reshape(B, S, NUM_HEADS, D_K).transpose(0, 2, 1, 3)
        B, S, _ = queries.shape
        Q = _split_heads(queries @ Wq + bq, B, S)
        K = _split_heads(keys @ Wk + bk, B, keys.shape[1])
        V = _split_heads(values @ Wv + bv, B, values.shape[1])
        scores = jnp.einsum('bhqd,bhkd->bhqk', Q, K) / jnp.sqrt(jnp.float32(D_K))
        Sk = scores.shape[-1]
        mask = jnp.tril(jnp.ones((scores.shape[-2], Sk), dtype=bool))
        scores = jnp.where(mask, scores, jnp.float32(NEG_INF))
        attn = jax.nn.softmax(scores, axis=-1)
        out = jnp.einsum('bhqk,bhkd->bhqd', attn, V)
        out = out.transpose(0, 2, 1, 3).reshape(B, S, D_MODEL)
        resid = out + queries
        mu = jnp.mean(resid, axis=-1, keepdims=True)
        var = jnp.var(resid, axis=-1, keepdims=True)
        normed = (resid - mu) / jnp.sqrt(var + EPS)
        return normed * gamma + beta
    x = _L0_xattn_ref(x, ctx_1024, L0_xattn_Wq1, L0_xattn_Wk1, L0_xattn_Wv1, L0_xattn_Wq2, L0_xattn_Wk2, L0_xattn_Wv2, L0_xattn_ln1_g, L0_xattn_ln1_b, L0_xattn_ln2_g, L0_xattn_ln2_b, L0_xattn_ln3_g, L0_xattn_ln3_b, L0_xattn_fc1_w, L0_xattn_fc1_b, L0_xattn_fc2_w, L0_xattn_fc2_b)
    x = _L1_xattn_ref(x, ctx_1024, mask_BxSxS_ik0, mask_BxSxS2_if1, L1_xattn_norm1_w, L1_xattn_norm2_w, L1_xattn_norm3_w, L1_xattn_sa_wq, L1_xattn_sa_wk, L1_xattn_sa_wv, L1_xattn_sa_wo, L1_xattn_ca_wq, L1_xattn_ca_wk, L1_xattn_ca_wv, L1_xattn_ca_wo, L1_xattn_gate_w, L1_xattn_exp_w1, L1_xattn_exp_w2, L1_xattn_sh_w1, L1_xattn_sh_w2)
    x = _L2_xattn_ref(x, ctx_1024, mask_BxSxS2_ik0, mask_BxSxS2_if1, L2_xattn_sa_wq, L2_xattn_sa_bq, L2_xattn_sa_wk, L2_xattn_sa_bk, L2_xattn_sa_wv, L2_xattn_sa_bv, L2_xattn_sa_wo, L2_xattn_sa_bo, L2_xattn_ca_wq, L2_xattn_ca_bq, L2_xattn_ca_wk, L2_xattn_ca_bk, L2_xattn_ca_wv, L2_xattn_ca_bv, L2_xattn_ca_wo, L2_xattn_ca_bo, L2_xattn_ff_w1, L2_xattn_ff_b1, L2_xattn_ff_w2, L2_xattn_ff_b2, L2_xattn_ln1_g, L2_xattn_ln1_b, L2_xattn_ln2_g, L2_xattn_ln2_b, L2_xattn_ln3_g, L2_xattn_ln3_b)
    x = _L3_xattn_ref(x, ctx_1024, ctx_1024, L3_xattn_Wq, L3_xattn_bq, L3_xattn_Wk, L3_xattn_bk, L3_xattn_Wv, L3_xattn_bv, L3_xattn_gamma, L3_xattn_beta)
    return x

_drawn_inputs = setup_inputs


def setup_inputs(seed=0):
    import zlib

    import numpy as np

    out = dict(_drawn_inputs(seed))
    spreads = {'L0_xattn_ln1_g': (1.0, 0.2),
     'L0_xattn_ln1_b': (0.0, 0.1),
     'L0_xattn_ln2_g': (1.0, 0.2),
     'L0_xattn_ln2_b': (0.0, 0.1),
     'L0_xattn_ln3_g': (1.0, 0.2),
     'L0_xattn_ln3_b': (0.0, 0.1),
     'L0_xattn_fc1_b': (0.0, 0.1),
     'L0_xattn_fc2_b': (0.0, 0.1),
     'L1_xattn_norm1_w': (1.0, 0.2),
     'L1_xattn_norm2_w': (1.0, 0.2),
     'L1_xattn_norm3_w': (1.0, 0.2),
     'L2_xattn_sa_bq': (0.0, 0.8),
     'L2_xattn_sa_bk': (0.0, 0.8),
     'L2_xattn_sa_bv': (0.0, 0.358),
     'L2_xattn_sa_bo': (0.0, 0.1),
     'L2_xattn_ca_bq': (0.0, 0.8),
     'L2_xattn_ca_bk': (0.0, 0.8),
     'L2_xattn_ca_bv': (0.0, 0.273),
     'L2_xattn_ca_bo': (0.0, 0.1),
     'L2_xattn_ff_b1': (0.0, 0.1),
     'L2_xattn_ff_b2': (0.0, 0.1),
     'L2_xattn_ln1_g': (1.0, 0.2),
     'L2_xattn_ln1_b': (0.0, 0.1),
     'L2_xattn_ln2_g': (1.0, 0.2),
     'L2_xattn_ln2_b': (0.0, 0.1),
     'L2_xattn_ln3_g': (1.0, 0.2),
     'L2_xattn_ln3_b': (0.0, 0.1),
     'L3_xattn_bq': (0.0, 0.357),
     'L3_xattn_bk': (0.0, 0.8),
     'L3_xattn_bv': (0.0, 0.1),
     'L3_xattn_gamma': (1.0, 0.2),
     'L3_xattn_beta': (0.0, 0.1)}
    factors = {'L0_xattn_Wq1': 6.845,
     'L0_xattn_Wk1': 6.249,
     'L0_xattn_Wq2': 3.742,
     'L0_xattn_Wk2': 3.739,
     'L2_xattn_sa_wq': 8.0,
     'L2_xattn_sa_wk': 8.0,
     'L2_xattn_ca_wq': 8.0,
     'L2_xattn_ca_wk': 8.0}
    for name, (base, spread) in spreads.items():
        noise = np.random.default_rng([zlib.crc32(name.encode()), seed]).standard_normal(out[name].shape)
        drawn = base * np.exp(spread * noise) if base else spread * noise
        out[name] = jnp.asarray(drawn.astype(out[name].dtype))
    for name, factor in factors.items():
        out[name] = (out[name] * factor).astype(out[name].dtype)
    return out
```

```python
from contextlib import ExitStack

import concourse.bass as bass
from concourse import mybir

F32 = mybir.dt.float32
F32R = mybir.dt.float32r
BF16 = mybir.dt.bfloat16
I32 = mybir.dt.int32
U32 = mybir.dt.uint32
ALU = mybir.AluOpType
ACT = mybir.ActivationFunctionType
AX = mybir.AxisListType

B, S, D = 4, 512, 256
P = 128
KB = D // P
QT = S // P
NT = B * QT
E, HID = 8, 4 * D
HB = HID // P
SLOTS = 512
G = SLOTS // P
NEG = -float(2 ** 66)
WQ, WK, WV, WO, WEND = 0, 512, 1024, 1280, 1536


class Stage:

    def __init__(self, name, dk=16, causal=False, mask=None, length=False, kv="self", rms=False,
                 wo=False, bias=False, ln=True, eps=1e-5):
        self.name, self.dk, self.causal, self.mask, self.length = name, dk, causal, mask, length
        self.kv, self.rms, self.wo, self.bias, self.ln, self.eps = kv, rms, wo, bias, ln, eps
        self.heads = D // dk
        self.slot = 2 * dk
        self.per_group = P // self.slot
        self.per_qt = self.heads // 2
        self.pairs = QT * self.per_qt
        self.group_pairs = self.per_group // 2
        jobs = [("x", 0, "A"), ("x", 1, "D")]
        if kv == "mctx":
            jobs += [("c", 0, "A"), ("c", 1, "D")]
        jobs += [("q", g, "D") for g in range(G)] + [("k", g, "D") for g in range(G)]
        jobs += [("v", t, "D" if bias or t % 2 else "A") for t in range(QT)]
        self.jobs = jobs

    def width(self, qt):
        return (qt + 1) * P if self.causal else S

    def pair(self, i):
        return i // self.per_qt, 2 * (i % self.per_qt)

    def finishing(self, step, lag):
        n = step - lag + 1
        return n // self.per_qt - 1 if n > 0 and n % self.per_qt == 0 and n // self.per_qt <= QT else None


def freed(jobs, n):
    return (sum(e == "A" for _, _, e in jobs[:n]), sum(e == "D" for _, _, e in jobs[:n]))


ATT = [
    Stage("L0 self", causal=True, length=True),
    Stage("L0 cross", length=True, kv="mctx"),
    Stage("L1 self", mask=0, rms=True, wo=True, ln=False),
    Stage("L1 cross", mask=1, kv="ctx", rms=True, wo=True, ln=False),
    Stage("L2 self", mask=2, wo=True, bias=True),
    Stage("L2 cross", mask=1, kv="ctx", wo=True, bias=True),
    Stage("L3", dk=32, causal=True, kv="ctx", bias=True, eps=1e-6),
]


class Feed:

    def __init__(self, hb, masked):
        self.hb, self.masked = hb, masked
        self.jobs = [("x", 0, "A"), ("x", 1, "D")]
        self.jobs += [("h", n, "D" if n % 2 else "A") for n in range(hb)]
        self.jobs += [("o", t, "D") for t in range(QT)]


FEED = {"f0": Feed(D // P, True), "f2": Feed(HID // P, False)}
PREP = [("x", 0, "A"), ("x", 1, "D")] + [("g", t, "D") for t in range(QT)]
ORDER = ["a0", "a1", "f0", "a2", "a3", "prep", "moe", "a4", "a5", "f2", "a6"]
STEPS_AFTER = 9


class Signal:

    def __init__(self, sem, per, unit=1, after=None):
        self.sem, self.per, self.unit, self.base = sem, per, unit, {}
        total = self.start = 1 if unit == 1 else 0
        for st in ORDER:
            self.base[st] = total
            total += (per.get(st, 0) * B + (after or {}).get(st, 0)) * unit
        self.total = total

    def at(self, st, b, k):
        return b * (self.per.get(st, 0) * self.unit) + (self.base[st] + k * self.unit)


def build(nc, io):
    ctx = ExitStack()
    with ctx:
        def sb(name, shape, dt):
            return ctx.enter_context(nc.sbuf_tensor(name, shape, dt))

        def sem(name):
            return ctx.enter_context(nc.semaphore(name))

        def signal(name, unit=1, after=None, **per):
            out = {}
            for key, n in per.items():
                for st in ORDER:
                    if st == key or (key == "att" and st[0] == "a") or (key == "feed" and st[0] == "f"):
                        out[st] = n(st) if callable(n) else n
            return Signal(sem(name), out, unit, after)

        att = {f"a{n}": s for n, s in enumerate(ATT)}

        X = sb("X", [P, NT, D], F32)
        wt = sb("wt", [P, 2, KB, WEND], F32)
        wcol = sb("wcol", [P, 2, 10], F32)
        wrow = sb("wrow", [P, 2, 4, D], F32)
        arena = sb("arena", [P, 4, QT * D], F32)
        xs = arena[:, 0, :].rearrange("p (q d) -> p q d", q=QT)
        cn = arena[:, 1, :].rearrange("p (q d) -> p q d", q=QT)
        cs = arena[:, 2, :].rearrange("p (q d) -> p q d", q=QT)
        kvT = arena[:, 3, :].rearrange("p (k n) -> p k n", k=KB)
        xT = sb("xT", [P, KB, S], F32)
        Q = sb("Q", [P, G, S], F32R)
        KH = sb("KH", [P, G, S], F32R)
        KL = sb("KL", [P, G, S], F32R)
        qhi = sb("qhi", [P, 2, S], F32R)
        V = sb("V", [P, QT, SLOTS], F32)
        prob = sb("prob", [P, 3, 2, S], F32)
        probT = sb("probT", [P, 3, 4 * S], F32)
        oT = sb("oT", [P, S], F32)
        o = sb("o", [P, D], F32)
        oTn = sb("oTn", [P, KB, P], F32)
        y = sb("y", [P, 2, D], F32)
        xh = sb("xh", [P, 2, D], F32)
        xg = sb("xg", [P, D], F32)
        junk = sb("junk", [P, D], F32)
        maski = sb("maski", [P, QT, S], I32)
        iota = maski[0:16, 0, :].bitcast(F32)
        selq = maski[:, 1, :].bitcast(F32).rearrange("p (g n) -> p g n", g=G)
        maskb = sb("maskb", [P, QT, S], BF16)
        hT = [sb("hT", [P, HB, S], F32)[:, :, :],
              arena[:, :, :].rearrange("p a n -> p (a n)").rearrange("p (h n) -> p h n", h=HB)]
        wcolf = sb("wcolf", [P, HB], F32)
        wrowf = sb("wrowf", [P, 3, D], F32)
        bqlow = sb("bqlow", [P, G], F32)
        norm3 = sb("norm3", [P, KB], F32)
        w1e = sb("w1e", [P, 2, KB, HID], F32)
        w2e = [prob[:, 0:2, :, :].rearrange("p a b n -> p (a b n)").rearrange("p (h n) -> p h n", h=HB),
               V[:, :, :].rearrange("p a b -> p (a b)").rearrange("p (h n) -> p h n", h=HB)]
        hnT = probT[:, 0:2, :].rearrange("p a n -> p (a n)").rearrange("p (k n) -> p k n", k=KB)
        identf = sb("identf", [P, P], F32)
        identb = sb("identb", [P, P], BF16)
        causal = sb("causal", [P, P], BF16)
        selh = sb("selh", [P, 16, P], BF16)
        lowrow = sb("lowrow", [P, 2], F32)
        gw = sb("gw", [P, KB, E], F32)
        iota8 = sb("iota8", [P, E], F32)
        epsilon = sb("epsilon", [P, 2], F32)
        minus_half = sb("minus_half", [P, 4], F32)
        qz = qhi[:, 0, :].rearrange("p (g n) -> p g n", g=G)
        nz = y[0:16, :, :].rearrange("p a n -> p (a n)")
        lens = sb("lens", [16, 4], F32)
        pen = sb("pen", [P, S], BF16)
        negm = sb("negm", [P, 4, 2], F32)
        rinv = sb("rinv", [P, 16, 1], F32)
        amax = sb("amax", [P, NT], F32)
        keep = sb("keep", [P, 2, NT], F32)
        bn = sb("bn", [P, 2, 6], F32)
        mv = sb("mv", [P, 2, 2], F32)
        ve = sb("ve", [P, 2, 1], F32)
        rstd = sb("rstd", [P, 2, 1], F32)
        ss = sb("ss", [P, QT], F32)
        ms = sb("ms", [P, QT], F32)
        rs4 = sb("rs4", [P, QT], F32)
        lg = sb("lg", [P, E], F32)
        top = sb("top", [P, E], F32)
        topi = sb("topi", [P, E], U32)
        topf = sb("topf", [P, E], F32)
        gex = sb("gex", [P, 4], F32)
        gpart = sb("gpart", [P, 2, E], F32)
        gates = sb("gates", [P, E + 1, NT], F32)

        SB = [ctx.enter_context(nc.psum_tensor(f"scores{n}", [P, 2, S], F32)) for n in range(2)]
        TB = [ctx.enter_context(nc.psum_tensor(f"turned{n}", [P, S], F32)) for n in range(2)]
        OB = ctx.enter_context(nc.psum_tensor("outputs", [P, S], F32))
        MB = ctx.enter_context(nc.psum_tensor("mixed", [P, S], F32))
        RING = [SB[n // 2][:, n % 2, :] for n in range(4)]
        OUTS = [TB[0], TB[1], OB, MB]

        jobs_of = {st: (att[st].jobs if st in att else FEED[st].jobs if st in FEED else PREP)
                   for st in ORDER if st != "moe"}

        def nA(st):
            return freed(jobs_of[st], 99)[0]

        def nD(st):
            return freed(jobs_of[st], 99)[1]

        def njob(st):
            return len(jobs_of[st])

        def npair(st):
            return att[st].pairs

        def with_wo(st):
            return QT if att[st].wo else 0

        def with_ln(st):
            return QT if att[st].ln else 0

        PER_TURN = E // B
        UNITS = B
        ROUTED_H, ROUTED_O = UNITS * HB, UNITS * QT
        c_const = sem("c_const")
        c_x = sem("c_x")
        c_w = [sem("c_weights0"), sem("c_weights1")]
        c_ready = sem("c_ready")
        c_keep = sem("c_keep")
        c_kv = signal("c_kv", 16, a1=1, a3=1, a5=1, a6=1)
        c_mask = signal("c_mask", 16, a2=1, a3=1, a4=1, a5=1)
        c_maskb = signal("c_maskb", a2=1, a3=1, a4=1, a5=1)
        c_xs = signal("c_xs", att=1, feed=1, prep=1)
        c_cs = signal("c_cs", a1=1)
        c_ss = signal("c_ss", a2=1, a3=1, prep=1)
        c_rs = signal("c_rs", a2=1, a3=1, prep=1)
        c_job = signal("c_job", att=njob, feed=njob, prep=njob, moe=PER_TURN * ROUTED_H,
                       after={"moe": ROUTED_H})
        c_hi = signal("c_hi", att=2 * G)
        c_A = signal("c_A", att=nA, feed=nA, prep=nA, moe=PER_TURN * ROUTED_H,
                     after={"moe": ROUTED_H})
        c_D = signal("c_D", att=nD, feed=nD, prep=nD)
        c_qz = signal("c_qz", a0=1, a1=1)
        c_e0 = signal("c_e0", a0=1, a1=1)
        c_pen = signal("c_pen", a0=1, a1=1)
        c_scores = signal("c_scores", att=npair)
        c_max = signal("c_max", att=npair)
        c_exp = signal("c_exp", att=npair)
        c_turn = signal("c_turn", att=lambda st: 2 * npair(st))
        c_tD = signal("c_tD", att=npair)
        c_tA = signal("c_tA", att=npair)
        c_pv = signal("c_pv", att=QT * G)
        c_oT = signal("c_oT", att=QT)
        c_on = signal("c_on", att=QT)
        c_o = signal("c_o", att=QT)
        c_ot = signal("c_ot", att=with_wo)
        c_otn = signal("c_otn", att=with_wo)
        c_y = signal("c_y", att=with_wo)
        c_yD = signal("c_yD", att=with_wo)
        c_var = signal("c_var", att=with_ln, feed=QT)
        c_rstd = signal("c_rstd", att=with_ln, feed=QT)
        c_xh = signal("c_xh", att=with_ln, feed=QT)
        c_xout = signal("c_xout", att=QT, feed=QT)
        c_hn = signal("c_hn", prep=1)
        c_gex = signal("c_gex", prep=QT)
        c_gate = signal("c_gate", prep=QT)
        c_w1 = [sem("c_first0"), sem("c_first1")]
        c_w2 = [sem("c_second0"), sem("c_second1")]
        c_wf = sem("c_wf")
        c_h = signal("c_h", moe=PER_TURN * ROUTED_O, after={"moe": ROUTED_O})
        c_hD = signal("c_hD", moe=PER_TURN * ROUTED_O, after={"moe": ROUTED_O})
        c_out = sem("c_out")

        block = ctx.enter_context(nc.Block())

        def tile(b, qt):
            return X[:, bass.ds(b * QT + qt, 1), :].rearrange("p o d -> p (o d)")

        def wait_x(eng, st):
            if st == "a0":
                eng.wait_ge(c_x, 16)
            elif st == "a4":
                eng.wait_ge(c_hD.sem, c_hD.total)
            else:
                eng.wait_ge(c_xout.sem, c_xout.at(st, 0, 0))

        def wait_weights(eng, n):
            eng.wait_ge(c_w[n % 2], 48 * (n // 2 + 1))

        @block.sync
        def _(sp):
            sp.dma_start(X[:, :, :], io["x"].rearrange("b (q p) d -> p (b q) d", p=P)).then_inc(c_x, 16)
            for dst, name in ((identf, "identf"), (identb, "identb"), (causal, "causal"), (selq, "selq"),
                              (selh, "selh"), (iota, "iota"), (lowrow, "lowrow"), (gw, "gw"),
                              (iota8, "iota8"), (norm3, "norm3")):
                sp.dma_start(dst[(slice(None),) * len(dst.shape)], io[name]).then_inc(c_const, 16)

            def weights(n):
                if n >= 2:
                    after = f"a{n - 1}"
                    sp.wait_ge(c_xout.sem, c_xout.at(after, 0, 0))
                    sp.wait_ge(c_pv.sem, c_pv.at(after, 0, 0))
                k = n % 2
                sp.dma_start(wt[:, k, :, :], io[f"w{n}"]).then_inc(c_w[k], 16)
                sp.dma_start(wcol[:, k, :], io[f"col{n}"]).then_inc(c_w[k], 16)
                sp.dma_start(wrow[:, k, :, :], io[f"row{n}"]).then_inc(c_w[k], 16)

            weights(0)
            weights(1)
            for st in ORDER:
                if st in att:
                    a, n = att[st], int(st[1:])
                    if n >= 1 and n + 1 < len(ATT):
                        weights(n + 1)
                    if a.kv == "self" and a.mask is None:
                        continue
                    if st == "a4":
                        sp.wait_ge(c_hD.sem, c_hD.total)
                    if st == "a2":
                        sp.wait_ge(c_pv.sem, c_pv.at(st, 0, 0))
                    with sp.Fori(0, B) as b:
                        if a.kv == "ctx":
                            sp.wait_ge(c_job.sem, c_job.at(st, b, 0))
                            sp.dma_start(kvT, io["ctxT"][bass.ds(b, 1), :, :, :]
                                         .rearrange("o p k n -> (o p) k n")).then_inc(c_kv.sem, 16)
                        if a.kv == "mctx":
                            sp.wait_ge(c_cs.sem, c_cs.at(st, b, 0))
                            sp.dma_start(cn, io["ctx"][bass.ds(b, 1), :, :]
                                         .rearrange("o (q p) d -> p (o q) d", p=P)).then_inc(c_kv.sem, 16)
                        if a.mask is not None:
                            sp.wait_ge(c_maskb.sem, c_maskb.at(st, b, 0))
                            sp.dma_start(maski[:, :, :], io[f"mask{a.mask}"][bass.ds(b, 1), :, :]
                                         .rearrange("o (q p) n -> p (o q) n", p=P)).then_inc(c_mask.sem, 16)
                elif st in FEED:
                    if st == "f2":
                        sp.wait_ge(c_h.sem, c_h.total)
                    hb = FEED[st].hb
                    sp.dma_start(w1e[:, 0, :, 0:hb * P], io[f"{st}w1"]).then_inc(c_wf, 16)
                    sp.dma_start(w1e[:, 1, :, :].rearrange("p k n -> p (k n)")[:, 0:hb * D]
                                 .rearrange("p (h n) -> p h n", h=hb), io[f"{st}w2"]).then_inc(c_wf, 16)
                    sp.dma_start(wrowf[:, :, :], io[f"{st}row"]).then_inc(c_wf, 16)
                    sp.dma_start(wcolf[:, 0:hb], io[f"{st}col"]).then_inc(c_wf, 16)
                elif st == "moe":
                    sp.wait_ge(c_pv.sem, c_pv.at("moe", 0, 0))

                    def expert(slot, w1, w2):
                        sp.dma_start(w1e[:, slot, :, :], w1).then_inc(c_w1[slot], 16)
                        sp.dma_start(w2e[slot], w2).then_inc(c_w2[slot], 16)

                    def routed(slot, e):
                        expert(slot, io["ew1"][bass.ds(e, 1), :, :, :].rearrange("o p k n -> (o p) k n"),
                               io["ew2"][bass.ds(e, 1), :, :, :].rearrange("o p k n -> (o p) k n"))

                    routed(0, 0)
                    routed(1, 1)
                    with sp.Fori(0, B - 1) as it:
                        for slot in range(PER_TURN):
                            sp.wait_ge(c_h.sem, c_h.at(st, it, (slot + 1) * ROUTED_O))
                            routed(slot, it * PER_TURN + (PER_TURN + slot))
                    sp.wait_ge(c_h.sem, c_h.at(st, B - 1, ROUTED_O))
                    expert(0, io["sw1"], io["sw2"])
            sp.wait_ge(c_xout.sem, c_xout.total)
            sp.dma_start(io["out"].rearrange("b (q p) d -> p (b q) d", p=P), X[:, :, :]).then_inc(c_out, 16)
            sp.wait_ge(c_out, 16)

        @block.gpsimd
        def _(pool):
            def layer_norm(st, b, qt, eps, gamma, beta):
                r = qt % 2
                pool.wait_ge(c_var.sem, c_var.at(st, b, qt + 1))
                pool.tensor_tensor(ve[:, r, :], mv[:, r, 1:2], eps_of[eps], ALU.add)
                pool.drain()
                pool.tensor_tensor(rstd[:, r, :], ve[:, r, :], minus_half[:, 0:1], ALU.pow)\
                    .then_inc(c_rstd.sem, 1)
                pool.wait_ge(c_xh.sem, c_xh.at(st, b, qt + 1))
                pool.tensor_tensor(xg[:, :], xh[:, r, :], gamma, ALU.mult)
                pool.drain()
                pool.tensor_tensor(tile(b, qt), xg[:, :], beta, ALU.add).then_inc(c_xout.sem, 1)

            def roots(st, b):
                pool.wait_ge(c_ss.sem, c_ss.at(st, b, 1))
                pool.tensor_tensor(rs4[:, :], ms[:, :], minus_half[:, :], ALU.pow).then_inc(c_rs.sem, 1)

            def stage_tokens(st, b):
                pool.wait_ge(c_job.sem, c_job.at(st, b, 0))
                pool.tensor_copy(xs, X[:, bass.ds(b * QT, QT), :]).then_inc(c_xs.sem, 1)

            for s in (c_xs, c_cs, c_rs, c_rstd, c_xout, c_hn):
                pool.sem_inc(s.sem, s.start)
            eps_of = {eps: epsilon[:, n:n + 1] for n, eps in enumerate((1e-5, 1e-6))}
            for eps, column in eps_of.items():
                pool.memset(column, eps)
            pool.memset(minus_half[:, :], -0.5)
            pool.memset(gates[:, E, :], 1.0)
            pool.wait_ge(c_const, 160)
            for st in ORDER:
                if st in att:
                    a, n = att[st], int(st[1:])
                    k = n % 2
                    wait_weights(pool, n)
                    wq = wt[:, k, :, WQ:WK]
                    pool.tensor_scalar(wq, wq, a.dk ** -0.5, None, ALU.mult)
                    pool.tensor_scalar(wcol[:, k, 0:G], wcol[:, k, 0:G], a.dk ** -0.5, None, ALU.mult)
                    pool.drain()
                    pool.wait_ge(c_pv.sem, c_pv.at(st, 0, 0))
                    wait_x(pool, st)
                    pool.tensor_scalar(bqlow[:, :], wcol[:, k, 0:G], lowrow[:, n // 6:n // 6 + 1], None,
                                       ALU.mult)
                    pool.memset(V[:, :, :], 0.0)
                    pool.drain()
                    pool.memset(V[:, :, :].rearrange("p t (h s) -> p (t h) s", s=a.slot)[:, :, a.dk:a.dk + 1],
                                1.0).then_inc(c_ready, 1)
                    with pool.Fori(0, B) as b:
                        if a.rms:
                            roots(st, b)
                        else:
                            stage_tokens(st, b)
                        if a.kv == "mctx":
                            pool.wait_ge(c_keep, 2)
                            pool.wait_ge(c_kv.sem, c_kv.at(st, b, 1))
                            pool.tensor_tensor(cs, cn, keep[:, 1, bass.ds(b * QT, QT)].unsqueeze(2)
                                               .to_broadcast([P, QT, D]), ALU.mult).then_inc(c_cs.sem, 1)
                        if a.ln:
                            for qt in range(QT):
                                layer_norm(st, b, qt, a.eps, wrow[:, k, 2, :], wrow[:, k, 3, :])
                elif st in FEED:
                    pool.wait_ge(c_wf, 64 if st == "f0" else 128)
                    with pool.Fori(0, B) as b:
                        stage_tokens(st, b)
                        for qt in range(QT):
                            layer_norm(st, b, qt, 1e-5, wrowf[:, 1, :], wrowf[:, 2, :])
                elif st == "prep":
                    with pool.Fori(0, B) as b:
                        roots(st, b)
                        pool.wait_ge(c_A.sem, c_A.at(st, b, 1))
                        pool.wait_ge(c_D.sem, c_D.at(st, b, 1))
                        pool.tensor_copy(hnT[:, :, bass.ds(b * S, S)], xT[:, :, :]).then_inc(c_hn.sem, 1)

        @block.tensor
        def _(pe):
            def turn_tokens(out, src, kb):
                for qt in range(QT):
                    last = pe.transpose(out[:, qt * P:(qt + 1) * P], src[:, qt, kb * P:(kb + 1) * P],
                                        identf[:, :])
                return last

            def bank_free(st, b, jobs, j):
                if j >= 4:
                    fa, fd = freed(jobs, j - 3)
                    if jobs[j - 4][2] == "A":
                        pe.wait_ge(c_A.sem, c_A.at(st, b, fa))
                    else:
                        pe.wait_ge(c_D.sem, c_D.at(st, b, fd))

            def all_free(st, b, jobs, n):
                fa, fd = freed(jobs, n)
                pe.wait_ge(c_A.sem, c_A.at(st, b, fa))
                pe.wait_ge(c_D.sem, c_D.at(st, b, fd))

            def scores(st, a, b, i, k):
                qt, h0 = a.pair(i)
                w = a.width(qt)
                if i >= 2:
                    pe.wait_ge(c_exp.sem, c_exp.at(st, b, i - 1))
                out, rows, g = [], [], []
                for e in range(2):
                    s = (h0 + e) % a.per_group
                    rows.append(slice(s * a.slot, (s + 1) * a.slot))
                    g.append((h0 + e) // a.per_group)
                    out.append(SB[i % 2][:, e, 0:w])
                for part in (KH, KL):
                    for e in range(2):
                        last = pe.matmul(out[e], Q[rows[e], g[e], qt * P:(qt + 1) * P],
                                         part[rows[e], g[e], 0:w], start=(part is KH),
                                         stop=(part is KL and not (a.causal or a.mask is not None or a.length)))
                for e in range(2):
                    if a.mask is not None:
                        last = pe.matmul(out[e], identb[:, :], maskb[:, qt, :], start=False, stop=True)
                    if a.length:
                        last = pe.matmul(out[e], selh[:, h0 + e, :], pen[:, 0:w], start=False,
                                         stop=not a.causal)
                    if a.causal:
                        last = pe.matmul(out[e][:, w - P:w], identb[:, :], causal[:, :], start=False, stop=True)
                last.then_inc(c_scores.sem, 1)

            def turns(st, a, b, i):
                qt, _ = a.pair(i)
                pe.wait_ge(c_exp.sem, c_exp.at(st, b, i + 1))
                for e in range(2):
                    free = c_tA if e else c_tD
                    pe.wait_ge(free.sem, free.at(st, b, i))
                    for kb in range(a.width(qt) // P):
                        last = pe.transpose(TB[e][:, kb * P:(kb + 1) * P],
                                            prob[:, i % 3, e, kb * P:(kb + 1) * P], identf[:, :])
                    last.then_inc(c_turn.sem, 1)

            def values(st, a, b, i):
                u = i // a.group_pairs
                qt, g = u // G, u % G
                pe.wait_ge(c_tD.sem, c_tD.at(st, b, i + 1))
                pe.wait_ge(c_tA.sem, c_tA.at(st, b, i + 1))
                if g == 0:
                    pe.wait_ge(c_oT.sem, c_oT.at(st, b, qt))
                blocks = a.width(qt) // P
                for kb in range(blocks):
                    for s in range(a.per_group):
                        rows = slice(s * a.slot, (s + 1) * a.slot)
                        h = g * a.per_group + s
                        last = pe.matmul(OB[rows, g * P:(g + 1) * P], V[:, kb, h * a.slot:(h + 1) * a.slot],
                                         probT[:, u % 3, s * S + kb * P:s * S + (kb + 1) * P],
                                         start=(kb == 0), stop=(kb == blocks - 1))
                last.then_inc(c_pv.sem, 1)

            def attention(st):
                a, n = att[st], int(st[1:])
                k = n % 2
                wait_weights(pe, n)
                pe.wait_ge(c_ready, n + 1)
                with pe.Fori(0, B) as b:
                    pe.wait_ge(c_exp.sem, c_exp.at(st, b, 0))
                    all_free(st, b, a.jobs, 0)
                    for j, (kind, idx, _) in enumerate(a.jobs):
                        bank = RING[j % 4]
                        bank_free(st, b, a.jobs, j)
                        if kind == "x":
                            if idx == 0:
                                pe.wait_ge(c_xs.sem, c_xs.at(st, b, 1))
                            last = turn_tokens(bank, xs, idx)
                        elif kind == "c":
                            if idx == 0:
                                pe.wait_ge(c_cs.sem, c_cs.at(st, b, 1))
                            last = turn_tokens(bank, cs, idx)
                        elif kind in "qk":
                            if (kind, idx) == ("q", 0):
                                all_free(st, b, a.jobs, 2)
                            if (kind, idx) == ("k", 0):
                                if a.kv == "ctx":
                                    pe.wait_ge(c_kv.sem, c_kv.at(st, b, 1))
                                if a.kv == "mctx":
                                    all_free(st, b, a.jobs, 4)
                            src = xT if kind == "q" or a.kv == "self" else kvT
                            c0 = (WQ if kind == "q" else WK) + idx * P
                            for kb in range(KB):
                                last = pe.matmul(bank, wt[:, k, kb, c0:c0 + P], src[:, kb, :],
                                                 start=(kb == 0), stop=(kb == KB - 1))
                        else:
                            src = xT if a.kv == "self" else kvT
                            for kb in range(KB):
                                last = pe.matmul(bank[:, 0:D], src[:, kb, idx * P:(idx + 1) * P],
                                                 wt[:, k, kb, WV:WO], start=(kb == 0), stop=(kb == KB - 1))
                        last.then_inc(c_job.sem, 1)
                    all_free(st, b, a.jobs, len(a.jobs))
                    if a.length:
                        pe.wait_ge(c_qz.sem, c_qz.at(st, b, 1))
                        pe.wait_ge(c_o.sem, c_o.at(st, b, 0))
                        for g in range(G):
                            for part in (KH, KL):
                                last = pe.matmul(MB[:, :], qz[:, g, :], part[:, g, :],
                                                 start=(g == 0 and part is KH), stop=(g == G - 1 and part is KL))
                        last.then_inc(c_e0.sem, 1)
                        pe.wait_ge(c_pen.sem, c_pen.at(st, b, 1))
                    if a.mask is not None:
                        pe.wait_ge(c_maskb.sem, c_maskb.at(st, b, 1))
                    for step in range(a.pairs + STEPS_AFTER):
                        if step < a.pairs:
                            scores(st, a, b, step, k)
                        if 2 <= step < a.pairs + 2:
                            turns(st, a, b, step - 2)
                        i = step - 3
                        if 0 <= i < a.pairs and (i + 1) % a.group_pairs == 0:
                            values(st, a, b, i)
                        qt = a.finishing(step, 5)
                        if qt is not None:
                            pe.wait_ge(c_oT.sem, c_oT.at(st, b, qt + 1))
                            pe.wait_ge(c_o.sem, c_o.at(st, b, qt))
                            if a.wo:
                                pe.wait_ge(c_yD.sem, c_yD.at(st, b, qt))
                            for g in range(G):
                                last = pe.transpose(MB[:, g * P:(g + 1) * P], oT[:, g * P:(g + 1) * P],
                                                    identf[:, :])
                            last.then_inc(c_on.sem, 1)
                        qt = a.finishing(step, 6) if a.wo else None
                        if qt is not None:
                            pe.wait_ge(c_o.sem, c_o.at(st, b, qt + 1))
                            for kb in range(KB):
                                last = pe.transpose(MB[:, kb * P:(kb + 1) * P], o[:, kb * P:(kb + 1) * P],
                                                    identf[:, :])
                            last.then_inc(c_ot.sem, 1)
                        qt = a.finishing(step, 7) if a.wo else None
                        if qt is not None:
                            pe.wait_ge(c_otn.sem, c_otn.at(st, b, qt + 1))
                            for kb in range(KB):
                                last = pe.matmul(MB[:, 0:D], oTn[:, kb, :], wt[:, k, kb, WO:WEND],
                                                 start=(kb == 0), stop=(kb == KB - 1))
                            last.then_inc(c_y.sem, 1)

            def feed(st):
                f = FEED[st]
                pe.wait_ge(c_wf, 64 if st == "f0" else 128)
                w2 = w1e[:, 1, :, :].rearrange("p k n -> p (k n)")
                with pe.Fori(0, B) as b:
                    pe.wait_ge(c_exp.sem, c_exp.at(st, b, 0))
                    all_free(st, b, f.jobs, 0)
                    for j, (kind, idx, _) in enumerate(f.jobs):
                        bank = RING[j % 4]
                        bank_free(st, b, f.jobs, j)
                        if kind == "x":
                            if idx == 0:
                                pe.wait_ge(c_xs.sem, c_xs.at(st, b, 1))
                            last = turn_tokens(bank, xs, idx)
                        elif kind == "h":
                            if idx == 0:
                                all_free(st, b, f.jobs, 2)
                            for kb in range(KB):
                                last = pe.matmul(bank, w1e[:, 0, kb, idx * P:(idx + 1) * P], xT[:, kb, :],
                                                 start=(kb == 0), stop=(kb == KB - 1))
                        else:
                            if idx == 0:
                                all_free(st, b, f.jobs, 2 + f.hb)
                            for n in range(f.hb):
                                last = pe.matmul(bank[:, 0:D], hT[0][:, n, idx * P:(idx + 1) * P],
                                                 w2[:, n * D:(n + 1) * D], start=(n == 0), stop=(n == f.hb - 1))
                        last.then_inc(c_job.sem, 1)

            def prepare(st):
                with pe.Fori(0, B) as b:
                    pe.wait_ge(c_exp.sem, c_exp.at(st, b, 0))
                    all_free(st, b, PREP, 0)
                    for j, (kind, idx, _) in enumerate(PREP):
                        bank = RING[j % 4]
                        bank_free(st, b, PREP, j)
                        if kind == "x":
                            if idx == 0:
                                pe.wait_ge(c_xs.sem, c_xs.at(st, b, 1))
                            last = turn_tokens(bank, xs, idx)
                        else:
                            if idx == 0:
                                all_free(st, b, PREP, 2)
                            for kb in range(KB):
                                last = pe.matmul(bank[:, 0:E], xT[:, kb, idx * P:(idx + 1) * P], gw[:, kb, :],
                                                 start=(kb == 0), stop=(kb == KB - 1))
                        last.then_inc(c_job.sem, 1)

            def experts(st):
                def hidden(it, unit, slot):
                    for n in range(HB):
                        j = unit * HB + n
                        bank = RING[j % 4]
                        if j >= 4:
                            pe.wait_ge(c_A.sem, c_A.at(st, it, j - 3))
                        for kb in range(KB):
                            last = pe.matmul(bank, w1e[:, slot, kb, n * P:(n + 1) * P],
                                             hnT[:, kb, (unit % UNITS) * S:(unit % UNITS + 1) * S],
                                             start=(kb == 0), stop=(kb == KB - 1))
                        last.then_inc(c_job.sem, 1)

                def outputs(it, unit, slot):
                    pe.wait_ge(c_A.sem, c_A.at(st, it, (unit + 1) * HB))
                    for t in range(QT):
                        j = unit * QT + t
                        pe.wait_ge(c_hD.sem, c_hD.at(st, it, j - 3) if j >= 4 else c_hD.at(st, it, 0))
                        for n in range(HB):
                            last = pe.matmul(OUTS[t][:, 0:D], hT[unit % 2][:, n, t * P:(t + 1) * P],
                                             w2e[slot][:, n, :], start=(n == 0), stop=(n == HB - 1))
                        last.then_inc(c_h.sem, 1)

                def turn(it, count, landed):
                    pe.wait_ge(c_A.sem, c_A.at(st, it, 0))
                    units = count * UNITS
                    for unit in range(units + 1):
                        if unit < units:
                            if unit % UNITS == 0:
                                pe.wait_ge(c_w1[unit // UNITS], landed)
                            hidden(it, unit, unit // UNITS)
                        if unit >= 1:
                            if (unit - 1) % UNITS == 0:
                                pe.wait_ge(c_w2[(unit - 1) // UNITS], landed)
                            outputs(it, unit - 1, (unit - 1) // UNITS)

                pe.wait_ge(c_hn.sem, c_hn.total)
                pe.wait_ge(c_D.sem, c_D.at(st, 0, 0))
                with pe.Fori(0, B) as it:
                    turn(it, PER_TURN, it * 16 + 16)
                turn(B, 1, 16 * (B + 1))

            for s in (c_job, c_e0, c_scores, c_turn, c_pv, c_on, c_ot, c_y, c_h):
                pe.sem_inc(s.sem, s.start)
            pe.wait_ge(c_const, 160)
            for st in ORDER:
                if st in att:
                    attention(st)
                elif st in FEED:
                    feed(st)
                elif st == "prep":
                    prepare(st)
                else:
                    experts(st)

        @block.scalar
        def _(act):
            def attention(st):
                a, n = att[st], int(st[1:])
                k = n % 2
                wait_weights(act, n)
                act.wait_ge(c_ready, n + 1)
                low = lowrow[:, n // 6:n // 6 + 1]
                with act.Fori(0, B) as b:
                    for j, (kind, idx, eng) in enumerate(a.jobs):
                        if eng == "D" and kind not in "qk":
                            continue
                        bank = RING[j % 4]
                        act.wait_ge(c_job.sem, c_job.at(st, b, j + 1))
                        if kind == "q":
                            act.wait_ge(c_D.sem, c_D.at(st, b, freed(a.jobs, j - 1 if idx >= 2 else 0)[1]))
                            act.activation(qhi[:, idx % 2, :], bank, ACT.Identity, bias=bqlow[:, idx:idx + 1],
                                           scale=low).then_inc(c_hi.sem, 1)
                        elif kind == "k":
                            act.activation(KH[:, idx, :], bank, ACT.Identity,
                                           bias=wcol[:, k, G + idx:G + idx + 1], scale=1.0).then_inc(c_hi.sem, 1)
                        elif kind == "x":
                            if a.rms:
                                act.activation(xT[:, idx, :], bank, ACT.Identity, bias=0.0,
                                               scale=wcol[:, k, 8 + idx:9 + idx]).then_inc(c_A.sem, 1)
                            else:
                                act.activation(xT[:, idx, :], bank, ACT.Copy).then_inc(c_A.sem, 1)
                        elif kind == "c":
                            act.activation(kvT[:, idx, :], bank, ACT.Copy).then_inc(c_A.sem, 1)
                        else:
                            act.activation(V[:, idx, :].rearrange("p (h s) -> p h s", s=a.slot)[:, :, 0:a.dk],
                                           bank[:, 0:D].rearrange("p (h s) -> p h s", s=a.dk), ACT.Copy)\
                                .then_inc(c_A.sem, 1)
                    for step in range(a.pairs + STEPS_AFTER):
                        qt = a.finishing(step, 4)
                        if qt is not None:
                            act.wait_ge(c_pv.sem, c_pv.at(st, b, (qt + 1) * G))
                            act.wait_ge(c_on.sem, c_on.at(st, b, qt))
                            act.activation(oT[:, :], OB[:, :], ACT.Copy).then_inc(c_oT.sem, 1)
                        i = step - 2
                        if 0 <= i < a.pairs:
                            t, h0 = a.pair(i)
                            u, s, w = i // a.group_pairs, (h0 + 1) % a.per_group, a.width(t)
                            act.wait_ge(c_turn.sem, c_turn.at(st, b, 2 * i + 2))
                            if u >= 3:
                                act.wait_ge(c_pv.sem, c_pv.at(st, b, u - 2))
                            act.activation(probT[:, u % 3, s * S:s * S + w], TB[1][:, 0:w], ACT.Copy)\
                                .then_inc(c_tA.sem, 1)
                        if step < a.pairs:
                            t, _ = a.pair(step)
                            w = a.width(t)
                            act.wait_ge(c_max.sem, c_max.at(st, b, step + 1))
                            if step >= 3:
                                act.wait_ge(c_turn.sem, c_turn.at(st, b, 2 * (step - 2)))
                            for e in range(2):
                                last = act.activation(prob[:, step % 3, e, 0:w], SB[step % 2][:, e, 0:w],
                                                      ACT.Exp, bias=negm[:, step % 4, e:e + 1], scale=1.0)
                            last.then_inc(c_exp.sem, 1)
                        qt = a.finishing(step, 6) if a.wo else None
                        if qt is not None:
                            act.wait_ge(c_ot.sem, c_ot.at(st, b, qt + 1))
                            act.wait_ge(c_y.sem, c_y.at(st, b, qt))
                            act.activation(oTn[:, :, :].rearrange("p k n -> p (k n)"), MB[:, 0:D], ACT.Copy)\
                                .then_inc(c_otn.sem, 1)

            def feed(st):
                f = FEED[st]
                act.wait_ge(c_wf, 64 if st == "f0" else 128)
                with act.Fori(0, B) as b:
                    for j, (kind, idx, eng) in enumerate(f.jobs):
                        if eng == "D":
                            continue
                        act.wait_ge(c_job.sem, c_job.at(st, b, j + 1))
                        if kind == "x":
                            act.activation(xT[:, idx, :], RING[j % 4], ACT.Copy).then_inc(c_A.sem, 1)
                        else:
                            act.activation(hT[0][:, idx, :], RING[j % 4], ACT.Relu, bias=wcolf[:, idx:idx + 1],
                                           scale=1.0).then_inc(c_A.sem, 1)

            def prepare(st):
                with act.Fori(0, B) as b:
                    act.wait_ge(c_job.sem, c_job.at(st, b, 1))
                    act.wait_ge(c_hn.sem, c_hn.at(st, b, 0))
                    act.activation(xT[:, 0, :], RING[0], ACT.Identity, bias=0.0, scale=norm3[:, 0:1])\
                        .then_inc(c_A.sem, 1)
                    for t in range(QT):
                        act.wait_ge(c_gex.sem, c_gex.at(st, b, t + 1))
                        act.activation(gex[:, 1:2], gex[:, 0:1], ACT.Exp).then_inc(c_gate.sem, 1)

            def experts(st):
                def turn(it, count):
                    for unit in range(count * UNITS):
                        act.wait_ge(c_h.sem, c_h.at(st, it, (unit - 1) * QT) if unit >= 2 else c_h.at(st, it, 0))
                        for n in range(HB):
                            j = unit * HB + n
                            act.wait_ge(c_job.sem, c_job.at(st, it, j + 1))
                            act.activation(hT[unit % 2][:, n, :], RING[j % 4], ACT.Silu).then_inc(c_A.sem, 1)

                with act.Fori(0, B) as it:
                    turn(it, PER_TURN)
                turn(B, 1)

            for s in (c_hi, c_A, c_exp, c_tA, c_oT, c_otn, c_gate):
                act.sem_inc(s.sem, s.start)
            act.wait_ge(c_const, 160)
            for st in ORDER:
                if st in att:
                    attention(st)
                elif st in FEED:
                    feed(st)
                elif st == "prep":
                    prepare(st)
                else:
                    experts(st)

        @block.vector
        def _(dve):
            def squares(st, b):
                dve.wait_ge(c_job.sem, c_job.at(st, b, 0))
                tiles = X[:, bass.ds(b * QT, QT), :]
                dve.tensor_tensor(xs, tiles, tiles, ALU.mult)
                dve.drain()
                dve.tensor_reduce(ss[:, :], xs, AX.X, ALU.add)
                dve.drain()
                dve.tensor_scalar(ms[:, :], ss[:, :], 1.0 / D, 1e-5, ALU.mult, ALU.add).then_inc(c_ss.sem, 1)
                dve.wait_ge(c_rs.sem, c_rs.at(st, b, 1))
                dve.tensor_tensor(xs, tiles, rs4[:, :].unsqueeze(2).to_broadcast([P, QT, D]), ALU.mult)\
                    .then_inc(c_xs.sem, 1)

            def moments(st, b, qt):
                r = qt % 2
                dve.drain()
                dve.bn_stats(bn[:, r, :], y[:, r, :])
                dve.drain()
                dve.bn_aggr(mv[:, r, :], bn[:, r, :]).then_inc(c_var.sem, 1)

            def centre(st, b, qt):
                r = qt % 2
                dve.wait_ge(c_rstd.sem, c_rstd.at(st, b, qt + 1))
                dve.wait_ge(c_xout.sem, c_xout.at(st, b, qt))
                dve.tensor_scalar(xh[:, r, :], y[:, r, :], mv[:, r, 0:1], rstd[:, r, :], ALU.subtract,
                                  ALU.mult).then_inc(c_xh.sem, 1)

            def lengths(st, b):
                dve.drain()
                dve.tensor_tensor(qz[:, :, :], Q[:, :, 0:1].bitcast(F32).to_broadcast([P, G, P]),
                                  selq[:, :, :], ALU.mult).then_inc(c_qz.sem, 1)
                dve.wait_ge(c_e0.sem, c_e0.at(st, b, 1))
                dve.tensor_scalar(nz[:, :], MB[0:16, :], 0.0, None, ALU.not_equal)
                dve.drain()
                dve.tensor_reduce(lens[:, 0:1], nz[:, :], AX.X, ALU.add)
                dve.drain()
                dve.reciprocal(lens[:, 1:2], lens[:, 0:1])
                dve.tensor_scalar(nz[:, :], iota[:, :], lens[:, 0:1], NEG, ALU.is_ge, ALU.mult)
                dve.drain()
                dve.tensor_scalar(lens[:, 2:3], lens[:, 1:2], 0.0, None, ALU.mult)
                dve.drain()
                dve.tensor_scalar(pen[0:16, :], nz[:, :], lens[:, 2:3], None, ALU.add).then_inc(c_pen.sem, 1)

            def attention(st):
                a, n = att[st], int(st[1:])
                k = n % 2
                wait_weights(dve, n)
                dve.wait_ge(c_ready, n + 1)
                wait_x(dve, st)
                if a.length:
                    dve.tensor_reduce(amax[:, :], X[:, :, :], AX.X, ALU.max, apply_absolute_value=True)
                    dve.drain()
                    dve.tensor_scalar(keep[:, n, :], amax[:, :], 0.0, None, ALU.is_gt).then_inc(c_keep, 1)
                with dve.Fori(0, B) as b:
                    if a.rms:
                        squares(st, b)
                    if a.mask is not None:
                        dve.wait_ge(c_pv.sem, c_pv.at(st, b, 0))
                        dve.wait_ge(c_mask.sem, c_mask.at(st, b, 1))
                        dve.tensor_scalar(maskb[:, :, :], maski[:, :, :], 0.0, NEG, ALU.is_equal,
                                          ALU.mult).then_inc(c_maskb.sem, 1)
                    for j, (kind, idx, eng) in enumerate(a.jobs):
                        if eng == "A":
                            continue
                        bank = RING[j % 4]
                        if kind in "qk":
                            hi = sum(x[0] in "qk" for x in a.jobs[:j + 1])
                            dve.wait_ge(c_hi.sem, c_hi.at(st, b, hi))
                            if kind == "q":
                                dve.scalar_tensor_tensor(
                                    out=Q[:, idx, :], in0=bank, scalar=wcol[:, k, idx:idx + 1],
                                    in1=qhi[:, idx % 2, :].bitcast(F32), op0=ALU.add, op1=ALU.subtract)\
                                    .then_inc(c_D.sem, 1)
                            else:
                                dve.scalar_tensor_tensor(
                                    out=KL[:, idx, :], in0=bank, scalar=wcol[:, k, G + idx:G + idx + 1],
                                    in1=KH[:, idx, :].bitcast(F32), op0=ALU.add, op1=ALU.subtract)\
                                    .then_inc(c_D.sem, 1)
                            continue
                        dve.wait_ge(c_job.sem, c_job.at(st, b, j + 1))
                        if kind == "x" and a.rms:
                            dve.tensor_scalar(xT[:, idx, :], bank, wcol[:, k, 8 + idx:9 + idx], None,
                                              ALU.mult).then_inc(c_D.sem, 1)
                        elif kind == "x":
                            dve.tensor_copy(xT[:, idx, :], bank).then_inc(c_D.sem, 1)
                        elif kind == "c":
                            dve.tensor_copy(kvT[:, idx, :], bank).then_inc(c_D.sem, 1)
                        else:
                            dst = V[:, idx, :].rearrange("p (h s) -> p h s", s=a.slot)[:, :, 0:a.dk]
                            src = bank[:, 0:D].rearrange("p (h s) -> p h s", s=a.dk)
                            if a.bias:
                                dve.tensor_tensor(dst, src, wrow[:, k, 0, :].rearrange("p (h s) -> p h s", s=a.dk),
                                                  ALU.add).then_inc(c_D.sem, 1)
                            else:
                                dve.tensor_copy(dst, src).then_inc(c_D.sem, 1)
                    if a.length:
                        lengths(st, b)
                    for step in range(a.pairs + STEPS_AFTER):
                        if step < a.pairs:
                            t, _ = a.pair(step)
                            dve.wait_ge(c_scores.sem, c_scores.at(st, b, step + 1))
                            dve.tensor_reduce(negm[:, step % 4, :], SB[step % 2][:, :, 0:a.width(t)], AX.X,
                                              ALU.max, negate=True).then_inc(c_max.sem, 1)
                        i = step - 2
                        if 0 <= i < a.pairs:
                            t, h0 = a.pair(i)
                            u, s, w = i // a.group_pairs, h0 % a.per_group, a.width(t)
                            dve.wait_ge(c_turn.sem, c_turn.at(st, b, 2 * i + 1))
                            if u >= 3:
                                dve.wait_ge(c_pv.sem, c_pv.at(st, b, u - 2))
                            dve.tensor_copy(probT[:, u % 3, s * S:s * S + w], TB[0][:, 0:w])\
                                .then_inc(c_tD.sem, 1)
                        qt = a.finishing(step, 5)
                        if qt is not None:
                            view = MB[:, :].rearrange("p (h s) -> p h s", s=a.slot)
                            r = rinv[:, 0:a.heads, :]
                            dve.wait_ge(c_on.sem, c_on.at(st, b, qt + 1))
                            dve.reciprocal(r, view[:, :, a.dk:a.dk + 1])
                            dve.drain()
                            if a.length:
                                dve.tensor_scalar(r, r, keep[:, n, bass.ds(b * QT + qt, 1)], None, ALU.mult)
                                dve.drain()
                            dve.tensor_tensor(o[:, :].rearrange("p (h s) -> p h s", s=a.dk), view[:, :, 0:a.dk],
                                              r.to_broadcast([P, a.heads, a.dk]), ALU.mult).then_inc(c_o.sem, 1)
                            if not a.wo:
                                dve.drain()
                                dve.tensor_tensor(y[:, qt % 2, :], o[:, :], tile(b, qt), ALU.add)
                                moments(st, b, qt)
                        qt = a.finishing(step, 7) if a.wo else None
                        if qt is not None:
                            dve.wait_ge(c_y.sem, c_y.at(st, b, qt + 1))
                            if not a.ln:
                                dve.tensor_tensor(y[:, qt % 2, :], MB[:, 0:D], tile(b, qt), ALU.add)\
                                    .then_inc(c_yD.sem, 1)
                                dve.drain()
                                dve.tensor_copy(tile(b, qt), y[:, qt % 2, :]).then_inc(c_xout.sem, 1)
                            else:
                                dve.tensor_tensor(junk[:, :], MB[:, 0:D], wrow[:, k, 1, :], ALU.add)\
                                    .then_inc(c_yD.sem, 1)
                                dve.drain()
                                dve.tensor_tensor(y[:, qt % 2, :], junk[:, :], tile(b, qt), ALU.add)
                                moments(st, b, qt)
                        qt = a.finishing(step, 8 if a.wo else 6) if a.ln else None
                        if qt is not None:
                            centre(st, b, qt)

            def feed(st):
                f = FEED[st]
                dve.wait_ge(c_wf, 64 if st == "f0" else 128)
                wait_x(dve, st)
                with dve.Fori(0, B) as b:
                    for j, (kind, idx, eng) in enumerate(f.jobs):
                        if eng == "A":
                            continue
                        bank = RING[j % 4]
                        dve.wait_ge(c_job.sem, c_job.at(st, b, j + 1))
                        if kind == "x":
                            dve.tensor_copy(xT[:, idx, :], bank).then_inc(c_D.sem, 1)
                        elif kind == "h":
                            dve.tensor_scalar(hT[0][:, idx, :], bank, wcolf[:, idx:idx + 1], 0.0, ALU.add,
                                              ALU.max).then_inc(c_D.sem, 1)
                        else:
                            dve.tensor_tensor(junk[:, :], bank[:, 0:D], wrowf[:, 0, :], ALU.add)\
                                .then_inc(c_D.sem, 1)
                            dve.drain()
                            if f.masked:
                                dve.scalar_tensor_tensor(
                                    out=y[:, idx % 2, :], in0=junk[:, :],
                                    scalar=keep[:, 0, bass.ds(b * QT + idx, 1)], in1=tile(b, idx),
                                    op0=ALU.mult, op1=ALU.add)
                            else:
                                dve.tensor_tensor(y[:, idx % 2, :], junk[:, :], tile(b, idx), ALU.add)
                            moments(st, b, idx)
                            if idx >= 1:
                                centre(st, b, idx - 1)
                    centre(st, b, QT - 1)

            def prepare(st):
                wait_x(dve, st)
                with dve.Fori(0, B) as b:
                    squares(st, b)
                    dve.wait_ge(c_job.sem, c_job.at(st, b, 2))
                    dve.wait_ge(c_hn.sem, c_hn.at(st, b, 0))
                    dve.tensor_scalar(xT[:, 1, :], RING[1], norm3[:, 1:2], None, ALU.mult).then_inc(c_D.sem, 1)
                    for t in range(QT):
                        dve.wait_ge(c_job.sem, c_job.at(st, b, 3 + t))
                        dve.tensor_copy(lg[:, :], RING[(2 + t) % 4][:, 0:E]).then_inc(c_D.sem, 1)
                        dve.drain()
                        dve.max(top[:, :], lg[:, :])
                        dve.drain()
                        dve.tensor_tensor(gex[:, 0:1], top[:, 1:2], top[:, 0:1], ALU.subtract)\
                            .then_inc(c_gex.sem, 1)
                        dve.max_index(topi[:, :], top[:, :], lg[:, :])
                        dve.drain()
                        dve.tensor_copy(topf[:, :], topi[:, :])
                        dve.wait_ge(c_gate.sem, c_gate.at(st, b, t + 1))
                        dve.tensor_scalar(gex[:, 2:3], gex[:, 1:2], 1.0, None, ALU.add)
                        dve.drain()
                        dve.reciprocal(gex[:, 2:3], gex[:, 2:3])
                        dve.drain()
                        dve.tensor_tensor(gex[:, 3:4], gex[:, 1:2], gex[:, 2:3], ALU.mult)
                        dve.drain()
                        for c in range(2):
                            dve.tensor_scalar(gpart[:, c, :], iota8[:, :], topf[:, c:c + 1], gex[:, 2 + c:3 + c],
                                              ALU.is_equal, ALU.mult)
                        dve.drain()
                        dve.tensor_tensor(gates[:, 0:E, bass.ds(b * QT + t, 1)].rearrange("p e o -> p (e o)"),
                                          gpart[:, 0, :], gpart[:, 1, :], ALU.add)

            def experts(st):
                def turn(it, count):
                    for unit in range(count * UNITS):
                        for t in range(QT):
                            j = unit * QT + t
                            n = (unit % UNITS) * QT + t
                            dve.wait_ge(c_h.sem, c_h.at(st, it, j + 1))
                            dve.scalar_tensor_tensor(
                                out=X[:, n, :], in0=OUTS[t][:, 0:D],
                                scalar=(gates[:, bass.ds(it * PER_TURN + unit // UNITS, 1), n:n + 1]
                                        .rearrange("p o n -> p (o n)") if count > 1 else gates[:, E, n:n + 1]),
                                in1=X[:, n, :], op0=ALU.mult, op1=ALU.add).then_inc(c_hD.sem, 1)

                dve.drain()
                with dve.Fori(0, B) as it:
                    turn(it, PER_TURN)
                turn(B, 1)

            for s in (c_maskb, c_ss, c_D, c_qz, c_pen, c_max, c_tD, c_o, c_yD, c_var, c_xh, c_gex, c_hD):
                dve.sem_inc(s.sem, s.start)
            dve.memset(pen[:, :], 0.0)
            dve.wait_ge(c_const, 160)
            for st in ORDER:
                if st in att:
                    attention(st)
                elif st in FEED:
                    feed(st)
                elif st == "prep":
                    prepare(st)
                else:
                    experts(st)


def kernel(**inputs):
    import ml_dtypes
    import numpy as np
    import concourse.bacc as bacc
    from concourse.bass_utils import run_bass_kernel_spmd

    v = {name: np.asarray(a) for name, a in inputs.items()}

    def rows(w):
        return w.reshape(-1, P, w.shape[-1]).transpose(1, 0, 2)

    def slots(w, dk):
        w = w.reshape(w.shape[:-1] + (D // dk, 1, dk))
        return np.broadcast_to(w, w.shape[:-2] + (2, dk)).reshape(w.shape[:-3] + (SLOTS,))

    zero = np.zeros(D, np.float32)
    zeros = np.zeros((D, D), np.float32)

    def heads(w):
        return w.transpose(1, 0, 2).reshape(D, D)

    L0, L1, L2, L3 = "L0_xattn_", "L1_xattn_", "L2_xattn_", "L3_xattn_"
    ws = []
    for n in (1, 2):
        ws.append([heads(v[f"{L0}W{c}{n}"]) for c in "qkv"] + [zeros, zero, zero, zero, zero,
                  v[f"{L0}ln{n}_g"], v[f"{L0}ln{n}_b"], zero])
    for n, p in ((1, "sa"), (2, "ca")):
        ws.append([v[f"{L1}{p}_w{c}"].T for c in "qkvo"] + [zero] * 6 + [v[f"{L1}norm{n}_w"]])
    for n, p in ((1, "sa"), (2, "ca")):
        ws.append([v[f"{L2}{p}_w{c}"] for c in "qkvo"] + [v[f"{L2}{p}_b{c}"] for c in "qkvo"]
                  + [v[f"{L2}ln{n}_g"], v[f"{L2}ln{n}_b"], zero])
    ws.append([v[f"{L3}W{c}"] for c in "qkv"] + [zeros] + [v[f"{L3}b{c}"] for c in "qkv"]
              + [zero, v[f"{L3}gamma"], v[f"{L3}beta"], zero])

    def spread(*vectors):
        return np.broadcast_to(np.stack(vectors)[None], (P, len(vectors), D))

    arrays = {"x": v["x"], "ctx": v["ctx_1024"],
              "ctxT": v["ctx_1024"].transpose(0, 2, 1).reshape(B, KB, P, S).transpose(0, 2, 1, 3),
              "mask0": v["mask_BxSxS_ik0"], "mask1": v["mask_BxSxS2_if1"], "mask2": v["mask_BxSxS2_ik0"]}
    for n, (wq, wk, wv, wo, bq, bk, bv, bo, g, be, nw) in enumerate(ws):
        dk = ATT[n].dk
        arrays[f"w{n}"] = rows(np.concatenate([slots(wq, dk), slots(wk, dk), wv, wo], 1))
        arrays[f"col{n}"] = np.concatenate([slots(bq, dk).reshape(G, P), slots(bk, dk).reshape(G, P),
                                            nw.reshape(KB, P)]).T
        arrays[f"row{n}"] = spread(bv, bo, g, be)
    for st, w1, b1, w2, b2, g, be in (
            ("f0", v[L0 + "fc1_w"].T, v[L0 + "fc1_b"], v[L0 + "fc2_w"].T, v[L0 + "fc2_b"],
             v[L0 + "ln3_g"], v[L0 + "ln3_b"]),
            ("f2", v[L2 + "ff_w1"], v[L2 + "ff_b1"], v[L2 + "ff_w2"], v[L2 + "ff_b2"],
             v[L2 + "ln3_g"], v[L2 + "ln3_b"])):
        arrays[f"{st}w1"], arrays[f"{st}w2"] = rows(w1), rows(w2)
        arrays[f"{st}col"], arrays[f"{st}row"] = b1.reshape(-1, P).T, spread(b2, g, be)
    arrays["ew1"] = v[L1 + "exp_w1"].transpose(0, 2, 1).reshape(E, KB, P, HID).transpose(0, 2, 1, 3)
    arrays["ew2"] = v[L1 + "exp_w2"].transpose(0, 2, 1).reshape(E, HB, P, D).transpose(0, 2, 1, 3)
    arrays["sw1"], arrays["sw2"] = rows(v[L1 + "sh_w1"].T), rows(v[L1 + "sh_w2"].T)
    arrays["gw"] = rows(v[L1 + "gate_w"].T)
    arrays["norm3"] = v[L1 + "norm3_w"].reshape(KB, P).T

    bf16 = ml_dtypes.bfloat16
    p = np.arange(P)
    arrays["identf"] = np.eye(P, dtype=np.float32)
    arrays["identb"] = np.eye(P).astype(bf16)
    arrays["causal"] = np.where(p[None, :] > p[:, None], NEG, 0.0).astype(bf16)
    arrays["selq"] = (np.arange(P)[None, None, :] == (4 * np.arange(G)[None, :, None] + p[:, None, None] // 32))\
        .astype(np.float32)
    arrays["selh"] = np.broadcast_to(np.eye(P, 16)[:, :, None], (P, 16, P)).astype(bf16)
    arrays["iota"] = np.broadcast_to(np.arange(S, dtype=np.float32), (16, S))
    arrays["iota8"] = np.broadcast_to(np.arange(E, dtype=np.float32), (P, E))
    arrays["lowrow"] = np.stack([p % 32 >= 16, p % 64 >= 32], 1).astype(np.float32)

    nc = bacc.Bacc("TRN2", target_bir_lowering=False, num_devices=1)
    arrays = {name: np.ascontiguousarray(a) for name, a in arrays.items()}
    io = {name: nc.dram_tensor(f"in_{name}", a.shape, mybir.dt.from_np(a.dtype), kind="ExternalInput").ap()
          for name, a in arrays.items()}
    io["out"] = nc.dram_tensor("out", (B, S, D), F32, kind="ExternalOutput").ap()
    build(nc, io)
    r = run_bass_kernel_spmd(nc, [{f"in_{name}": a for name, a in arrays.items()}], core_ids=[0])
    return r.results[0]["out"]
```

```python
from contextlib import ExitStack

import concourse.bass as bass
from concourse import mybir

F32 = mybir.dt.float32
F32R = mybir.dt.float32r
BF16 = mybir.dt.bfloat16
I32 = mybir.dt.int32
U32 = mybir.dt.uint32
ALU = mybir.AluOpType
ACT = mybir.ActivationFunctionType
AX = mybir.AxisListType

B, S, D = 4, 512, 256
P = 128
KB = D // P
QT = S // P
NT = B * QT
E, HID = 8, 4 * D
HB = HID // P
SLOTS = 512
G = SLOTS // P
GS = 2 * G
BIG = float(2 ** 66)
WQ, WK, WV, WO, WEND = 0, 256, 512, 768, 1024
SELW = 512 + 64


class Stage:

    def __init__(self, name, dk=16, causal=False, mask=None, length=False, kv="self", rms=False,
                 wo=False, bias=False, ln=True, eps=1e-5):
        self.name, self.dk, self.causal, self.mask, self.length = name, dk, causal, mask, length
        self.kv, self.rms, self.wo, self.bias, self.ln, self.eps = kv, rms, wo, bias, ln, eps
        self.heads = D // dk
        self.slot = 2 * dk
        self.stack = 4 * dk
        self.per_stack = P // self.stack
        self.per_group = P // self.slot
        self.per_qt = self.heads // 2
        self.pairs = QT * self.per_qt
        self.group_pairs = self.per_group // 2
        jobs = [("x", 0, "A"), ("x", 1, "D")]
        if kv == "mctx":
            jobs += [("c", 0, "A"), ("c", 1, "D")]
        half = [[(kind, g, "AD"[g % 2]) for g in range(n * G, (n + 1) * G)] for kind in "QK" for n in range(KB)]
        jobs += [("q", 0, "D"), ("q", 1, "D"), *half[0], ("k", 0, "D"), *half[1], ("k", 1, "D"), *half[2], *half[3]]
        jobs += [("v", t, "D" if bias or t % 2 else "A") for t in range(QT)]
        self.jobs = jobs

    def width(self, qt):
        return (qt + 1) * P if self.causal else S

    def pair(self, i):
        return i // self.per_qt, 2 * (i % self.per_qt)

    def finishing(self, step, lag):
        n = step - lag + 1
        return n // self.per_qt - 1 if n > 0 and n % self.per_qt == 0 and n // self.per_qt <= QT else None


def freed(jobs, n):
    return (sum(e == "A" for _, _, e in jobs[:n]), sum(e == "D" for _, _, e in jobs[:n]))


ATT = [
    Stage("L0 self", causal=True, length=True),
    Stage("L0 cross", length=True, kv="mctx"),
    Stage("L1 self", mask=0, rms=True, wo=True, ln=False),
    Stage("L1 cross", mask=1, kv="ctx", rms=True, wo=True, ln=False),
    Stage("L2 self", mask=2, wo=True, bias=True),
    Stage("L2 cross", mask=1, kv="ctx", wo=True, bias=True),
    Stage("L3", dk=32, causal=True, kv="ctx", bias=True, eps=1e-6),
]


class Feed:

    def __init__(self, hb, masked):
        self.hb, self.masked = hb, masked
        self.jobs = [("x", 0, "A"), ("x", 1, "D")]
        self.jobs += [("h", n, "D" if n % 2 else "A") for n in range(hb)]
        self.jobs += [("o", t, "D") for t in range(QT)]


FEED = {"f0": Feed(D // P, True), "f2": Feed(HID // P, False)}
PREP = [("x", 0, "A"), ("x", 1, "D")] + [("g", t, "D") for t in range(QT)]
ORDER = ["a0", "a1", "f0", "a2", "a3", "prep", "moe", "a4", "a5", "f2", "a6"]
STEPS_AFTER = 9


class Signal:

    def __init__(self, sem, per, unit=1, after=None):
        self.sem, self.per, self.unit, self.base = sem, per, unit, {}
        total = self.start = 1 if unit == 1 else 0
        for st in ORDER:
            self.base[st] = total
            total += (per.get(st, 0) * B + (after or {}).get(st, 0)) * unit
        self.total = total

    def at(self, st, b, k):
        b, off = b if isinstance(b, tuple) else (b, 0)
        per = self.per.get(st, 0) * self.unit
        return b * per + (self.base[st] + off * per + k * self.unit)


def times(b, n, more=0):
    b, off = b if isinstance(b, tuple) else (b, 0)
    return b * n + (off * n + more)


def transition(prev, new):
    steps, jobs, out = [], [], []
    if prev:
        a = ATT[int(prev[0][1:])]
        steps = [("step", *prev, k) for k in range(a.pairs, a.pairs + STEPS_AFTER)]
    if new:
        a = ATT[int(new[0][1:])]
        out = [("tokens", *new, 0)]
        jobs = [("job", *new, j) for j in range(len(a.jobs))]
    while steps or jobs:
        out += steps[:1] + jobs[:3]
        steps, jobs = steps[1:], jobs[3:]
    return out + ([("length", *new, 0)] if new and a.length else [])


def attention_items(eng, st):
    n, a = ORDER.index(st), ATT[int(st[1:])]
    before = ORDER[n - 1] if n and ORDER[n - 1][0] == "a" else None

    def batch(prev, new):
        for item in transition(prev, new):
            yield item
        if new:
            for k in range(a.pairs):
                yield ("step", *new, k)

    yield from batch((before, B - 1) if before else None, (st, 0))
    with eng.Fori(1, B) as b:
        yield from batch((st, (b, -1)), (st, b))
    if n + 1 == len(ORDER) or ORDER[n + 1][0] != "a":
        yield from batch((st, B - 1), None)


def build(nc, io):
    ctx = ExitStack()
    with ctx:
        def sb(name, shape, dt):
            return ctx.enter_context(nc.sbuf_tensor(name, shape, dt))

        def sem(name):
            return ctx.enter_context(nc.semaphore(name))

        def signal(name, unit=1, after=None, **per):
            out = {}
            for key, n in per.items():
                for st in ORDER:
                    if st == key or (key == "att" and st[0] == "a") or (key == "feed" and st[0] == "f"):
                        out[st] = n(st) if callable(n) else n
            return Signal(sem(name), out, unit, after)

        att = {f"a{n}": s for n, s in enumerate(ATT)}

        X = sb("X", [P, NT, D], F32)
        wt = sb("wt", [P, 2, KB, WEND], F32)
        wcol = sb("wcol", [P, 2, 6], F32)
        wrow = sb("wrow", [P, 2, 4, D], F32)
        arena = sb("arena", [P, 4, QT * D], F32)
        xs = arena[:, 0, :].rearrange("p (q d) -> p q d", q=QT)
        cn = arena[:, 1, :].rearrange("p (q d) -> p q d", q=QT)
        cs = arena[:, 2, :].rearrange("p (q d) -> p q d", q=QT)
        kvT = arena[:, 3, :].rearrange("p (k n) -> p k n", k=KB)
        xT = sb("xT", [P, KB, S], F32)
        Q = sb("Q", [P, GS, S], F32R)
        K = sb("K", [P, GS, S], F32R)
        parts = sb("parts", [P, KB, 2, S], F32R)
        select = sb("select", [P, 2, SELW], F32R)
        V = sb("V", [P, QT, SLOTS], F32)
        prob = sb("prob", [P, 3, 2, S], F32)
        probT = sb("probT", [P, 3, 4 * S], F32)
        oT = sb("oT", [P, S], F32)
        o = sb("o", [P, D], F32)
        oTn = sb("oTn", [P, KB, P], F32)
        y = sb("y", [P, 2, D], F32)
        xh = sb("xh", [P, 2, D], F32)
        xg = sb("xg", [P, D], F32)
        junk = sb("junk", [P, D], F32)
        hT = [sb("hT", [P, HB, S], F32)[:, :, :],
              arena[:, :, :].rearrange("p a n -> p (a n)").rearrange("p (h n) -> p h n", h=HB)]
        maski = hT[0][:, 0:4, :].bitcast(I32)
        maskb = hT[0][:, 4:6, :].rearrange("p a n -> p (a n)").bitcast(BF16).rearrange("p (q n) -> p q n", q=QT)
        iota = hT[0][0:16, 0, :]
        selq = hT[0][:, 1:3, :].rearrange("p a n -> p (a n)").rearrange("p (g n) -> p g n", g=GS)
        wcolf = sb("wcolf", [P, HB], F32)
        wrowf = sb("wrowf", [P, 3, D], F32)
        norm3 = sb("norm3", [P, KB], F32)
        w1e = sb("w1e", [P, 2, KB, HID], F32)
        w2e = [prob[:, 0:2, :, :].rearrange("p a b n -> p (a b n)").rearrange("p (h n) -> p h n", h=HB),
               V[:, :, :].rearrange("p a b -> p (a b)").rearrange("p (h n) -> p h n", h=HB)]
        hnT = probT[:, 0:2, :].rearrange("p a n -> p (a n)").rearrange("p (k n) -> p k n", k=KB)
        identf = sb("identf", [P, P], F32)
        identb = sb("identb", [P, P], BF16)
        causal = sb("causal", [P, P], BF16)
        selh = sb("selh", [P, 16, P], BF16)
        selectf = probT[:, 0, 0:2 * SELW].rearrange("p (a n) -> p a n", a=2)
        gw = sb("gw", [P, KB, E], F32)
        iota8 = sb("iota8", [P, E], F32)
        epsilon = sb("epsilon", [P, 2], F32)
        minus_half = sb("minus_half", [P, 4], F32)
        qz = parts[:, 0, :, :].rearrange("p a n -> p (a n)").rearrange("p (g n) -> p g n", g=GS)
        nz = y[0:16, :, :].rearrange("p a n -> p (a n)")
        lens = sb("lens", [16, 4], F32)
        pen = sb("pen", [P, S], BF16)
        negm = sb("negm", [P, 4, 2], F32)
        rinv = sb("rinv", [P, 16, 1], F32)
        amax = sb("amax", [P, 2, QT], F32)
        keep = sb("keep", [P, 2, NT], F32)
        bn = sb("bn", [P, 2, 6], F32)
        mv = sb("mv", [P, 2, 2], F32)
        ve = sb("ve", [P, 2, 1], F32)
        rstd = sb("rstd", [P, 2, 1], F32)
        ss = sb("ss", [P, QT], F32)
        ms = sb("ms", [P, QT], F32)
        rs4 = sb("rs4", [P, QT], F32)
        lg = sb("lg", [P, E], F32)
        top = sb("top", [P, E], F32)
        topi = sb("topi", [P, E], U32)
        topf = sb("topf", [P, E], F32)
        gex = sb("gex", [P, 4], F32)
        gpart = sb("gpart", [P, 2, E], F32)
        gates = sb("gates", [P, E + 1, NT], F32)

        SB = [ctx.enter_context(nc.psum_tensor(f"scores{n}", [P, 2, S], F32)) for n in range(2)]
        TB = [ctx.enter_context(nc.psum_tensor(f"turned{n}", [P, S], F32)) for n in range(2)]
        OB = ctx.enter_context(nc.psum_tensor("outputs", [P, S], F32))
        MB = ctx.enter_context(nc.psum_tensor("mixed", [P, S], F32))
        RING = [SB[n // 2][:, n % 2, :] for n in range(4)]
        OUTS = [TB[0], TB[1], OB, MB]

        jobs_of = {st: (att[st].jobs if st in att else FEED[st].jobs if st in FEED else PREP)
                   for st in ORDER if st != "moe"}

        def nA(st):
            return freed(jobs_of[st], 99)[0]

        def nD(st):
            return freed(jobs_of[st], 99)[1]

        def njob(st):
            return len(jobs_of[st])

        def npair(st):
            return att[st].pairs

        def with_wo(st):
            return QT if att[st].wo else 0

        def with_ln(st):
            return QT if att[st].ln else 0

        PER_TURN = E // B
        UNITS = B
        ROUTED_H, ROUTED_O = UNITS * HB, UNITS * QT
        c_const = sem("c_const")
        c_x = sem("c_x")
        c_w = [sem("c_weights0"), sem("c_weights1")]
        c_ready = sem("c_ready")
        c_sel = sem("c_sel")
        c_select = sem("c_select")
        c_ones = sem("c_ones")
        c_keep = signal("c_keep", a0=1, a1=1)
        c_kv = signal("c_kv", 16, a1=1, a3=1, a5=1, a6=1)
        c_mask = signal("c_mask", 16, a2=1, a3=1, a4=1, a5=1)
        c_maskb = signal("c_maskb", a2=1, a3=1, a4=1, a5=1)
        c_xs = signal("c_xs", att=1, feed=1, prep=1)
        c_cs = signal("c_cs", a1=1)
        c_ss = signal("c_ss", a2=1, a3=1, prep=1)
        c_rs = signal("c_rs", a2=1, a3=1, prep=1)
        c_job = signal("c_job", att=njob, feed=njob, prep=njob, moe=PER_TURN * ROUTED_H,
                       after={"moe": ROUTED_H})
        c_hi = signal("c_hi", att=2 * KB)
        c_A = signal("c_A", att=nA, feed=nA, prep=nA, moe=PER_TURN * ROUTED_H,
                     after={"moe": ROUTED_H})
        c_D = signal("c_D", att=nD, feed=nD, prep=nD)
        c_qz = signal("c_qz", a0=1, a1=1)
        c_e0 = signal("c_e0", a0=1, a1=1)
        c_seen = sem("c_seen")
        c_pen = signal("c_pen", a0=1, a1=1)
        c_scores = signal("c_scores", att=npair)
        c_max = signal("c_max", att=npair)
        c_exp = signal("c_exp", att=npair)
        c_turn = signal("c_turn", att=lambda st: 2 * npair(st))
        c_tD = signal("c_tD", att=npair)
        c_tA = signal("c_tA", att=npair)
        c_pv = signal("c_pv", att=QT * G)
        c_oT = signal("c_oT", att=QT)
        c_on = signal("c_on", att=QT)
        c_o = signal("c_o", att=QT)
        c_ot = signal("c_ot", att=with_wo)
        c_otn = signal("c_otn", att=with_wo)
        c_y = signal("c_y", att=with_wo)
        c_yD = signal("c_yD", att=with_wo)
        c_var = signal("c_var", att=with_ln, feed=QT)
        c_rstd = signal("c_rstd", att=with_ln, feed=QT)
        c_xh = signal("c_xh", att=with_ln, feed=QT)
        c_xout = signal("c_xout", att=QT, feed=QT)
        c_hn = signal("c_hn", prep=1)
        c_gex = signal("c_gex", prep=QT)
        c_gate = signal("c_gate", prep=QT)
        c_w1 = [sem("c_first0"), sem("c_first1")]
        c_w2 = [sem("c_second0"), sem("c_second1")]
        c_wf = sem("c_wf")
        c_h = signal("c_h", moe=PER_TURN * ROUTED_O, after={"moe": ROUTED_O})
        c_hD = signal("c_hD", moe=PER_TURN * ROUTED_O, after={"moe": ROUTED_O})
        c_out = sem("c_out")

        block = ctx.enter_context(nc.Block())

        def tile(b, qt):
            return X[:, bass.ds(times(b, QT, qt), 1), :].rearrange("p o d -> p (o d)")

        def wait_x(eng, st, b):
            before = ORDER[ORDER.index(st) - 1]
            if st == "a0":
                eng.wait_ge(c_x, 16)
            elif before == "moe":
                eng.wait_ge(c_hD.sem, c_hD.total)
            else:
                eng.wait_ge(c_xout.sem, c_xout.at(before, b, QT))

        def wait_weights(eng, n):
            eng.wait_ge(c_w[n % 2], 48 * (n // 2 + 1))

        @block.sync
        def _(sp):
            sp.dma_start(X[:, :, :], io["x"].rearrange("b (q p) d -> p (b q) d", p=P)).then_inc(c_x, 16)
            for dst, name in ((identf, "identf"), (identb, "identb"), (causal, "causal"), (selq, "selq"),
                              (selh, "selh"), (iota, "iota"), (selectf, "select16"), (gw, "gw"),
                              (iota8, "iota8"), (norm3, "norm3")):
                sp.dma_start(dst[(slice(None),) * len(dst.shape)], io[name]).then_inc(c_const, 16)

            def weights(n):
                if n >= 2:
                    after = f"a{n - 1}"
                    sp.wait_ge(c_xout.sem, c_xout.at(after, 0, 0))
                    sp.wait_ge(c_pv.sem, c_pv.at(after, 0, 0))
                k = n % 2
                sp.dma_start(wt[:, k, :, :], io[f"w{n}"]).then_inc(c_w[k], 16)
                sp.dma_start(wcol[:, k, :], io[f"col{n}"]).then_inc(c_w[k], 16)
                sp.dma_start(wrow[:, k, :, :], io[f"row{n}"]).then_inc(c_w[k], 16)

            def batch_inputs(st, b):
                a = att[st]
                if a.kv == "ctx":
                    sp.wait_ge(c_job.sem, c_job.at(st, b, 0))
                    sp.dma_start(kvT, io["ctxT"][bass.ds(b, 1), :, :, :]
                                 .rearrange("o p k n -> (o p) k n")).then_inc(c_kv.sem, 16)
                if a.kv == "mctx":
                    sp.wait_ge(c_cs.sem, c_cs.at(st, b, 0))
                    sp.dma_start(cn, io["ctx"][bass.ds(b, 1), :, :]
                                 .rearrange("o (q p) d -> p (o q) d", p=P)).then_inc(c_kv.sem, 16)
                if a.mask is not None:
                    sp.wait_ge(c_maskb.sem, c_maskb.at(st, b, 0))
                    sp.dma_start(maski[:, :, :], io[f"mask{a.mask}"][bass.ds(b, 1), :, :]
                                 .rearrange("o (q p) n -> p (o q) n", p=P)).then_inc(c_mask.sem, 16)

            weights(0)
            weights(1)
            for st in ORDER:
                if st in att:
                    a, n = att[st], int(st[1:])
                    if st == "a4":
                        sp.wait_ge(c_hD.sem, c_hD.total)
                    if st == "a2":
                        sp.wait_ge(c_xout.sem, c_xout.at(st, 0, 0))
                    if st == "a6":
                        sp.wait_ge(c_pv.sem, c_pv.at(st, 0, 0))
                        sp.dma_start(selectf, io["select32"]).then_inc(c_sel, 16)
                    batch_inputs(st, 0)
                    if n >= 1 and n + 1 < len(ATT):
                        weights(n + 1)
                    if a.kv != "self" or a.mask is not None:
                        with sp.Fori(1, B) as b:
                            batch_inputs(st, b)
                elif st in FEED:
                    if st == "f2":
                        sp.wait_ge(c_h.sem, c_h.total)
                    hb = FEED[st].hb
                    sp.dma_start(w1e[:, 0, :, 0:hb * P], io[f"{st}w1"]).then_inc(c_wf, 16)
                    sp.dma_start(w1e[:, 1, :, :].rearrange("p k n -> p (k n)")[:, 0:hb * D]
                                 .rearrange("p (h n) -> p h n", h=hb), io[f"{st}w2"]).then_inc(c_wf, 16)
                    sp.dma_start(wrowf[:, :, :], io[f"{st}row"]).then_inc(c_wf, 16)
                    sp.dma_start(wcolf[:, 0:hb], io[f"{st}col"]).then_inc(c_wf, 16)
                elif st == "moe":
                    sp.wait_ge(c_pv.sem, c_pv.at("moe", 0, 0))

                    def expert(slot, w1, w2):
                        sp.dma_start(w1e[:, slot, :, :], w1).then_inc(c_w1[slot], 16)
                        sp.dma_start(w2e[slot], w2).then_inc(c_w2[slot], 16)

                    def routed(slot, e):
                        expert(slot, io["ew1"][bass.ds(e, 1), :, :, :].rearrange("o p k n -> (o p) k n"),
                               io["ew2"][bass.ds(e, 1), :, :, :].rearrange("o p k n -> (o p) k n"))

                    routed(0, 0)
                    routed(1, 1)
                    with sp.Fori(0, B - 1) as it:
                        for slot in range(PER_TURN):
                            sp.wait_ge(c_h.sem, c_h.at(st, it, (slot + 1) * ROUTED_O))
                            routed(slot, it * PER_TURN + (PER_TURN + slot))
                    sp.wait_ge(c_h.sem, c_h.at(st, B - 1, ROUTED_O))
                    expert(0, io["sw1"], io["sw2"])
            sp.wait_ge(c_xout.sem, c_xout.total)
            sp.dma_start(io["out"].rearrange("b (q p) d -> p (b q) d", p=P), X[:, :, :]).then_inc(c_out, 16)
            sp.wait_ge(c_out, 16)

        @block.gpsimd
        def _(pool):
            def layer_norm(st, b, qt, eps, gamma, beta):
                r = qt % 2
                pool.wait_ge(c_var.sem, c_var.at(st, b, qt + 1))
                pool.tensor_tensor(ve[:, r, :], mv[:, r, 1:2], eps_of[eps], ALU.add)
                pool.drain()
                pool.tensor_tensor(rstd[:, r, :], ve[:, r, :], minus_half[:, 0:1], ALU.pow)\
                    .then_inc(c_rstd.sem, 1)
                pool.wait_ge(c_xh.sem, c_xh.at(st, b, qt + 1))
                pool.tensor_tensor(xg[:, :], xh[:, r, :], gamma, ALU.mult)
                pool.drain()
                pool.tensor_tensor(tile(b, qt), xg[:, :], beta, ALU.add).then_inc(c_xout.sem, 1)

            def roots(st, b):
                pool.wait_ge(c_ss.sem, c_ss.at(st, b, 1))
                pool.tensor_tensor(rs4[:, :], ms[:, :], minus_half[:, :], ALU.pow).then_inc(c_rs.sem, 1)

            def stage_tokens(st, b):
                wait_x(pool, st, b)
                pool.wait_ge(c_job.sem, c_job.at(st, b, 0))
                pool.tensor_copy(xs, X[:, bass.ds(times(b, QT), QT), :]).then_inc(c_xs.sem, 1)

            def weights(n):
                a, k = ATT[n], n % 2
                wait_weights(pool, n)
                wq = wt[:, k, :, WQ:WK]
                pool.tensor_scalar(wq, wq, -a.dk ** -0.5, None, ALU.mult)
                pool.tensor_scalar(wcol[:, k, 0:KB], wcol[:, k, 0:KB], -a.dk ** -0.5, None, ALU.mult)
                pool.drain()
                pool.sem_inc(c_ready, 1)

            def ones(a):
                pool.memset(V[:, :, :], 0.0)
                pool.drain()
                pool.memset(V[:, :, :].rearrange("p t (h s) -> p (t h) s", s=a.slot)[:, :, a.dk:a.dk + 1],
                            1.0).then_inc(c_ones, 1)

            def attention(item, st, b, n):
                a = att[st]
                k = int(st[1:]) % 2
                if item == "tokens":
                    if a.rms:
                        roots(st, b)
                    else:
                        stage_tokens(st, b)
                    if a.kv == "mctx":
                        pool.wait_ge(c_keep.sem, c_keep.at(st, b, 1))
                        pool.wait_ge(c_kv.sem, c_kv.at(st, b, 1))
                        pool.wait_ge(c_job.sem, c_job.at(st, b, 0))
                        pool.tensor_tensor(cs, cn, keep[:, 1, bass.ds(times(b, QT), QT)].unsqueeze(2)
                                           .to_broadcast([P, QT, D]), ALU.mult).then_inc(c_cs.sem, 1)
                if item == "step" and n == 0 and type(b) is int and int(st[1:]) + 1 < len(ATT):
                    weights(int(st[1:]) + 1)
                if item == "step" and a.ln:
                    qt = a.finishing(n, 8 if a.wo else 6)
                    if qt is not None:
                        layer_norm(st, b, qt, a.eps, wrow[:, k, 2, :], wrow[:, k, 3, :])

            for s in (c_xs, c_cs, c_rs, c_rstd, c_xout, c_hn):
                pool.sem_inc(s.sem, s.start)
            eps_of = {eps: epsilon[:, n:n + 1] for n, eps in enumerate((1e-5, 1e-6))}
            for eps, column in eps_of.items():
                pool.memset(column, eps)
            pool.memset(minus_half[:, :], -0.5)
            pool.memset(gates[:, E, :], 1.0)
            ones(ATT[0])
            pool.wait_ge(c_const, 160)
            pool.drain()
            weights(0)
            for st in ORDER:
                if st in att:
                    n = int(st[1:])
                    if st == "a4":
                        pool.wait_ge(c_h.sem, c_h.total)
                        ones(ATT[4])
                    if st == "a6":
                        pool.wait_ge(c_pv.sem, c_pv.at(st, 0, 0))
                        ones(ATT[6])
                    for entry in attention_items(pool, st):
                        attention(*entry)
                elif st in FEED:
                    pool.wait_ge(c_wf, 64 if st == "f0" else 128)
                    with pool.Fori(0, B) as b:
                        stage_tokens(st, b)
                        for qt in range(QT):
                            layer_norm(st, b, qt, 1e-5, wrowf[:, 1, :], wrowf[:, 2, :])
                elif st == "prep":
                    with pool.Fori(0, B) as b:
                        roots(st, b)
                        pool.wait_ge(c_A.sem, c_A.at(st, b, 1))
                        pool.wait_ge(c_D.sem, c_D.at(st, b, 1))
                        pool.tensor_copy(hnT[:, :, bass.ds(b * S, S)], xT[:, :, :]).then_inc(c_hn.sem, 1)

        @block.tensor
        def _(pe):
            def turn_tokens(out, src, kb):
                for qt in range(QT):
                    last = pe.transpose(out[:, qt * P:(qt + 1) * P], src[:, qt, kb * P:(kb + 1) * P],
                                        identf[:, :])
                return last

            def bank_free(st, b, jobs, j):
                if j >= 4:
                    fa, fd = freed(jobs, j - 3)
                    if jobs[j - 4][2] == "A":
                        pe.wait_ge(c_A.sem, c_A.at(st, b, fa))
                    else:
                        pe.wait_ge(c_D.sem, c_D.at(st, b, fd))

            def all_free(st, b, jobs, n):
                fa, fd = freed(jobs, n)
                pe.wait_ge(c_A.sem, c_A.at(st, b, fa))
                pe.wait_ge(c_D.sem, c_D.at(st, b, fd))

            def scores(st, a, b, i):
                qt, h0 = a.pair(i)
                w = a.width(qt)
                if i == 0:
                    all_free(st, b, a.jobs, len(a.jobs))
                    if a.length:
                        pe.wait_ge(c_pen.sem, c_pen.at(st, b, 1))
                if i >= 2:
                    pe.wait_ge(c_exp.sem, c_exp.at(st, b, i - 1))
                out, rows, g = [], [], []
                for e in range(2):
                    s = (h0 + e) % a.per_stack
                    rows.append(slice(s * a.stack, (s + 1) * a.stack))
                    g.append((h0 + e) // a.per_stack)
                    out.append(SB[i % 2][:, e, 0:w])
                for e in range(2):
                    last = pe.matmul(out[e], Q[rows[e], g[e], qt * P:(qt + 1) * P], K[rows[e], g[e], 0:w],
                                     start=True, stop=not (a.causal or a.length))
                for e in range(2):
                    if a.length:
                        last = pe.matmul(out[e], selh[:, h0 + e, :], pen[:, 0:w], start=False,
                                         stop=not a.causal)
                    if a.causal:
                        last = pe.matmul(out[e][:, w - P:w], identb[:, :], causal[:, :], start=False, stop=True)
                last.then_inc(c_scores.sem, 1)

            def turns(st, a, b, i):
                qt, _ = a.pair(i)
                pe.wait_ge(c_exp.sem, c_exp.at(st, b, i + 1))
                for e in range(2):
                    free = c_tA if e else c_tD
                    pe.wait_ge(free.sem, free.at(st, b, i))
                    for kb in range(a.width(qt) // P):
                        last = pe.transpose(TB[e][:, kb * P:(kb + 1) * P],
                                            prob[:, i % 3, e, kb * P:(kb + 1) * P], identf[:, :])
                    last.then_inc(c_turn.sem, 1)

            def values(st, a, b, i):
                u = i // a.group_pairs
                qt, g = u // G, u % G
                pe.wait_ge(c_tD.sem, c_tD.at(st, b, i + 1))
                pe.wait_ge(c_tA.sem, c_tA.at(st, b, i + 1))
                if g == 0:
                    pe.wait_ge(c_oT.sem, c_oT.at(st, b, qt))
                blocks = a.width(qt) // P
                for kb in range(blocks):
                    for s in range(a.per_group):
                        rows = slice(s * a.slot, (s + 1) * a.slot)
                        h = g * a.per_group + s
                        last = pe.matmul(OB[rows, g * P:(g + 1) * P], V[:, kb, h * a.slot:(h + 1) * a.slot],
                                         probT[:, u % 3, s * S + kb * P:s * S + (kb + 1) * P],
                                         start=(kb == 0), stop=(kb == blocks - 1))
                last.then_inc(c_pv.sem, 1)

            def attention(item, st, b, n):
                a = att[st]
                k = int(st[1:]) % 2
                if item == "job":
                    kind, idx, _ = a.jobs[n]
                    bank = RING[n % 4]
                    if n == 0:
                        if type(b) is int and b == 0:
                            wait_weights(pe, int(st[1:]))
                            pe.wait_ge(c_ready, int(st[1:]) + 1)
                            pe.wait_ge(c_select, 1 + (st == "a6"))
                        all_free(st, b, a.jobs, 0)
                    if n in (0, 2) and not (st == "a0" and type(b) is int):
                        pe.wait_ge(c_exp.sem, c_exp.at(st, b, 0 if n else -1))
                    bank_free(st, b, a.jobs, n)
                    if kind == "x":
                        if idx == 0:
                            pe.wait_ge(c_xs.sem, c_xs.at(st, b, 1))
                        last = turn_tokens(bank, xs, idx)
                    elif kind == "c":
                        if idx == 0:
                            pe.wait_ge(c_cs.sem, c_cs.at(st, b, 1))
                        last = turn_tokens(bank, cs, idx)
                    elif kind in "qk":
                        if (kind, idx) == ("q", 0):
                            all_free(st, b, a.jobs, 2)
                        if (kind, idx) == ("k", 0):
                            if a.kv == "ctx":
                                pe.wait_ge(c_kv.sem, c_kv.at(st, b, 1))
                            if a.kv == "mctx":
                                all_free(st, b, a.jobs, 4)
                        src = xT if kind == "q" or a.kv == "self" else kvT
                        c0 = (WQ if kind == "q" else WK) + idx * P
                        for kb in range(KB):
                            last = pe.matmul(bank, wt[:, k, kb, c0:c0 + P], src[:, kb, :],
                                             start=(kb == 0), stop=(kb == KB - 1))
                    elif kind in "QK":
                        block, c0 = idx // G, idx % G * P
                        shift = a.dk if kind == "Q" else 2 * a.dk
                        if c0 == 0:
                            all_free(st, b, a.jobs, a.jobs.index((kind.lower(), block, "D")) + 1)
                        for part in range(2):
                            c = c0 + 64 - part * shift
                            last = pe.matmul(bank, select[:, "QK".index(kind), c:c + P], parts[:, block, part, :],
                                             start=(part == 0), stop=(part == 1))
                    else:
                        src = xT if a.kv == "self" else kvT
                        for kb in range(KB):
                            last = pe.matmul(bank[:, 0:D], src[:, kb, idx * P:(idx + 1) * P],
                                             wt[:, k, kb, WV:WO], start=(kb == 0), stop=(kb == KB - 1))
                    last.then_inc(c_job.sem, 1)
                if item == "length":
                    pe.wait_ge(c_qz.sem, c_qz.at(st, b, 1))
                    pe.wait_ge(c_o.sem, c_o.at(st, b, 0))
                    for g in range(GS):
                        last = pe.matmul(MB[:, :], qz[:, g, :], K[:, g, :], start=(g == 0), stop=(g == GS - 1))
                    last.then_inc(c_e0.sem, 1)
                if item == "step":
                    if n < a.pairs:
                        scores(st, a, b, n)
                    if 2 <= n < a.pairs + 2:
                        turns(st, a, b, n - 2)
                    i = n - 3
                    if 0 <= i < a.pairs and (i + 1) % a.group_pairs == 0:
                        values(st, a, b, i)
                    qt = a.finishing(n, 5)
                    if qt is not None:
                        pe.wait_ge(c_oT.sem, c_oT.at(st, b, qt + 1))
                        pe.wait_ge(c_o.sem, c_o.at(st, b, qt))
                        if a.wo:
                            pe.wait_ge(c_yD.sem, c_yD.at(st, b, qt))
                        for g in range(G):
                            last = pe.transpose(MB[:, g * P:(g + 1) * P], oT[:, g * P:(g + 1) * P],
                                                identf[:, :])
                        last.then_inc(c_on.sem, 1)
                    qt = a.finishing(n, 6) if a.wo else None
                    if qt is not None:
                        pe.wait_ge(c_o.sem, c_o.at(st, b, qt + 1))
                        for kb in range(KB):
                            last = pe.transpose(MB[:, kb * P:(kb + 1) * P], o[:, kb * P:(kb + 1) * P],
                                                identf[:, :])
                        last.then_inc(c_ot.sem, 1)
                    qt = a.finishing(n, 7) if a.wo else None
                    if qt is not None:
                        pe.wait_ge(c_otn.sem, c_otn.at(st, b, qt + 1))
                        for kb in range(KB):
                            last = pe.matmul(MB[:, 0:D], oTn[:, kb, :], wt[:, k, kb, WO:WEND],
                                             start=(kb == 0), stop=(kb == KB - 1))
                        last.then_inc(c_y.sem, 1)

            def feed(st):
                f = FEED[st]
                pe.wait_ge(c_wf, 64 if st == "f0" else 128)
                w2 = w1e[:, 1, :, :].rearrange("p k n -> p (k n)")
                with pe.Fori(0, B) as b:
                    pe.wait_ge(c_exp.sem, c_exp.at(st, b, 0))
                    all_free(st, b, f.jobs, 0)
                    for j, (kind, idx, _) in enumerate(f.jobs):
                        bank = RING[j % 4]
                        bank_free(st, b, f.jobs, j)
                        if kind == "x":
                            if idx == 0:
                                pe.wait_ge(c_xs.sem, c_xs.at(st, b, 1))
                            last = turn_tokens(bank, xs, idx)
                        elif kind == "h":
                            if idx == 0:
                                all_free(st, b, f.jobs, 2)
                            for kb in range(KB):
                                last = pe.matmul(bank, w1e[:, 0, kb, idx * P:(idx + 1) * P], xT[:, kb, :],
                                                 start=(kb == 0), stop=(kb == KB - 1))
                        else:
                            if idx == 0:
                                all_free(st, b, f.jobs, 2 + f.hb)
                            for n in range(f.hb):
                                last = pe.matmul(bank[:, 0:D], hT[0][:, n, idx * P:(idx + 1) * P],
                                                 w2[:, n * D:(n + 1) * D], start=(n == 0), stop=(n == f.hb - 1))
                        last.then_inc(c_job.sem, 1)

            def prepare(st):
                with pe.Fori(0, B) as b:
                    pe.wait_ge(c_exp.sem, c_exp.at(st, b, 0))
                    all_free(st, b, PREP, 0)
                    for j, (kind, idx, _) in enumerate(PREP):
                        bank = RING[j % 4]
                        bank_free(st, b, PREP, j)
                        if kind == "x":
                            if idx == 0:
                                pe.wait_ge(c_xs.sem, c_xs.at(st, b, 1))
                            last = turn_tokens(bank, xs, idx)
                        else:
                            if idx == 0:
                                all_free(st, b, PREP, 2)
                            for kb in range(KB):
                                last = pe.matmul(bank[:, 0:E], xT[:, kb, idx * P:(idx + 1) * P], gw[:, kb, :],
                                                 start=(kb == 0), stop=(kb == KB - 1))
                        last.then_inc(c_job.sem, 1)

            def experts(st):
                def hidden(it, unit, slot):
                    for n in range(HB):
                        j = unit * HB + n
                        bank = RING[j % 4]
                        if j >= 4:
                            pe.wait_ge(c_A.sem, c_A.at(st, it, j - 3))
                        for kb in range(KB):
                            last = pe.matmul(bank, w1e[:, slot, kb, n * P:(n + 1) * P],
                                             hnT[:, kb, (unit % UNITS) * S:(unit % UNITS + 1) * S],
                                             start=(kb == 0), stop=(kb == KB - 1))
                        last.then_inc(c_job.sem, 1)

                def outputs(it, unit, slot):
                    pe.wait_ge(c_A.sem, c_A.at(st, it, (unit + 1) * HB))
                    for t in range(QT):
                        j = unit * QT + t
                        pe.wait_ge(c_hD.sem, c_hD.at(st, it, j - 3) if j >= 4 else c_hD.at(st, it, 0))
                        for n in range(HB):
                            last = pe.matmul(OUTS[t][:, 0:D], hT[unit % 2][:, n, t * P:(t + 1) * P],
                                             w2e[slot][:, n, :], start=(n == 0), stop=(n == HB - 1))
                        last.then_inc(c_h.sem, 1)

                def turn(it, count, landed):
                    pe.wait_ge(c_A.sem, c_A.at(st, it, 0))
                    units = count * UNITS
                    for unit in range(units + 1):
                        if unit < units:
                            if unit % UNITS == 0:
                                pe.wait_ge(c_w1[unit // UNITS], landed)
                            hidden(it, unit, unit // UNITS)
                        if unit >= 1:
                            if (unit - 1) % UNITS == 0:
                                pe.wait_ge(c_w2[(unit - 1) // UNITS], landed)
                            outputs(it, unit - 1, (unit - 1) // UNITS)

                pe.wait_ge(c_hn.sem, c_hn.total)
                pe.wait_ge(c_D.sem, c_D.at(st, 0, 0))
                with pe.Fori(0, B) as it:
                    turn(it, PER_TURN, it * 16 + 16)
                turn(B, 1, 16 * (B + 1))

            for s in (c_job, c_e0, c_scores, c_turn, c_pv, c_on, c_ot, c_y, c_h):
                pe.sem_inc(s.sem, s.start)
            pe.wait_ge(c_const, 160)
            for st in ORDER:
                if st in att:
                    for entry in attention_items(pe, st):
                        attention(*entry)
                elif st in FEED:
                    feed(st)
                elif st == "prep":
                    prepare(st)
                else:
                    experts(st)

        @block.scalar
        def _(act):
            def attention(item, st, b, n):
                a = att[st]
                k = int(st[1:]) % 2
                if item == "job":
                    kind, idx, eng = a.jobs[n]
                    if eng == "D" and kind not in "qk":
                        return
                    if n == 0 and type(b) is int:
                        wait_weights(act, int(st[1:]))
                        act.wait_ge(c_ready, int(st[1:]) + 1)
                        act.wait_ge(c_ones, 1 + (st in ("a4", "a5", "a6")) + (st == "a6"))
                    bank = RING[n % 4]
                    act.wait_ge(c_job.sem, c_job.at(st, b, n + 1))
                    if kind in "qk":
                        col = idx + (KB if kind == "k" else 0)
                        act.activation(parts[:, idx, 0, :], bank, ACT.Identity,
                                       bias=wcol[:, k, col:col + 1], scale=1.0).then_inc(c_hi.sem, 1)
                    elif kind in "QK":
                        act.activation((Q if kind == "Q" else K)[:, idx, :], bank, ACT.Copy)\
                            .then_inc(c_A.sem, 1)
                    elif kind == "x":
                        if a.rms:
                            act.activation(xT[:, idx, :], bank, ACT.Identity, bias=0.0,
                                           scale=wcol[:, k, 4 + idx:5 + idx]).then_inc(c_A.sem, 1)
                        else:
                            act.activation(xT[:, idx, :], bank, ACT.Copy).then_inc(c_A.sem, 1)
                    elif kind == "c":
                        act.activation(kvT[:, idx, :], bank, ACT.Copy).then_inc(c_A.sem, 1)
                    else:
                        act.activation(V[:, idx, :].rearrange("p (h s) -> p h s", s=a.slot)[:, :, 0:a.dk],
                                       bank[:, 0:D].rearrange("p (h s) -> p h s", s=a.dk), ACT.Copy)\
                            .then_inc(c_A.sem, 1)
                if item == "step":
                    qt = a.finishing(n, 4)
                    if qt is not None:
                        act.wait_ge(c_pv.sem, c_pv.at(st, b, (qt + 1) * G))
                        act.wait_ge(c_on.sem, c_on.at(st, b, qt))
                        act.activation(oT[:, :], OB[:, :], ACT.Copy).then_inc(c_oT.sem, 1)
                    i = n - 2
                    if 0 <= i < a.pairs:
                        t, h0 = a.pair(i)
                        u, s, w = i // a.group_pairs, (h0 + 1) % a.per_group, a.width(t)
                        act.wait_ge(c_turn.sem, c_turn.at(st, b, 2 * i + 2))
                        if u >= 3:
                            act.wait_ge(c_pv.sem, c_pv.at(st, b, u - 2))
                        act.activation(probT[:, u % 3, s * S:s * S + w], TB[1][:, 0:w], ACT.Copy)\
                            .then_inc(c_tA.sem, 1)
                    if n < a.pairs:
                        t, _ = a.pair(n)
                        w = a.width(t)
                        act.wait_ge(c_max.sem, c_max.at(st, b, n + 1))
                        if n >= 3:
                            act.wait_ge(c_turn.sem, c_turn.at(st, b, 2 * (n - 2)))
                        for e in range(2):
                            last = act.activation(prob[:, n % 3, e, 0:w], SB[n % 2][:, e, 0:w],
                                                  ACT.Exp, bias=negm[:, n % 4, e:e + 1], scale=-1.0)
                        last.then_inc(c_exp.sem, 1)
                    qt = a.finishing(n, 6) if a.wo else None
                    if qt is not None:
                        act.wait_ge(c_ot.sem, c_ot.at(st, b, qt + 1))
                        act.wait_ge(c_y.sem, c_y.at(st, b, qt))
                        act.activation(oTn[:, :, :].rearrange("p k n -> p (k n)"), MB[:, 0:D], ACT.Copy)\
                            .then_inc(c_otn.sem, 1)

            def feed(st):
                f = FEED[st]
                act.wait_ge(c_wf, 64 if st == "f0" else 128)
                with act.Fori(0, B) as b:
                    for j, (kind, idx, eng) in enumerate(f.jobs):
                        if eng == "D":
                            continue
                        act.wait_ge(c_job.sem, c_job.at(st, b, j + 1))
                        if kind == "x":
                            act.activation(xT[:, idx, :], RING[j % 4], ACT.Copy).then_inc(c_A.sem, 1)
                        else:
                            act.activation(hT[0][:, idx, :], RING[j % 4], ACT.Relu, bias=wcolf[:, idx:idx + 1],
                                           scale=1.0).then_inc(c_A.sem, 1)

            def prepare(st):
                with act.Fori(0, B) as b:
                    act.wait_ge(c_job.sem, c_job.at(st, b, 1))
                    act.wait_ge(c_hn.sem, c_hn.at(st, b, 0))
                    act.activation(xT[:, 0, :], RING[0], ACT.Identity, bias=0.0, scale=norm3[:, 0:1])\
                        .then_inc(c_A.sem, 1)
                    for t in range(QT):
                        act.wait_ge(c_gex.sem, c_gex.at(st, b, t + 1))
                        act.activation(gex[:, 1:2], gex[:, 0:1], ACT.Exp).then_inc(c_gate.sem, 1)

            def experts(st):
                def turn(it, count):
                    for unit in range(count * UNITS):
                        act.wait_ge(c_h.sem, c_h.at(st, it, (unit - 1) * QT) if unit >= 2 else c_h.at(st, it, 0))
                        for n in range(HB):
                            j = unit * HB + n
                            act.wait_ge(c_job.sem, c_job.at(st, it, j + 1))
                            act.activation(hT[unit % 2][:, n, :], RING[j % 4], ACT.Silu).then_inc(c_A.sem, 1)

                with act.Fori(0, B) as it:
                    turn(it, PER_TURN)
                turn(B, 1)

            for s in (c_hi, c_A, c_exp, c_tA, c_oT, c_otn, c_gate):
                act.sem_inc(s.sem, s.start)
            act.wait_ge(c_const, 160)
            act.activation(select[:, :, :], selectf, ACT.Copy).then_inc(c_select, 1)
            for st in ORDER:
                if st == "a6":
                    act.wait_ge(c_sel, 16)
                    act.wait_ge(c_job.sem, c_job.at(st, 0, 0))
                    act.activation(select[:, :, :], selectf, ACT.Copy).then_inc(c_select, 1)
                if st in att:
                    for entry in attention_items(act, st):
                        attention(*entry)
                elif st in FEED:
                    feed(st)
                elif st == "prep":
                    prepare(st)
                else:
                    experts(st)

        @block.vector
        def _(dve):
            def squares(st, b):
                dve.wait_ge(c_job.sem, c_job.at(st, b, 0))
                tiles = X[:, bass.ds(times(b, QT), QT), :]
                dve.tensor_tensor(xs, tiles, tiles, ALU.mult)
                dve.drain()
                dve.tensor_reduce(ss[:, :], xs, AX.X, ALU.add)
                dve.drain()
                dve.tensor_scalar(ms[:, :], ss[:, :], 1.0 / D, 1e-5, ALU.mult, ALU.add).then_inc(c_ss.sem, 1)
                dve.wait_ge(c_rs.sem, c_rs.at(st, b, 1))
                dve.tensor_tensor(xs, tiles, rs4[:, :].unsqueeze(2).to_broadcast([P, QT, D]), ALU.mult)\
                    .then_inc(c_xs.sem, 1)

            def moments(st, b, qt):
                r = qt % 2
                dve.drain()
                dve.bn_stats(bn[:, r, :], y[:, r, :])
                dve.drain()
                dve.bn_aggr(mv[:, r, :], bn[:, r, :]).then_inc(c_var.sem, 1)

            def centre(st, b, qt):
                r = qt % 2
                dve.wait_ge(c_rstd.sem, c_rstd.at(st, b, qt + 1))
                dve.wait_ge(c_xout.sem, c_xout.at(st, b, qt))
                dve.tensor_scalar(xh[:, r, :], y[:, r, :], mv[:, r, 0:1], rstd[:, r, :], ALU.subtract,
                                  ALU.mult).then_inc(c_xh.sem, 1)

            def lengths(st, b):
                dve.drain()
                dve.tensor_tensor(qz[:, :, :], Q[:, :, 0:1].bitcast(F32).to_broadcast([P, GS, P]),
                                  selq[:, :, :], ALU.mult).then_inc(c_qz.sem, 1)
                dve.wait_ge(c_e0.sem, c_e0.at(st, b, 1))
                dve.tensor_scalar(nz[:, :], MB[0:16, :], 0.0, None, ALU.not_equal)
                dve.drain()
                dve.tensor_reduce(lens[:, 0:1], nz[:, :], AX.X, ALU.add)
                dve.drain()
                dve.reciprocal(lens[:, 1:2], lens[:, 0:1])
                dve.tensor_scalar(nz[:, :], iota[:, :], lens[:, 0:1], BIG, ALU.is_ge, ALU.mult)
                dve.drain()
                dve.tensor_scalar(lens[:, 2:3], lens[:, 1:2], 0.0, None, ALU.mult)
                dve.drain()
                dve.tensor_scalar(pen[0:16, :], nz[:, :], lens[:, 2:3], None, ALU.add).then_inc(c_pen.sem, 1)

            def attention(item, st, b, n):
                a = att[st]
                k = int(st[1:]) % 2
                if item == "tokens":
                    if type(b) is int:
                        wait_weights(dve, int(st[1:]))
                        dve.wait_ge(c_ready, int(st[1:]) + 1)
                    if a.rms or a.length:
                        wait_x(dve, st, b)
                    if a.length:
                        which = int(st[1:])
                        dve.tensor_reduce(amax[:, which, :], X[:, bass.ds(times(b, QT), QT), :], AX.X, ALU.max,
                                          apply_absolute_value=True)
                        dve.drain()
                        dve.tensor_scalar(keep[:, which, bass.ds(times(b, QT), QT)], amax[:, which, :], 0.0, None,
                                          ALU.is_gt).then_inc(c_keep.sem, 1)
                    if a.rms:
                        squares(st, b)
                    if a.mask is not None:
                        dve.drain()
                        dve.wait_ge(c_mask.sem, c_mask.at(st, b, 1))
                        dve.tensor_scalar(maskb[:, :, :], maski[:, :, :], 0.0, BIG, ALU.is_equal,
                                          ALU.mult).then_inc(c_maskb.sem, 1)
                        dve.drain()
                if item == "job":
                    kind, idx, eng = a.jobs[n]
                    if eng == "A":
                        return
                    bank = RING[n % 4]
                    if kind in "qk":
                        hi = sum(x[0] in "qk" for x in a.jobs[:n + 1])
                        dve.wait_ge(c_hi.sem, c_hi.at(st, b, hi))
                        col = idx + (KB if kind == "k" else 0)
                        dve.scalar_tensor_tensor(
                            out=parts[:, idx, 1, :], in0=bank, scalar=wcol[:, k, col:col + 1],
                            in1=parts[:, idx, 0, :].bitcast(F32), op0=ALU.add, op1=ALU.subtract)\
                            .then_inc(c_D.sem, 1)
                        return
                    dve.wait_ge(c_job.sem, c_job.at(st, b, n + 1))
                    if kind == "x" and a.rms:
                        dve.tensor_scalar(xT[:, idx, :], bank, wcol[:, k, 4 + idx:5 + idx], None,
                                          ALU.mult).then_inc(c_D.sem, 1)
                    elif kind == "x":
                        dve.tensor_copy(xT[:, idx, :], bank).then_inc(c_D.sem, 1)
                    elif kind in "QK":
                        dve.tensor_copy((Q if kind == "Q" else K)[:, idx, :], bank).then_inc(c_D.sem, 1)
                    elif kind == "c":
                        dve.tensor_copy(kvT[:, idx, :], bank).then_inc(c_D.sem, 1)
                    else:
                        if type(b) is int:
                            dve.wait_ge(c_ones, 1 + (st in ("a4", "a5", "a6")) + (st == "a6"))
                        dst = V[:, idx, :].rearrange("p (h s) -> p h s", s=a.slot)[:, :, 0:a.dk]
                        src = bank[:, 0:D].rearrange("p (h s) -> p h s", s=a.dk)
                        if a.bias:
                            dve.tensor_tensor(dst, src, wrow[:, k, 0, :].rearrange("p (h s) -> p h s", s=a.dk),
                                              ALU.add).then_inc(c_D.sem, 1)
                        else:
                            dve.tensor_copy(dst, src).then_inc(c_D.sem, 1)
                if item == "length":
                    lengths(st, b)
                if item == "step":
                    def least(e):
                        t, _ = a.pair(n)
                        sc, out = SB[n % 2][:, e, 0:a.width(t)], negm[:, n % 4, e:e + 1]
                        if a.mask is None:
                            return dve.tensor_reduce(out, sc, AX.X, ALU.min)
                        return dve.tensor_tensor_reduce(sc, sc, maskb[:, t, :], 1.0, BIG * 2, ALU.add, ALU.min, out)

                    if n < a.pairs:
                        dve.wait_ge(c_scores.sem, c_scores.at(st, b, n + 1))
                        if a.mask is not None:
                            dve.sem_inc(c_seen, 1)
                        least(0)
                    i = n - 2
                    if 0 <= i < a.pairs:
                        t, h0 = a.pair(i)
                        u, s, w = i // a.group_pairs, h0 % a.per_group, a.width(t)
                        dve.wait_ge(c_turn.sem, c_turn.at(st, b, 2 * i + 1))
                        if u >= 3:
                            dve.wait_ge(c_pv.sem, c_pv.at(st, b, u - 2))
                        dve.tensor_copy(probT[:, u % 3, s * S:s * S + w], TB[0][:, 0:w])\
                            .then_inc(c_tD.sem, 1)
                    if n < a.pairs:
                        least(1).then_inc(c_max.sem, 1)
                    qt = a.finishing(n, 5)
                    if qt is not None:
                        view = MB[:, :].rearrange("p (h s) -> p h s", s=a.slot)
                        r = rinv[:, 0:a.heads, :]
                        dve.wait_ge(c_on.sem, c_on.at(st, b, qt + 1))
                        dve.reciprocal(r, view[:, :, a.dk:a.dk + 1])
                        dve.drain()
                        if a.length:
                            dve.tensor_scalar(r, r, keep[:, int(st[1:]), bass.ds(times(b, QT, qt), 1)], None,
                                              ALU.mult)
                            dve.drain()
                        dve.tensor_tensor(o[:, :].rearrange("p (h s) -> p h s", s=a.dk), view[:, :, 0:a.dk],
                                          r.to_broadcast([P, a.heads, a.dk]), ALU.mult).then_inc(c_o.sem, 1)
                        if not a.wo:
                            dve.drain()
                            dve.tensor_tensor(y[:, qt % 2, :], o[:, :], tile(b, qt), ALU.add)
                            moments(st, b, qt)
                    qt = a.finishing(n, 7) if a.wo else None
                    if qt is not None:
                        dve.wait_ge(c_y.sem, c_y.at(st, b, qt + 1))
                        if not a.ln:
                            dve.tensor_tensor(y[:, qt % 2, :], MB[:, 0:D], tile(b, qt), ALU.add)\
                                .then_inc(c_yD.sem, 1)
                            dve.drain()
                            dve.tensor_copy(tile(b, qt), y[:, qt % 2, :]).then_inc(c_xout.sem, 1)
                        else:
                            dve.tensor_tensor(junk[:, :], MB[:, 0:D], wrow[:, k, 1, :], ALU.add)\
                                .then_inc(c_yD.sem, 1)
                            dve.drain()
                            dve.tensor_tensor(y[:, qt % 2, :], junk[:, :], tile(b, qt), ALU.add)
                            moments(st, b, qt)
                    qt = a.finishing(n, 8 if a.wo else 6) if a.ln else None
                    if qt is not None:
                        centre(st, b, qt)

            def feed(st):
                f = FEED[st]
                dve.wait_ge(c_wf, 64 if st == "f0" else 128)
                wait_x(dve, st, B - 1)
                with dve.Fori(0, B) as b:
                    for j, (kind, idx, eng) in enumerate(f.jobs):
                        if eng == "A":
                            continue
                        bank = RING[j % 4]
                        dve.wait_ge(c_job.sem, c_job.at(st, b, j + 1))
                        if kind == "x":
                            dve.tensor_copy(xT[:, idx, :], bank).then_inc(c_D.sem, 1)
                        elif kind == "h":
                            dve.tensor_scalar(hT[0][:, idx, :], bank, wcolf[:, idx:idx + 1], 0.0, ALU.add,
                                              ALU.max).then_inc(c_D.sem, 1)
                        else:
                            dve.tensor_tensor(junk[:, :], bank[:, 0:D], wrowf[:, 0, :], ALU.add)\
                                .then_inc(c_D.sem, 1)
                            dve.drain()
                            if f.masked:
                                dve.scalar_tensor_tensor(
                                    out=y[:, idx % 2, :], in0=junk[:, :],
                                    scalar=keep[:, 0, bass.ds(times(b, QT, idx), 1)], in1=tile(b, idx),
                                    op0=ALU.mult, op1=ALU.add)
                            else:
                                dve.tensor_tensor(y[:, idx % 2, :], junk[:, :], tile(b, idx), ALU.add)
                            moments(st, b, idx)
                            if idx >= 1:
                                centre(st, b, idx - 1)
                    centre(st, b, QT - 1)

            def prepare(st):
                wait_x(dve, st, B - 1)
                with dve.Fori(0, B) as b:
                    squares(st, b)
                    dve.wait_ge(c_job.sem, c_job.at(st, b, 2))
                    dve.wait_ge(c_hn.sem, c_hn.at(st, b, 0))
                    dve.tensor_scalar(xT[:, 1, :], RING[1], norm3[:, 1:2], None, ALU.mult).then_inc(c_D.sem, 1)
                    for t in range(QT):
                        dve.wait_ge(c_job.sem, c_job.at(st, b, 3 + t))
                        dve.tensor_copy(lg[:, :], RING[(2 + t) % 4][:, 0:E]).then_inc(c_D.sem, 1)
                        dve.drain()
                        dve.max(top[:, :], lg[:, :])
                        dve.drain()
                        dve.tensor_tensor(gex[:, 0:1], top[:, 1:2], top[:, 0:1], ALU.subtract)\
                            .then_inc(c_gex.sem, 1)
                        dve.max_index(topi[:, :], top[:, :], lg[:, :])
                        dve.drain()
                        dve.tensor_copy(topf[:, :], topi[:, :])
                        dve.wait_ge(c_gate.sem, c_gate.at(st, b, t + 1))
                        dve.tensor_scalar(gex[:, 2:3], gex[:, 1:2], 1.0, None, ALU.add)
                        dve.drain()
                        dve.reciprocal(gex[:, 2:3], gex[:, 2:3])
                        dve.drain()
                        dve.tensor_tensor(gex[:, 3:4], gex[:, 1:2], gex[:, 2:3], ALU.mult)
                        dve.drain()
                        for c in range(2):
                            dve.tensor_scalar(gpart[:, c, :], iota8[:, :], topf[:, c:c + 1], gex[:, 2 + c:3 + c],
                                              ALU.is_equal, ALU.mult)
                        dve.drain()
                        dve.tensor_tensor(gates[:, 0:E, bass.ds(b * QT + t, 1)].rearrange("p e o -> p (e o)"),
                                          gpart[:, 0, :], gpart[:, 1, :], ALU.add)

            def experts(st):
                def turn(it, count):
                    for unit in range(count * UNITS):
                        for t in range(QT):
                            j = unit * QT + t
                            n = (unit % UNITS) * QT + t
                            dve.wait_ge(c_h.sem, c_h.at(st, it, j + 1))
                            dve.scalar_tensor_tensor(
                                out=X[:, n, :], in0=OUTS[t][:, 0:D],
                                scalar=(gates[:, bass.ds(it * PER_TURN + unit // UNITS, 1), n:n + 1]
                                        .rearrange("p o n -> p (o n)") if count > 1 else gates[:, E, n:n + 1]),
                                in1=X[:, n, :], op0=ALU.mult, op1=ALU.add).then_inc(c_hD.sem, 1)

                dve.drain()
                with dve.Fori(0, B) as it:
                    turn(it, PER_TURN)
                turn(B, 1)

            for s in (c_keep, c_maskb, c_ss, c_D, c_qz, c_pen, c_max, c_tD, c_o, c_yD, c_var, c_xh, c_gex, c_hD):
                dve.sem_inc(s.sem, s.start)
            dve.memset(pen[:, :], 0.0)
            dve.wait_ge(c_const, 160)
            for st in ORDER:
                if st in att:
                    for entry in attention_items(dve, st):
                        attention(*entry)
                elif st in FEED:
                    feed(st)
                elif st == "prep":
                    prepare(st)
                else:
                    experts(st)


def kernel(**inputs):
    import ml_dtypes
    import numpy as np
    import concourse.bacc as bacc
    from concourse.bass_utils import run_bass_kernel_spmd

    v = {name: np.asarray(a) for name, a in inputs.items()}

    def rows(w):
        return w.reshape(-1, P, w.shape[-1]).transpose(1, 0, 2)

    zero = np.zeros(D, np.float32)
    zeros = np.zeros((D, D), np.float32)

    def heads(w):
        return w.transpose(1, 0, 2).reshape(D, D)

    L0, L1, L2, L3 = "L0_xattn_", "L1_xattn_", "L2_xattn_", "L3_xattn_"
    ws = []
    for n in (1, 2):
        ws.append([heads(v[f"{L0}W{c}{n}"]) for c in "qkv"] + [zeros, zero, zero, zero, zero,
                  v[f"{L0}ln{n}_g"], v[f"{L0}ln{n}_b"], zero])
    for n, p in ((1, "sa"), (2, "ca")):
        ws.append([v[f"{L1}{p}_w{c}"].T for c in "qkvo"] + [zero] * 6 + [v[f"{L1}norm{n}_w"]])
    for n, p in ((1, "sa"), (2, "ca")):
        ws.append([v[f"{L2}{p}_w{c}"] for c in "qkvo"] + [v[f"{L2}{p}_b{c}"] for c in "qkvo"]
                  + [v[f"{L2}ln{n}_g"], v[f"{L2}ln{n}_b"], zero])
    ws.append([v[f"{L3}W{c}"] for c in "qkv"] + [zeros] + [v[f"{L3}b{c}"] for c in "qkv"]
              + [zero, v[f"{L3}gamma"], v[f"{L3}beta"], zero])

    def spread(*vectors):
        return np.broadcast_to(np.stack(vectors)[None], (P, len(vectors), D))

    arrays = {"x": v["x"], "ctx": v["ctx_1024"],
              "ctxT": v["ctx_1024"].transpose(0, 2, 1).reshape(B, KB, P, S).transpose(0, 2, 1, 3),
              "mask0": v["mask_BxSxS_ik0"], "mask1": v["mask_BxSxS2_if1"], "mask2": v["mask_BxSxS2_ik0"]}
    for n, (wq, wk, wv, wo, bq, bk, bv, bo, g, be, nw) in enumerate(ws):
        arrays[f"w{n}"] = rows(np.concatenate([wq, wk, wv, wo], 1))
        arrays[f"col{n}"] = np.concatenate([bq.reshape(KB, P), bk.reshape(KB, P), nw.reshape(KB, P)]).T
        arrays[f"row{n}"] = spread(bv, bo, g, be)
    for st, w1, b1, w2, b2, g, be in (
            ("f0", v[L0 + "fc1_w"].T, v[L0 + "fc1_b"], v[L0 + "fc2_w"].T, v[L0 + "fc2_b"],
             v[L0 + "ln3_g"], v[L0 + "ln3_b"]),
            ("f2", v[L2 + "ff_w1"], v[L2 + "ff_b1"], v[L2 + "ff_w2"], v[L2 + "ff_b2"],
             v[L2 + "ln3_g"], v[L2 + "ln3_b"])):
        arrays[f"{st}w1"], arrays[f"{st}w2"] = rows(w1), rows(w2)
        arrays[f"{st}col"], arrays[f"{st}row"] = b1.reshape(-1, P).T, spread(b2, g, be)
    arrays["ew1"] = v[L1 + "exp_w1"].transpose(0, 2, 1).reshape(E, KB, P, HID).transpose(0, 2, 1, 3)
    arrays["ew2"] = v[L1 + "exp_w2"].transpose(0, 2, 1).reshape(E, HB, P, D).transpose(0, 2, 1, 3)
    arrays["sw1"], arrays["sw2"] = rows(v[L1 + "sh_w1"].T), rows(v[L1 + "sh_w2"].T)
    arrays["gw"] = rows(v[L1 + "gate_w"].T)
    arrays["norm3"] = v[L1 + "norm3_w"].reshape(KB, P).T

    bf16 = ml_dtypes.bfloat16
    p = np.arange(P)
    arrays["identf"] = np.eye(P, dtype=np.float32)
    arrays["identb"] = np.eye(P).astype(bf16)
    arrays["causal"] = np.where(p[None, :] > p[:, None], BIG, 0.0).astype(bf16)
    arrays["selq"] = (np.arange(P)[None, None, :] == (2 * np.arange(GS)[None, :, None] + p[:, None, None] // 64))\
        .astype(np.float32)
    arrays["selh"] = np.broadcast_to(np.eye(P, 16)[:, :, None], (P, 16, P)).astype(bf16)
    arrays["iota"] = np.broadcast_to(np.arange(S, dtype=np.float32), (16, S))
    arrays["iota8"] = np.broadcast_to(np.arange(E, dtype=np.float32), (P, E))
    column = np.arange(SELW)[None, :] - 64
    for dk in (16, 32):
        own = (column >= 0) & (column // (4 * dk) == p[:, None] // dk) & (column % dk == p[:, None] % dk)
        which = column // dk % 4
        arrays[f"select{dk}"] = np.stack([own & (which % 2 == 0), own & (which < 2)], 1).astype(np.float32)

    nc = bacc.Bacc("TRN2", target_bir_lowering=False, num_devices=1)
    arrays = {name: np.ascontiguousarray(a) for name, a in arrays.items()}
    io = {name: nc.dram_tensor(f"in_{name}", a.shape, mybir.dt.from_np(a.dtype), kind="ExternalInput").ap()
          for name, a in arrays.items()}
    io["out"] = nc.dram_tensor("out", (B, S, D), F32, kind="ExternalOutput").ap()
    build(nc, io)
    r = run_bass_kernel_spmd(nc, [{f"in_{name}": a for name, a in arrays.items()}], core_ids=[0])
    return r.results[0]["out"]
```

```python
from contextlib import ExitStack

import concourse.bass as bass
from concourse import mybir

F32 = mybir.dt.float32
F32R = mybir.dt.float32r
BF16 = mybir.dt.bfloat16
I32 = mybir.dt.int32
U32 = mybir.dt.uint32
ALU = mybir.AluOpType
ACT = mybir.ActivationFunctionType
AX = mybir.AxisListType

B, S, D = 4, 512, 256
P = 128
KB = D // P
QT = S // P
NT = B * QT
E, HID = 8, 4 * D
HB = HID // P
SLOTS = 512
G = SLOTS // P
GS = 2 * G
BIG = float(2 ** 66)
WQ, WK, WV, WO, WEND = 0, 256, 512, 768, 1024
SELW = 512 + 64


class Stage:

    def __init__(self, name, dk=16, causal=False, mask=None, length=False, kv="self", rms=False,
                 wo=False, bias=False, ln=True, eps=1e-5):
        self.name, self.dk, self.causal, self.mask, self.length = name, dk, causal, mask, length
        self.kv, self.rms, self.wo, self.bias, self.ln, self.eps = kv, rms, wo, bias, ln, eps
        self.heads = D // dk
        self.slot = 2 * dk
        self.stack = 4 * dk
        self.per_stack = P // self.stack
        self.per_group = P // self.slot
        self.unit = self.per_group
        self.half = G * self.unit
        self.pairs = 2 * self.half
        self.later = 3 if wo else 1
        self.after = (9 if wo else 7) + self.later
        jobs = [("x", 0, "A"), ("x", 1, "D")]
        if kv == "mctx":
            jobs += [("c", 0, "A"), ("c", 1, "D")]
        half = [[(kind, g, "AD"[g % 2]) for g in range(n * G, (n + 1) * G)] for kind in "QK" for n in range(KB)]
        jobs += [("q", 0, "D"), ("q", 1, "D"), *half[0], ("k", 0, "D"), *half[1], ("k", 1, "D"), *half[2], *half[3]]
        self.jobs = jobs
        self.values = "DDDD" if bias else "ADAD"

    def width(self, qt):
        return (qt + 1) * P if self.causal else S

    def pair(self, i):
        u, r = i // self.unit, i % self.unit
        return u // G * 2 + 2 * r // self.unit, u % G * self.per_group + 2 * r % self.unit

    def place(self, i, e):
        qt, h0 = self.pair(i)
        return i // self.unit % 2, (h0 + e) % self.per_group, qt % 2

    def finishing(self, step, lag):
        for qt in range(QT):
            if step == (qt // 2 + 1) * self.half - 1 + lag + qt % 2 * self.later:
                return qt


def freed(jobs, n):
    return (sum(e == "A" for _, _, e in jobs[:n]), sum(e == "D" for _, _, e in jobs[:n]))


ATT = [
    Stage("L0 self", causal=True, length=True),
    Stage("L0 cross", length=True, kv="mctx"),
    Stage("L1 self", mask=0, rms=True, wo=True, ln=False),
    Stage("L1 cross", mask=1, kv="ctx", rms=True, wo=True, ln=False),
    Stage("L2 self", mask=2, wo=True, bias=True),
    Stage("L2 cross", mask=1, kv="ctx", wo=True, bias=True),
    Stage("L3", dk=32, causal=True, kv="ctx", bias=True, eps=1e-6),
]


class Feed:

    def __init__(self, hb, experts=1, masked=False):
        self.hb, self.experts, self.masked = hb, experts, masked
        self.width = hb * P * 2 * KB
        self.chunks = self.width // S
        self.blocks = QT * hb
        self.ahead = 2


FEED = {"f0": Feed(D // P, masked=True), "moe": Feed(HB, E + 1), "f2": Feed(HB)}
ORDER = ["a0", "a1", "f0", "a2", "a3", "moe", "a4", "a5", "f2", "a6"]
BLOCKS = [["a0", "a1"], ["f0"], ["a2", "a3"], ["moe"], ["a4", "a5"], ["f2"], ["a6"]]
PER_TURN = 2
TURNS = E // PER_TURN
assert TURNS == B
PARTS = ((0, 0), (1, 0), (0, 1))
FEW = 5


class Signal:

    def __init__(self, sem, per, unit=1, after=None):
        self.sem, self.per, self.unit, self.base = sem, per, unit, {}
        total = self.start = 1 if unit == 1 else 0
        for st in ORDER:
            self.base[st] = total
            total += (per.get(st, 0) * B + (after or {}).get(st, 0)) * unit
        self.total = total

    def at(self, st, b, k):
        b, off = b if isinstance(b, tuple) else (b, 0)
        per = self.per.get(st, 0) * self.unit
        return b * per + (self.base[st] + off * per + k * self.unit)


def times(b, n, more=0):
    b, off = b if isinstance(b, tuple) else (b, 0)
    return b * n + (off * n + more)


def transition(prev, new):
    steps, jobs, out, total = [], [], [], 0
    if prev:
        a = ATT[int(prev[0][1:])]
        steps = [("step", *prev, k) for k in range(a.pairs, a.pairs + a.after)]
        total = len(steps)
    if new:
        a = ATT[int(new[0][1:])]
        out = [("mask", *new, 0)]
        jobs = [("job", *new, j) for j in range(len(a.jobs))]
    while steps or jobs:
        few = 2 if total - len(steps) < FEW else 3
        out += steps[:1] + jobs[:few]
        steps, jobs = steps[1:], jobs[few:]
    return out + ([("length", *new, 0)] if new and a.length else [])


def attention_items(eng, stages, st):
    n, a = stages.index(st), ATT[int(st[1:])]

    def steps(b, following):
        for k in range(a.pairs):
            if k == a.pairs // 4 and following:
                yield ("tokens", *following, 0)
            if k == a.pairs // 2 and following:
                yield ("norms", *following, 0)
            yield ("step", st, b, k)
            for t in (2 * k, 2 * k + 1) if k < 2 else ():
                yield ("value", st, b, t)

    if n == 0:
        yield ("tokens", st, 0, 0)
        yield ("norms", st, 0, 0)
    yield from transition((stages[n - 1], B - 1) if n else None, (st, 0))
    yield ("settled", st, 0, 0)
    with eng.Fori(0, B - 1) as b:
        yield from steps(b, (st, (b, 1)))
        yield from transition((st, b), (st, (b, 1)))
    if n + 1 < len(stages):
        yield from steps(B - 1, (stages[n + 1], 0))
    else:
        yield from steps(B - 1, None)
        yield from transition((st, B - 1), None)


def build(nc, io, ctx):
    def sb(name, shape, dt):
        return ctx.enter_context(nc.sbuf_tensor(name, shape, dt))

    def sem(name):
        return ctx.enter_context(nc.semaphore(name))

    def signal(name, unit=1, after=None, **per):
        out = {}
        for key, n in per.items():
            for st in ORDER:
                if st == key or (key == "att" and st[0] == "a") or (key == "feed" and st[0] == "f"):
                    out[st] = n(st) if callable(n) else n
        return Signal(sem(name), out, unit, after)

    att = {f"a{n}": s for n, s in enumerate(ATT)}

    X = sb("X", [P, NT, D], F32)
    wt = sb("wt", [P, 2, KB, WEND], F32)
    wcol = sb("wcol", [P, 2, 6], F32)
    wrow = sb("wrow", [P, 2, 4, D], F32)
    raw = sb("raw", [P, 2 * KB * HID], F32)
    wcolf = sb("wcolf", [P, HB], F32)
    wrowf = sb("wrowf", [P, 3, D], F32)
    y = sb("y", [P, 2, D], F32)
    xh = sb("xh", [P, 2, D], F32)
    junk = sb("junk", [P, D], F32)
    identf = sb("identf", [P, P], F32)
    identb = sb("identb", [P, P], BF16)
    causal = sb("causal", [P, P], BF16)
    gw = sb("gw", [P, KB, E], F32)
    norm3 = sb("norm3", [P, KB], F32)
    iota8 = sb("iota8", [P, E], F32)
    select = sb("select", [P, 2, SELW], F32R)
    epsilon = sb("epsilon", [P, 2], F32)
    eps_of = {eps: epsilon[:, n:n + 1] for n, eps in enumerate((1e-5, 1e-6))}
    minus_half = sb("minus_half", [P, 4], F32)
    keep = sb("keep", [P, 2, NT], F32)
    bn = sb("bn", [P, 2, 6], F32)
    mv = sb("mv", [P, 2, 2], F32)
    ve = sb("ve", [P, 2, 1], F32)
    rstd = sb("rstd", [P, 2, 1], F32)
    ss = sb("ss", [P, QT], F32)
    ms = sb("ms", [P, QT], F32)
    rs4 = sb("rs4", [P, QT], F32)

    SB = [ctx.enter_context(nc.psum_tensor(f"scores{n}", [P, 2, S], F32)) for n in range(2)]
    TB = [ctx.enter_context(nc.psum_tensor(f"turned{n}", [P, S], F32)) for n in range(2)]
    OB = ctx.enter_context(nc.psum_tensor("outputs", [P, S], F32))
    MB = ctx.enter_context(nc.psum_tensor("mixed", [P, S], F32))
    RING = [SB[n // 2][:, n % 2, :] for n in range(4)]
    OUTS = [TB[0], TB[1], OB, MB]

    def nA(st):
        return freed(att[st].jobs, 99)[0]

    def nD(st):
        return freed(att[st].jobs, 99)[1]

    def njob(st):
        return len(att[st].jobs)

    def npair(st):
        return att[st].pairs

    def with_wo(st):
        return QT if att[st].wo else 0

    def with_ln(st):
        return QT if att[st].ln else 0

    c_first = sem("c_first")
    c_const = sem("c_const")
    c_x0 = sem("c_x0")
    c_x = sem("c_x")
    c_selh = sem("c_selh")
    c_w = [sem("c_weights0"), sem("c_weights1")]
    c_ready = sem("c_ready")
    c_sel = sem("c_sel")
    c_select = sem("c_select")
    c_ones = sem("c_ones")
    c_keep = signal("c_keep", a0=1, a1=1)
    c_kv = signal("c_kv", 16, a1=1, a3=1, a5=1, a6=1)
    c_mask = signal("c_mask", 16, a2=1, a3=1, a4=1, a5=1)
    c_maskb = signal("c_maskb", a2=1, a3=1, a4=1, a5=1)
    c_xs = signal("c_xs", att=1, after={"moe": QT})
    c_cs = signal("c_cs", a1=1)
    c_ss = signal("c_ss", a2=1, a3=1, after={"moe": QT})
    c_job = signal("c_job", att=njob)
    c_hi = signal("c_hi", att=2 * KB)
    c_A = signal("c_A", att=nA)
    c_D = signal("c_D", att=nD)
    c_V = signal("c_V", att=QT)
    c_VA = signal("c_VA", att=lambda st: att[st].values.count("A"))
    c_VD = signal("c_VD", att=lambda st: att[st].values.count("D"))
    c_qz = signal("c_qz", a0=1, a1=1)
    c_e0 = signal("c_e0", a0=1, a1=1)
    c_sq = signal("c_sq", a2=1, a3=1, after={"moe": QT})
    c_masking = sem("c_masking")
    c_seen = sem("c_seen")
    c_pen = signal("c_pen", a0=1, a1=1)
    c_scores = signal("c_scores", att=lambda st: 2 * npair(st))
    c_max = signal("c_max", att=lambda st: 2 * npair(st))
    c_exp = signal("c_exp", att=lambda st: 2 * npair(st))
    c_turn = signal("c_turn", att=lambda st: 2 * npair(st))
    c_tD = signal("c_tD", att=npair)
    c_tA = signal("c_tA", att=npair)
    c_pv = signal("c_pv", att=2 * G)
    c_oT = signal("c_oT", att=2 * G)
    c_on = signal("c_on", att=QT)
    c_o = signal("c_o", att=QT)
    c_ot = signal("c_ot", att=with_wo)
    c_otn = signal("c_otn", att=with_wo)
    c_y = signal("c_y", att=with_wo)
    c_yD = signal("c_yD", att=with_wo)
    c_var = signal("c_var", att=with_ln, feed=QT)
    c_rstd = signal("c_rstd", att=with_ln, feed=QT)
    c_xh = signal("c_xh", att=with_ln, feed=QT)
    c_xout = signal("c_xout", att=QT, feed=QT)
    def count(f):
        return {"moe": {"moe": f(FEED["moe"]) * PER_TURN},
                "rest": {"f0": f(FEED["f0"]), "f2": f(FEED["f2"]), "moe": f(FEED["moe"])}}

    def counted(name, f):
        n = count(f)
        return Signal(sem(name), n["moe"], 1, n["rest"])

    token_blocks = {st: QT * KB for st in FEED}
    c_raw = sem("c_raw")
    c_rawb = sem("c_rawb")
    c_turned = Signal(sem("c_turned"), {}, 1, token_blocks)
    c_thigh = Signal(sem("c_thigh"), {}, 1, token_blocks)
    c_tlow = Signal(sem("c_tlow"), {}, 1, token_blocks)
    c_gwsplit = sem("c_gwsplit")
    c_logits = sem("c_logits")
    c_gex = sem("c_gex")
    c_gate = sem("c_gate")
    c_whigh = counted("c_whigh", lambda f: f.chunks)
    c_wlow = counted("c_wlow", lambda f: f.chunks)
    c_hid = counted("c_hid", lambda f: f.blocks)
    c_high = counted("c_high", lambda f: f.blocks)
    c_low = counted("c_low", lambda f: f.blocks)
    c_h = counted("c_h", lambda f: NT)
    c_hD = counted("c_hD", lambda f: NT)
    c_out = sem("c_out")

    def tile(b, qt):
        return X[:, bass.ds(times(b, QT, qt), 1), :].rearrange("p o d -> p (o d)")

    def wait_x(eng, st, b):
        before = ORDER[ORDER.index(st) - 1]
        if st == "a0":
            eng.wait_ge(*((c_x0, 16) if type(b) is int and b == 0 else (c_x, 16)))
        elif before == "moe":
            eng.wait_ge(c_hD.sem, c_hD.at(st, 0, 0))
        else:
            eng.wait_ge(c_xout.sem, c_xout.at(before, b, QT))

    def wait_weights(eng, n):
        eng.wait_ge(c_w[n % 2], 48 * (n // 2 + 1))

    def deviation(pool, st, b, qt, eps):
        r = qt % 2
        pool.wait_ge(c_var.sem, c_var.at(st, b, qt + 1))
        pool.tensor_tensor(ve[:, r, :], mv[:, r, 1:2], eps_of[eps], ALU.add)
        pool.drain()
        pool.tensor_tensor(rstd[:, r, :], ve[:, r, :], minus_half[:, 0:1], ALU.pow).then_inc(c_rstd.sem, 1)

    def gain(pool, st, b, qt, gamma, beta):
        pool.wait_ge(c_xh.sem, c_xh.at(st, b, qt + 1))
        pool.tensor_tensor(xh[:, qt % 2, :], xh[:, qt % 2, :], gamma, ALU.mult)
        pool.drain()
        pool.tensor_tensor(tile(b, qt), xh[:, qt % 2, :], beta, ALU.add).then_inc(c_xout.sem, 1)

    def moments(dve, st, b, qt):
        r = qt % 2
        dve.drain()
        dve.bn_stats(bn[:, r, :], y[:, r, :])
        dve.drain()
        dve.bn_aggr(mv[:, r, :], bn[:, r, :]).then_inc(c_var.sem, 1)

    def centre(dve, st, b, qt):
        r = qt % 2
        dve.wait_ge(c_rstd.sem, c_rstd.at(st, b, qt + 1))
        dve.wait_ge(c_xout.sem, c_xout.at(st, b, max(qt - 1, 0)))
        dve.tensor_scalar(xh[:, r, :], y[:, r, :], mv[:, r, 0:1], rstd[:, r, :], ALU.subtract,
                          ALU.mult).then_inc(c_xh.sem, 1)

    def load_expert(sp, st, e):
        f = FEED[st]
        if f.experts == 1:
            sp.dma_start(wcolf[:, 0:f.hb], io[f"{st}col"]).then_inc(c_rawb, 16)
            sp.dma_start(wrowf[:, :, :], io[f"{st}row"]).then_inc(c_rawb, 16)
        src = io[f"{st}w"] if f.experts == 1 else io[f"{st}w"][bass.ds(e, 1), :, :].rearrange("o p n -> (o p) n")
        sp.dma_start(raw[:, 0:f.width], src).then_inc(c_raw, 16)

    def attention_block(mem, stages):
        def sb(name, shape, dt):
            return mem.enter_context(nc.sbuf_tensor(f"{name}_{stages[0]}", shape, dt))

        arena = sb("arena", [P, 4, QT * D], F32)
        xs = arena[:, 0, :].rearrange("p (q d) -> p q d", q=QT)
        cn = arena[:, 1, :].rearrange("p (q d) -> p q d", q=QT)
        cs = arena[:, 2, :].rearrange("p (q d) -> p q d", q=QT)
        kvT = arena[:, 3, :].rearrange("p (k n) -> p k n", k=KB)
        xT = sb("xT", [P, KB, S], F32)
        Q = sb("Q", [P, GS, S], F32R)
        K = sb("K", [P, GS, S], F32R)
        parts = sb("parts", [P, KB, 2, S], F32R)
        V = sb("V", [P, QT, SLOTS], F32)
        prob = sb("prob", [P, 3, 2, S], F32)
        probT = sb("probT", [P, 2, 4, QT, 2 * P], F32)
        selectf = (probT[:, 0, :, :, :].rearrange("p s k n -> p (s k n)")[:, 0:2 * SELW]
                   .rearrange("p (a n) -> p a n", a=2))
        oT = sb("oT", [P, G, 2 * P], F32)
        o = sb("o", [P, D], F32)
        oTn = sb("oTn", [P, KB, P], F32)
        maski = sb("maski", [P, QT, S], I32)
        maskb = sb("maskb", [P, QT, S], BF16)
        iota = maski[0:16, 0, :].bitcast(F32)
        selq = maski[:, 1, 0:GS * 32].bitcast(F32).rearrange("p (g n) -> p g n", g=GS)
        selh = sb("selh", [P, 16, P], BF16)
        qz = parts[:, 0, 0, 0:GS * 32].rearrange("p (g n) -> p g n", g=GS)
        nz = y[0:16, :, :].rearrange("p a n -> p (a n)")
        lens = sb("lens", [16, 4], F32)
        pen = sb("pen", [P, S], BF16)
        negm = sb("negm", [P, 4, 2], F32)
        rinv = sb("rinv", [P, 16, 1], F32)
        amax = sb("amax", [P, 2, QT], F32)
        block = mem.enter_context(nc.Block())

        def value_bank(t):
            return (OB, MB)[t % 2][:, 0:D]

        first, last = stages[0] == ORDER[0], stages[-1] == ORDER[-1]
        ones_at = {st: sum(s[0][0] == "a" for s in BLOCKS[:BLOCKS.index(stages) + 1]) for st in stages}


        @block.sync
        def _(sp):
            def weights(n):
                if n >= 2:
                    after = f"a{n - 1}"
                    sp.wait_ge(c_xout.sem, c_xout.at(after, 0, 0))
                    sp.wait_ge(c_pv.sem, c_pv.at(after, 0, 0))
                k = n % 2
                sp.dma_start(wt[:, k, :, :], io[f"w{n}"]).then_inc(c_w[k], 16)
                sp.dma_start(wcol[:, k, :], io[f"col{n}"]).then_inc(c_w[k], 16)
                sp.dma_start(wrow[:, k, :, :], io[f"row{n}"]).then_inc(c_w[k], 16)

            def batch_inputs(st, b):
                a = att[st]
                if a.kv == "ctx":
                    sp.wait_ge(c_V.sem, c_V.at(st, b, 0))
                    sp.dma_start(kvT, io["ctxT"][bass.ds(b, 1), :, :, :]
                                 .rearrange("o p k n -> (o p) k n")).then_inc(c_kv.sem, 16)
                if a.kv == "mctx":
                    sp.wait_ge(c_cs.sem, c_cs.at(st, b, 0))
                    sp.dma_start(cn, io["ctx"][bass.ds(b, 1), :, :]
                                 .rearrange("o (q p) d -> p (o q) d", p=P)).then_inc(c_kv.sem, 16)
                if a.mask is not None:
                    sp.wait_ge(c_maskb.sem, c_maskb.at(st, b, 0))
                    sp.dma_start(maski[:, :, :], io[f"mask{a.mask}"][bass.ds(b, 1), :, :]
                                 .rearrange("o (q p) n -> p (o q) n", p=P)).then_inc(c_mask.sem, 16)

            if first:
                tokens = io["x"].rearrange("b (q p) d -> p (b q) d", p=P)
                sp.dma_start(X[:, 0:QT, :], tokens[:, 0:QT, :]).then_inc(c_x0, 16)
                for dst, name in ((identf, "identf"), (selectf, "select16")):
                    sp.dma_start(dst[(slice(None),) * len(dst.shape)], io[name]).then_inc(c_first, 16)
                weights(0)
                sp.dma_start(X[:, QT:NT, :], tokens[:, QT:NT, :]).then_inc(c_x, 16)
                for dst, name in ((identb, "identb"), (causal, "causal"), (selq, "selq"), (iota, "iota"), (gw, "gw"),
                                  (iota8, "iota8"), (norm3, "norm3")):
                    sp.dma_start(dst[(slice(None),) * len(dst.shape)], io[name]).then_inc(c_const, 16)
                weights(1)
            if stages == ["a6"]:
                sp.dma_start(selectf, io["select32"]).then_inc(c_sel, 16)
            for st in stages:
                if st in att:
                    a, n = att[st], int(st[1:])
                    batch_inputs(st, 0)
                    if n >= 1 and n + 1 < len(ATT):
                        weights(n + 1)
                    if a.kv != "self" or a.mask is not None:
                        with sp.Fori(1, B) as b:
                            batch_inputs(st, b)
            if last:
                sp.wait_ge(c_xout.sem, c_xout.total)
                sp.dma_start(io["out"].rearrange("b (q p) d -> p (b q) d", p=P), X[:, :, :]).then_inc(c_out, 16)
                sp.wait_ge(c_out, 16)
            else:
                ahead = ORDER[ORDER.index(stages[-1]) + 1]
                load_expert(sp, ahead, 0)

        @block.gpsimd
        def _(pool):
            def stage_tokens(st, b):
                wait_x(pool, st, b)
                pool.wait_ge(c_job.sem, c_job.at(st, b, 0))
                tiles = X[:, bass.ds(times(b, QT), QT), :]
                if not att[st].rms:
                    pool.tensor_copy(xs, tiles).then_inc(c_xs.sem, 1)
                    return
                pool.tensor_tensor(xs, tiles, tiles, ALU.mult).then_inc(c_sq.sem, 1)

            def norms(st, b):
                tiles = X[:, bass.ds(times(b, QT), QT), :]
                pool.wait_ge(c_ss.sem, c_ss.at(st, b, 1))
                pool.tensor_tensor(rs4[:, :], ms[:, :], minus_half[:, :], ALU.pow)
                pool.drain()
                pool.tensor_tensor(xs, tiles, rs4[:, :].unsqueeze(2).to_broadcast([P, QT, D]), ALU.mult)\
                    .then_inc(c_xs.sem, 1)

            def weights(n):
                a, k = ATT[n], n % 2
                wait_weights(pool, n)
                wq = wt[:, k, :, WQ:WK]
                pool.tensor_scalar(wq, wq, -a.dk ** -0.5, None, ALU.mult)
                pool.tensor_scalar(wcol[:, k, 0:KB], wcol[:, k, 0:KB], -a.dk ** -0.5, None, ALU.mult)
                pool.drain()
                pool.sem_inc(c_ready, 1)

            def attention(item, st, b, n):
                a = att[st]
                k = int(st[1:]) % 2
                if item == "tokens":
                    stage_tokens(st, b)
                    if st == "a0" and type(b) is int:
                        weights(0)
                    if a.kv == "mctx":
                        pool.wait_ge(c_keep.sem, c_keep.at(st, b, 1))
                        pool.wait_ge(c_kv.sem, c_kv.at(st, b, 1))
                        pool.wait_ge(c_job.sem, c_job.at(st, b, 0))
                        pool.tensor_tensor(cs, cn, keep[:, 1, bass.ds(times(b, QT), QT)].unsqueeze(2)
                                           .to_broadcast([P, QT, D]), ALU.mult).then_inc(c_cs.sem, 1)
                if item == "norms" and a.rms:
                    norms(st, b)
                if item == "settled" and int(st[1:]) + 1 < len(ATT):
                    weights(int(st[1:]) + 1)
                if item == "mask" and a.mask is not None:
                    pool.wait_ge(c_mask.sem, c_mask.at(st, b, 1))
                    pool.wait_ge(c_max.sem, c_max.at(st, b, 0))
                    pool.sem_inc(c_masking, 1)
                    pool.tensor_scalar(maskb[:, :, :], maski[:, :, :], 0.0, BIG, ALU.is_equal, ALU.mult)\
                        .then_inc(c_maskb.sem, 1)
                if item == "step" and a.ln:
                    qt = a.finishing(n, 9 if a.wo else 7)
                    if qt is not None:
                        deviation(pool, st, b, qt, a.eps)
                        gain(pool, st, b, qt, wrow[:, k, 2, :], wrow[:, k, 3, :])

            if first:
                for s in (c_maskb, c_sq, c_xs, c_cs, c_rstd, c_xout):
                    pool.sem_inc(s.sem, s.start)
                for eps, column in eps_of.items():
                    pool.memset(column, eps)
                pool.memset(minus_half[:, :], -0.5)
                pool.drain()
            for st in stages:
                for entry in attention_items(pool, stages, st):
                    attention(*entry)

        @block.tensor
        def _(pe):
            def turn_tokens(out, src, kb):
                for qt in range(QT):
                    last = pe.transpose(out[:, qt * P:(qt + 1) * P], src[:, qt, kb * P:(kb + 1) * P],
                                        identf[:, :])
                return last

            def bank_free(st, b, jobs, j):
                if j >= 4:
                    fa, fd = freed(jobs, j - 3)
                    if jobs[j - 4][2] == "A":
                        pe.wait_ge(c_A.sem, c_A.at(st, b, fa))
                    else:
                        pe.wait_ge(c_D.sem, c_D.at(st, b, fd))

            def all_free(st, b, jobs, n):
                fa, fd = freed(jobs, n)
                pe.wait_ge(c_A.sem, c_A.at(st, b, fa))
                pe.wait_ge(c_D.sem, c_D.at(st, b, fd))

            def scores(st, a, b, i):
                qt, h0 = a.pair(i)
                w = a.width(qt)
                if i == 0:
                    all_free(st, b, a.jobs, len(a.jobs))
                    if a.length:
                        pe.wait_ge(c_pen.sem, c_pen.at(st, b, 1))
                for e in range(2):
                    s, g = (h0 + e) % a.per_stack, (h0 + e) // a.per_stack
                    rows = slice(s * a.stack, (s + 1) * a.stack)
                    out = SB[i % 2][:, e, 0:w]
                    if i >= 2:
                        pe.wait_ge(c_exp.sem, c_exp.at(st, b, 2 * i - 3 + e))
                    last = pe.matmul(out, Q[rows, g, qt * P:(qt + 1) * P], K[rows, g, 0:w],
                                     start=True, stop=not (a.causal or a.length))
                    if a.length:
                        last = pe.matmul(out, selh[:, h0 + e, :], pen[:, 0:w], start=False, stop=not a.causal)
                    if a.causal:
                        last = pe.matmul(out[:, w - P:w], identb[:, :], causal[:, :], start=False, stop=True)
                    last.then_inc(c_scores.sem, 1)

            def turns(st, a, b, i):
                qt, _ = a.pair(i)
                for e in range(2):
                    pe.wait_ge(c_exp.sem, c_exp.at(st, b, 2 * i + 1 + e))
                    free = c_tA if e else c_tD
                    pe.wait_ge(free.sem, free.at(st, b, i))
                    for kb in range(a.width(qt) // P):
                        last = pe.transpose(TB[e][:, kb * P:(kb + 1) * P],
                                            prob[:, i % 3, e, kb * P:(kb + 1) * P], identf[:, :])
                    last.then_inc(c_turn.sem, 1)

            def values(st, a, b, i, part):
                u = i // a.unit
                half, g = u // G, u % G
                if part == 0:
                    pe.wait_ge(c_tD.sem, c_tD.at(st, b, i + 1))
                    pe.wait_ge(c_tA.sem, c_tA.at(st, b, i + 1))
                    if u == 0:
                        pe.wait_ge(c_VA.sem, c_VA.at(st, b, a.values.count("A")))
                        pe.wait_ge(c_VD.sem, c_VD.at(st, b, a.values.count("D")))
                    pe.wait_ge(c_oT.sem, c_oT.at(st, b, u))
                if a.causal:
                    tokens, blocks = slice(part * P, (part + 1) * P), a.width(2 * half + part) // P
                    todo = range(blocks)
                else:
                    tokens, blocks = slice(0, 2 * P), QT
                    todo = range(part * 2, part * 2 + 2)
                for kb in todo:
                    for s in range(a.per_group):
                        rows = slice(s * a.slot, (s + 1) * a.slot)
                        h = g * a.per_group + s
                        last = pe.matmul(OB[rows, tokens], V[:, kb, h * a.slot:(h + 1) * a.slot],
                                         probT[:, u % 2, s, kb, tokens], start=(kb == 0), stop=(kb == blocks - 1))
                if part == 1:
                    last.then_inc(c_pv.sem, 1)

            def attention(item, st, b, n):
                a = att[st]
                k = int(st[1:]) % 2
                if item == "job":
                    kind, idx, _ = a.jobs[n]
                    bank = RING[n % 4]
                    if n == 0:
                        if type(b) is int and b == 0:
                            wait_weights(pe, int(st[1:]))
                            pe.wait_ge(c_ready, int(st[1:]) + 1)
                            pe.wait_ge(c_select, 1 + (st == "a6"))
                        all_free(st, b, a.jobs, 0)
                    if n in (0, 2) and not (st == "a0" and type(b) is int):
                        pe.wait_ge(c_exp.sem, c_exp.at(st, b, 0 if n else -2))
                    bank_free(st, b, a.jobs, n)
                    if kind == "x":
                        if idx == 0:
                            pe.wait_ge(c_xs.sem, c_xs.at(st, b, 1))
                        last = turn_tokens(bank, xs, idx)
                    elif kind == "c":
                        if idx == 0:
                            pe.wait_ge(c_cs.sem, c_cs.at(st, b, 1))
                        last = turn_tokens(bank, cs, idx)
                    elif kind in "qk":
                        if (kind, idx) == ("q", 0):
                            all_free(st, b, a.jobs, 2)
                        if (kind, idx) == ("k", 0):
                            if a.kv == "ctx":
                                pe.wait_ge(c_kv.sem, c_kv.at(st, b, 1))
                            if a.kv == "mctx":
                                all_free(st, b, a.jobs, 4)
                        src = xT if kind == "q" or a.kv == "self" else kvT
                        c0 = (WQ if kind == "q" else WK) + idx * P
                        for kb in range(KB):
                            last = pe.matmul(bank, wt[:, k, kb, c0:c0 + P], src[:, kb, :],
                                             start=(kb == 0), stop=(kb == KB - 1))
                    elif kind in "QK":
                        block, c0 = idx // G, idx % G * P
                        shift = a.dk if kind == "Q" else 2 * a.dk
                        if c0 == 0:
                            all_free(st, b, a.jobs, a.jobs.index((kind.lower(), block, "D")) + 1)
                        for part in range(2):
                            c = c0 + 64 - part * shift
                            last = pe.matmul(bank, select[:, "QK".index(kind), c:c + P], parts[:, block, part, :],
                                             start=(part == 0), stop=(part == 1))
                    last.then_inc(c_job.sem, 1)
                if item == "value":
                    if n == 0:
                        pe.wait_ge(c_oT.sem, c_oT.at(st, b, 0))
                    if n == 1:
                        pe.wait_ge(c_o.sem, c_o.at(st, b, 0))
                        pe.wait_ge(c_yD.sem, c_yD.at(st, b, 0))
                    if n >= 2:
                        free = c_VA if a.values[n - 2] == "A" else c_VD
                        pe.wait_ge(free.sem, free.at(st, b, a.values[:n - 1].count(a.values[n - 2])))
                    src = xT if a.kv == "self" else kvT
                    for kb in range(KB):
                        last = pe.matmul(value_bank(n), src[:, kb, n * P:(n + 1) * P], wt[:, k, kb, WV:WO],
                                         start=(kb == 0), stop=(kb == KB - 1))
                    last.then_inc(c_V.sem, 1)
                if item == "length":
                    if st == "a0" and type(b) is int:
                        pe.wait_ge(c_const, 112)
                        pe.wait_ge(c_selh, 1)
                    all_free(st, b, a.jobs, len(a.jobs))
                    pe.wait_ge(c_qz.sem, c_qz.at(st, b, 1))
                    pe.wait_ge(c_o.sem, c_o.at(st, b, 0))
                    for g in range(GS):
                        last = pe.matmul(MB[0:32, :], qz[:, g, :], K[:, g, :], start=(g == 0), stop=(g == GS - 1))
                    last.then_inc(c_e0.sem, 1)
                if item == "step":
                    if n < a.pairs:
                        scores(st, a, b, n)
                    if 2 <= n < a.pairs + 2:
                        turns(st, a, b, n - 2)
                    qt = a.finishing(n, 6)
                    if qt is not None:
                        pe.wait_ge(c_oT.sem, c_oT.at(st, b, (qt // 2 + 1) * G))
                        pe.wait_ge(c_o.sem, c_o.at(st, b, qt))
                        if a.wo:
                            pe.wait_ge(c_yD.sem, c_yD.at(st, b, qt))
                        for g in range(G):
                            last = pe.transpose(MB[:, g * P:(g + 1) * P], oT[:, g, qt % 2 * P:(qt % 2 + 1) * P],
                                                identf[:, :])
                        last.then_inc(c_on.sem, 1)
                    for part in range(2):
                        i = n - 3 - part
                        if 0 <= i < a.pairs and (i + 1) % a.unit == 0:
                            values(st, a, b, i, part)
                    qt = a.finishing(n, 7) if a.wo else None
                    if qt is not None:
                        pe.wait_ge(c_o.sem, c_o.at(st, b, qt + 1))
                        for kb in range(KB):
                            last = pe.transpose(MB[:, kb * P:(kb + 1) * P], o[:, kb * P:(kb + 1) * P],
                                                identf[:, :])
                        last.then_inc(c_ot.sem, 1)
                    qt = a.finishing(n, 8) if a.wo else None
                    if qt is not None:
                        pe.wait_ge(c_otn.sem, c_otn.at(st, b, qt + 1))
                        for kb in range(KB):
                            last = pe.matmul(MB[:, 0:D], oTn[:, kb, :], wt[:, k, kb, WO:WEND],
                                             start=(kb == 0), stop=(kb == KB - 1))
                        last.then_inc(c_y.sem, 1)

            if first:
                for s in (c_job, c_V, c_e0, c_scores, c_turn, c_pv, c_on, c_ot, c_y, c_turned, c_hid, c_h):
                    pe.sem_inc(s.sem, s.start)
                pe.wait_ge(c_first, 32)
            for st in stages:
                for entry in attention_items(pe, stages, st):
                    attention(*entry)

        @block.scalar
        def _(act):
            def attention(item, st, b, n):
                a = att[st]
                k = int(st[1:]) % 2
                if item == "job":
                    kind, idx, eng = a.jobs[n]
                    if eng == "D" and kind not in "qk":
                        return
                    if n == 0 and type(b) is int:
                        wait_weights(act, int(st[1:]))
                        act.wait_ge(c_ready, int(st[1:]) + 1)
                    bank = RING[n % 4]
                    act.wait_ge(c_job.sem, c_job.at(st, b, n + 1))
                    if kind in "qk":
                        col = idx + (KB if kind == "k" else 0)
                        act.activation(parts[:, idx, 0, :], bank, ACT.Identity,
                                       bias=wcol[:, k, col:col + 1], scale=1.0).then_inc(c_hi.sem, 1)
                    elif kind in "QK":
                        act.activation((Q if kind == "Q" else K)[:, idx, :], bank, ACT.Copy)\
                            .then_inc(c_A.sem, 1)
                    elif kind == "x":
                        if a.rms:
                            act.activation(xT[:, idx, :], bank, ACT.Identity, bias=0.0,
                                           scale=wcol[:, k, 4 + idx:5 + idx]).then_inc(c_A.sem, 1)
                        else:
                            act.activation(xT[:, idx, :], bank, ACT.Copy).then_inc(c_A.sem, 1)
                    elif kind == "c":
                        act.activation(kvT[:, idx, :], bank, ACT.Copy).then_inc(c_A.sem, 1)
                if item == "value" and a.values[n] == "A":
                    if n == 0:
                        act.wait_ge(c_ones, ones_at[st])
                    act.wait_ge(c_V.sem, c_V.at(st, b, n + 1))
                    act.activation(V[:, n, :].rearrange("p (h s) -> p h s", s=a.slot)[:, :, 0:a.dk],
                                   value_bank(n).rearrange("p (h s) -> p h s", s=a.dk), ACT.Copy)\
                        .then_inc(c_VA.sem, 1)
                if item == "step":
                    i = n - 5
                    if 0 <= i < a.pairs and (i + 1) % a.unit == 0:
                        u = i // a.unit
                        act.wait_ge(c_pv.sem, c_pv.at(st, b, u + 1))
                        act.wait_ge(c_on.sem, c_on.at(st, b, u // G * 2))
                        act.activation(oT[:, u % G, :], OB[:, 0:2 * P], ACT.Copy).then_inc(c_oT.sem, 1)
                    def exponentials(e):
                        t, _ = a.pair(n)
                        w = a.width(t)
                        if n >= 3:
                            act.wait_ge(c_turn.sem, c_turn.at(st, b, 2 * (n - 3) + 1 + e))
                        act.wait_ge(c_max.sem, c_max.at(st, b, 2 * n + 1 + e))
                        act.activation(prob[:, n % 3, e, 0:w], SB[n % 2][:, e, 0:w], ACT.Exp,
                                       bias=negm[:, n % 4, e:e + 1], scale=-1.0).then_inc(c_exp.sem, 1)

                    if n < a.pairs:
                        exponentials(0)
                    i = n - 2
                    if 0 <= i < a.pairs:
                        blocks, u = a.width(a.pair(i)[0]) // P, i // a.unit
                        buffer, slot, q = a.place(i, 1)
                        act.wait_ge(c_turn.sem, c_turn.at(st, b, 2 * i + 2))
                        if u >= 2:
                            act.wait_ge(c_pv.sem, c_pv.at(st, b, u - 1))
                        act.activation(probT[:, buffer, slot, 0:blocks, q * P:(q + 1) * P],
                                       TB[1][:, 0:blocks * P].rearrange("p (k n) -> p k n", k=blocks), ACT.Copy)\
                            .then_inc(c_tA.sem, 1)
                    if n < a.pairs:
                        exponentials(1)
                    qt = a.finishing(n, 7) if a.wo else None
                    if qt is not None:
                        act.wait_ge(c_ot.sem, c_ot.at(st, b, qt + 1))
                        act.wait_ge(c_y.sem, c_y.at(st, b, qt))
                        act.activation(oTn[:, :, :].rearrange("p k n -> p (k n)"), MB[:, 0:D], ACT.Copy)\
                            .then_inc(c_otn.sem, 1)

            if first:
                for s in (c_hi, c_A, c_VA, c_exp, c_tA, c_oT, c_otn, c_thigh, c_whigh, c_high):
                    act.sem_inc(s.sem, s.start)
                act.wait_ge(c_first, 32)
            if stages == ["a6"]:
                act.wait_ge(c_sel, 16)
            if first or last:
                act.activation(select[:, :, :], selectf, ACT.Copy).then_inc(c_select, 1)
            for st in stages:
                for entry in attention_items(act, stages, st):
                    attention(*entry)

        @block.vector
        def _(dve):
            def ones(a):
                dve.memset(V[:, :, :], 0.0)
                dve.drain()
                dve.memset(V[:, :, :].rearrange("p t (h s) -> p (t h) s", s=a.slot)[:, :, a.dk:a.dk + 1],
                            1.0).then_inc(c_ones, 1)

            def lengths(st, b):
                dve.drain()
                dve.tensor_tensor(qz[:, :, :], Q[:, :, 0:1].bitcast(F32).to_broadcast([P, GS, 32]),
                                  selq[:, :, :], ALU.mult).then_inc(c_qz.sem, 1)
                dve.wait_ge(c_e0.sem, c_e0.at(st, b, 1))
                dve.tensor_scalar(nz[:, :], MB[0:16, :], 0.0, None, ALU.not_equal)
                dve.drain()
                dve.tensor_reduce(lens[:, 0:1], nz[:, :], AX.X, ALU.add)
                dve.drain()
                dve.reciprocal(lens[:, 1:2], lens[:, 0:1])
                dve.tensor_scalar(nz[:, :], iota[:, :], lens[:, 0:1], BIG, ALU.is_ge, ALU.mult)
                dve.drain()
                dve.tensor_scalar(lens[:, 2:3], lens[:, 1:2], 0.0, None, ALU.mult)
                dve.drain()
                dve.tensor_scalar(pen[0:16, :], nz[:, :], lens[:, 2:3], None, ALU.add).then_inc(c_pen.sem, 1)

            def attention(item, st, b, n):
                a = att[st]
                k = int(st[1:]) % 2
                if item == "tokens":
                    if type(b) is int:
                        wait_weights(dve, int(st[1:]))
                        dve.wait_ge(c_ready, int(st[1:]) + 1)
                    if a.length:
                        wait_x(dve, st, b)
                        which = int(st[1:])
                        dve.tensor_reduce(amax[:, which, :], X[:, bass.ds(times(b, QT), QT), :], AX.X, ALU.max,
                                          apply_absolute_value=True)
                        dve.drain()
                        dve.tensor_scalar(keep[:, which, bass.ds(times(b, QT), QT)], amax[:, which, :], 0.0, None,
                                          ALU.is_gt).then_inc(c_keep.sem, 1)
                if item == "norms" and a.rms:
                    dve.wait_ge(c_sq.sem, c_sq.at(st, b, 1))
                    dve.tensor_reduce(ss[:, :], xs, AX.X, ALU.add)
                    dve.drain()
                    dve.tensor_scalar(ms[:, :], ss[:, :], 1.0 / D, 1e-5, ALU.mult, ALU.add).then_inc(c_ss.sem, 1)
                if item == "job":
                    kind, idx, eng = a.jobs[n]
                    if eng == "A":
                        return
                    bank = RING[n % 4]
                    if kind in "qk":
                        hi = sum(x[0] in "qk" for x in a.jobs[:n + 1])
                        dve.wait_ge(c_hi.sem, c_hi.at(st, b, hi))
                        col = idx + (KB if kind == "k" else 0)
                        dve.scalar_tensor_tensor(
                            out=parts[:, idx, 1, :], in0=bank, scalar=wcol[:, k, col:col + 1],
                            in1=parts[:, idx, 0, :].bitcast(F32), op0=ALU.add, op1=ALU.subtract)\
                            .then_inc(c_D.sem, 1)
                        return
                    dve.wait_ge(c_job.sem, c_job.at(st, b, n + 1))
                    if kind == "x" and a.rms:
                        dve.tensor_scalar(xT[:, idx, :], bank, wcol[:, k, 4 + idx:5 + idx], None,
                                          ALU.mult).then_inc(c_D.sem, 1)
                    elif kind == "x":
                        dve.tensor_copy(xT[:, idx, :], bank).then_inc(c_D.sem, 1)
                    elif kind in "QK":
                        dve.tensor_copy((Q if kind == "Q" else K)[:, idx, :], bank).then_inc(c_D.sem, 1)
                    elif kind == "c":
                        dve.tensor_copy(kvT[:, idx, :], bank).then_inc(c_D.sem, 1)
                if item == "value" and a.values[n] == "D":
                    dve.wait_ge(c_V.sem, c_V.at(st, b, n + 1))
                    dst = V[:, n, :].rearrange("p (h s) -> p h s", s=a.slot)[:, :, 0:a.dk]
                    src = value_bank(n).rearrange("p (h s) -> p h s", s=a.dk)
                    if a.bias:
                        dve.tensor_tensor(dst, src, wrow[:, k, 0, :].rearrange("p (h s) -> p h s", s=a.dk),
                                          ALU.add).then_inc(c_VD.sem, 1)
                    else:
                        dve.tensor_copy(dst, src).then_inc(c_VD.sem, 1)
                if item == "length":
                    if st == "a0" and type(b) is int:
                        dve.wait_ge(c_const, 112)
                        dve.tensor_copy(selh[:, :, :], identb[:, 0:16].unsqueeze(2).to_broadcast([P, 16, P]))\
                            .then_inc(c_selh, 1)
                    lengths(st, b)
                if item == "step":
                    def minimum(e):
                        t, _ = a.pair(n)
                        dve.wait_ge(c_scores.sem, c_scores.at(st, b, 2 * n + 1 + e))
                        if a.mask is not None:
                            dve.sem_inc(c_seen, 1)
                        sc, out = SB[n % 2][:, e, 0:a.width(t)], negm[:, n % 4, e:e + 1]
                        if a.mask is None:
                            least = dve.tensor_reduce(out, sc, AX.X, ALU.min)
                        else:
                            least = dve.tensor_tensor_reduce(sc, sc, maskb[:, t, :], 1.0, BIG * 2, ALU.add,
                                                             ALU.min, out)
                        least.then_inc(c_max.sem, 1)

                    if n < a.pairs:
                        if a.mask is not None and n == 0:
                            dve.wait_ge(c_maskb.sem, c_maskb.at(st, b, 1))
                        minimum(0)
                    i = n - 2
                    if 0 <= i < a.pairs:
                        blocks, u = a.width(a.pair(i)[0]) // P, i // a.unit
                        buffer, slot, q = a.place(i, 0)
                        dve.wait_ge(c_turn.sem, c_turn.at(st, b, 2 * i + 1))
                        if u >= 2:
                            dve.wait_ge(c_pv.sem, c_pv.at(st, b, u - 1))
                        dve.tensor_copy(probT[:, buffer, slot, 0:blocks, q * P:(q + 1) * P],
                                        TB[0][:, 0:blocks * P].rearrange("p (k n) -> p k n", k=blocks))\
                            .then_inc(c_tD.sem, 1)
                    if n < a.pairs:
                        minimum(1)
                    qt = a.finishing(n, 6)
                    if qt is not None:
                        view = MB[:, :].rearrange("p (h s) -> p h s", s=a.slot)
                        r = rinv[:, 0:a.heads, :]
                        dve.wait_ge(c_on.sem, c_on.at(st, b, qt + 1))
                        dve.reciprocal(r, view[:, :, a.dk:a.dk + 1])
                        dve.drain()
                        if a.length:
                            dve.tensor_scalar(r, r, keep[:, int(st[1:]), bass.ds(times(b, QT, qt), 1)], None,
                                              ALU.mult)
                            dve.drain()
                        dve.tensor_tensor(o[:, :].rearrange("p (h s) -> p h s", s=a.dk), view[:, :, 0:a.dk],
                                          r.to_broadcast([P, a.heads, a.dk]), ALU.mult).then_inc(c_o.sem, 1)
                        if not a.wo:
                            dve.drain()
                            dve.tensor_tensor(y[:, qt % 2, :], o[:, :], tile(b, qt), ALU.add)
                            moments(dve, st, b, qt)
                    qt = a.finishing(n, 8) if a.wo else None
                    if qt is not None:
                        dve.wait_ge(c_y.sem, c_y.at(st, b, qt + 1))
                        if not a.ln:
                            dve.tensor_tensor(y[:, qt % 2, :], MB[:, 0:D], tile(b, qt), ALU.add)\
                                .then_inc(c_yD.sem, 1)
                            dve.drain()
                            dve.tensor_copy(tile(b, qt), y[:, qt % 2, :]).then_inc(c_xout.sem, 1)
                        else:
                            dve.tensor_tensor(junk[:, :], MB[:, 0:D], wrow[:, k, 1, :], ALU.add)\
                                .then_inc(c_yD.sem, 1)
                            dve.drain()
                            dve.tensor_tensor(y[:, qt % 2, :], junk[:, :], tile(b, qt), ALU.add)
                            moments(dve, st, b, qt)
                    qt = a.finishing(n, 9 if a.wo else 7) if a.ln else None
                    if qt is not None:
                        centre(dve, st, b, qt)

            if first:
                for s in (c_keep, c_ss, c_D, c_VD, c_qz, c_pen, c_max, c_tD, c_o, c_yD, c_var, c_xh, c_tlow,
                          c_wlow, c_low, c_hD):
                    dve.sem_inc(s.sem, s.start)
                dve.memset(pen[:, :], 0.0)
            ones(att[stages[0]])
            for st in stages:
                for entry in attention_items(dve, stages, st):
                    attention(*entry)

    def feed_block(mem, stages):
        st = stages[0]
        f = FEED[st]
        moe = st == "moe"

        def sb(name, shape, dt):
            return mem.enter_context(nc.sbuf_tensor(f"{name}_{st}", shape, dt))

        tokens = sb("tokens", [P, 2, KB, B * S], F32R)
        weights = sb("weights", [P, 2, 2, 2 * KB * HID], F32R)
        whole = sb("whole", [P, 2, S], F32)
        hidden = sb("hidden", [P, 4, 2, S], F32R)
        xs = sb("xs", [P, 2, QT, D], F32)
        gwp = sb("gwp", [P, KB, 2, E], F32R)
        lg = sb("lg", [P, NT, E], F32)
        top = sb("top", [P, NT, E], F32)
        topi = sb("topi", [P, NT, E], U32)
        topf = sb("topf", [P, NT, 2], F32)
        gex = sb("gex", [P, 4, NT], F32)
        gpart = sb("gpart", [P, 2, NT, E], F32)
        gates = sb("gates", [P, E + 1, NT], F32)
        block = mem.enter_context(nc.Block())

        def w1(slot, part, kb, n):
            c = kb * f.hb * P + n * P
            return weights[:, slot, part, c:c + P]

        def w2(slot, part, n):
            c = KB * f.hb * P + n * D
            return weights[:, slot, part, c:c + D]

        def chunk(q):
            return slice(q * S, (q + 1) * S)

        SPLIT = {6 + 3 * q: q for q in range(f.chunks)} if moe else {}

        def landed(it, more):
            before = {"f0": 0, "moe": 1, "f2": 1 + FEED["moe"].experts}[st]
            return it * (16 * PER_TURN) + 16 * (before + more + 1)

        @block.sync
        def _(sp):
            if moe:
                with sp.Fori(0, TURNS) as it:
                    for n in range(PER_TURN):
                        sp.wait_ge(c_wlow.sem, c_wlow.at(st, it, (n + 1) * f.chunks))
                        load_expert(sp, st, it * PER_TURN + (n + 1))

        @block.gpsimd
        def _(pool):
            if moe:
                pool.memset(gates[:, E, :], 1.0)
                for b in range(B):
                    pool.wait_ge(c_ss.sem, c_ss.at(st, 0, b + 1))
                    pool.tensor_tensor(rs4[:, :], ms[:, :], minus_half[:, :], ALU.pow)
                    pool.drain()
                    pool.tensor_tensor(xs[:, b % 2, :, :], X[:, b * QT:(b + 1) * QT, :],
                                       rs4[:, :].unsqueeze(2).to_broadcast([P, QT, D]), ALU.mult)\
                        .then_inc(c_xs.sem, 1)
            else:
                pool.wait_ge(c_rawb, 32 if st == "f0" else 64)
                for n in range(NT + 1):
                    if n < NT:
                        deviation(pool, st, n // QT, n % QT, 1e-5)
                    if n >= 1:
                        gain(pool, st, (n - 1) // QT, (n - 1) % QT, wrowf[:, 1, :], wrowf[:, 2, :])

        @block.tensor
        def _(pe):
            def turn(it, base, experts):
                total = experts * f.blocks
                for m in range(total + f.ahead):
                    if m < total:
                        slot, unit, n = m // f.blocks, m // f.hb % QT, m % f.hb
                        bank = RING[m % 4]
                        if m % f.blocks == 0:
                            pe.wait_ge(c_wlow.sem, c_wlow.at(st, it, (slot + 1) * f.chunks))
                        pe.wait_ge(c_high.sem, c_high.at(st, it, base + max(m - 3, 0)))
                        for kb in range(KB):
                            for a, c in PARTS:
                                last = pe.matmul(bank, w1(slot, a, kb, n), tokens[:, c, kb, unit * S:(unit + 1) * S],
                                                 start=(kb == 0 and (a, c) == PARTS[0]),
                                                 stop=(kb == KB - 1 and (a, c) == PARTS[-1]))
                        last.then_inc(c_hid.sem, 1)
                    i = m - f.ahead
                    if i >= 0:
                        slot, unit, n = i // f.blocks, i // f.hb, i % f.hb
                        pe.wait_ge(c_low.sem, c_low.at(st, it, base + i + 1))
                        for t in range(QT):
                            if n == 0:
                                pe.wait_ge(c_hD.sem, c_hD.at(st, it, max(unit - 1, 0) * QT + (t + 1 if unit else 0)))
                            for a, c in PARTS:
                                last = pe.matmul(OUTS[t][:, 0:D], hidden[:, i % 4, a, t * P:(t + 1) * P],
                                                 w2(slot, c, n), start=(n == 0 and (a, c) == PARTS[0]),
                                                 stop=(n == f.hb - 1 and (a, c) == PARTS[-1]))
                            if n == f.hb - 1:
                                last.then_inc(c_h.sem, 1)

            def logits(b):
                pe.wait_ge(c_tlow.sem, c_tlow.at(st, 0, (b + 1) * KB))
                if b == 0:
                    pe.wait_ge(c_gwsplit, 2)
                for t in range(b * QT, (b + 1) * QT):
                    for kb in range(KB):
                        for a in range(2):
                            last = pe.matmul(OUTS[3][:, t * 2 * E:(t + 1) * 2 * E],
                                             tokens[:, a, kb, t * P:(t + 1) * P],
                                             gwp[:, kb, :, :].rearrange("p a e -> p (a e)"),
                                             start=(kb == 0 and a == 0), stop=(kb == KB - 1 and a == 1))
                if b == B - 1:
                    last.then_inc(c_logits, 1)

            for b in range(B):
                for kb in range(KB):
                    j = b * KB + kb
                    if moe and kb == 0:
                        pe.wait_ge(c_xs.sem, c_xs.at(st, 0, b + 1))
                    if not moe and j == 0:
                        wait_x(pe, st, B - 1)
                    if j >= 4:
                        pe.wait_ge(c_tlow.sem, c_tlow.at(st, 0, j - 3))
                    for qt in range(QT):
                        src = xs[:, b % 2, qt, :] if moe else X[:, b * QT + qt, :]
                        last = pe.transpose(RING[j % 4][:, qt * P:(qt + 1) * P], src[:, kb * P:(kb + 1) * P],
                                            identf[:, :])
                    last.then_inc(c_turned.sem, 1)
                if moe and b >= 1:
                    logits(b - 1)
            if moe:
                logits(B - 1)
            else:
                pe.wait_ge(c_tlow.sem, c_tlow.at(st, 0, QT * KB))
            if moe:
                with pe.Fori(0, TURNS) as it:
                    turn(it, 0, PER_TURN)
                turn(TURNS, 0, 1)
            else:
                turn(0, 0, 1)

        @block.scalar
        def _(act):
            def split(it, slot, q, done):
                if q == 0:
                    act.wait_ge(c_raw, landed(it, done))
                act.activation(weights[:, slot, 0, chunk(q)], raw[:, chunk(q)], ACT.Copy).then_inc(c_whigh.sem, 1)

            def turn(it, experts):
                for m in range(experts * f.blocks):
                    slot, n, at = m // f.blocks, m % f.hb, m % f.blocks
                    act.wait_ge(c_hid.sem, c_hid.at(st, it, m + 1))
                    act.wait_ge(c_low.sem, c_low.at(st, it, max(m - 1, 0)))
                    for dst in (hidden[:, m % 4, 0, :], whole[:, m % 2, :]):
                        if moe:
                            last = act.activation(dst, RING[m % 4], ACT.Silu)
                        else:
                            last = act.activation(dst, RING[m % 4], ACT.Relu, bias=wcolf[:, n:n + 1], scale=1.0)
                    last.then_inc(c_high.sem, 1)
                    if experts > 1 and at in SPLIT:
                        split(it, 1 - slot, SPLIT[at], slot + 1)

            if moe:
                act.wait_ge(c_const, 112)
                act.activation(gwp[:, :, 0, :], gw[:, :, :], ACT.Copy)\
                    .then_inc(c_gwsplit, 1)
            else:
                act.wait_ge(c_rawb, 32 if st == "f0" else 64)
            wait_x(act, st, B - 1)
            for j in range(QT * KB):
                b, kb = j // KB, j % KB
                if moe and kb == 0:
                    for n in (0, 1) if b == 0 else (b + 1,) if b + 1 < QT else ():
                        if n >= 2:
                            act.wait_ge(c_turned.sem, c_turned.at(st, 0, (n - 1) * KB))
                        act.activation(xs[:, n % 2, :, :], X[:, n * QT:(n + 1) * QT, :], ACT.Square)\
                            .then_inc(c_sq.sem, 1)
                if j < f.chunks:
                    split(0, 0, j, 0)
                act.wait_ge(c_turned.sem, c_turned.at(st, 0, j + 1))
                dst = tokens[:, 0, kb, b * S:(b + 1) * S]
                if moe:
                    act.activation(dst, RING[j % 4], ACT.Identity, bias=0.0, scale=norm3[:, kb:kb + 1])\
                        .then_inc(c_thigh.sem, 1)
                else:
                    act.activation(dst, RING[j % 4], ACT.Copy).then_inc(c_thigh.sem, 1)
            if moe:
                act.wait_ge(c_gex, 1)
                act.activation(gex[:, 1, :], gex[:, 0, :], ACT.Exp).then_inc(c_gate, 1)
                with act.Fori(0, TURNS) as it:
                    turn(it, PER_TURN)
                turn(TURNS, 1)
            else:
                turn(0, 1)

        @block.vector
        def _(dve):
            def split(it, slot, q):
                dve.wait_ge(c_whigh.sem, c_whigh.at(st, it, q + 1))
                q %= f.chunks
                dve.tensor_tensor(weights[:, slot, 1, chunk(q)], raw[:, chunk(q)],
                                  weights[:, slot, 0, chunk(q)].bitcast(F32), ALU.subtract)\
                    .then_inc(c_wlow.sem, 1)

            def add(it, unit, experts):
                for t in range(QT):
                    n = unit % QT * QT + t
                    dve.wait_ge(c_h.sem, c_h.at(st, it, unit * QT + t + 1))
                    if moe:
                        gate = (gates[:, bass.ds(it * PER_TURN + unit // QT, 1), n:n + 1]
                                .rearrange("p o n -> p (o n)") if experts > 1 else gates[:, E, n:n + 1])
                        dve.scalar_tensor_tensor(out=X[:, n, :], in0=OUTS[t][:, 0:D], scalar=gate,
                                                 in1=X[:, n, :], op0=ALU.mult, op1=ALU.add).then_inc(c_hD.sem, 1)
                        continue
                    dve.tensor_tensor(junk[:, :], OUTS[t][:, 0:D], wrowf[:, 0, :], ALU.add).then_inc(c_hD.sem, 1)
                    dve.drain()
                    if f.masked:
                        dve.scalar_tensor_tensor(out=y[:, t % 2, :], in0=junk[:, :], scalar=keep[:, 0, n:n + 1],
                                                 in1=X[:, n, :], op0=ALU.mult, op1=ALU.add)
                    else:
                        dve.tensor_tensor(y[:, t % 2, :], junk[:, :], X[:, n, :], ALU.add)
                    moments(dve, st, unit, t)
                    if n >= 1:
                        centre(dve, st, (n - 1) // QT, (n - 1) % QT)
                if not moe and unit == QT - 1:
                    centre(dve, st, unit, QT - 1)

            def turn(it, experts):
                for m in range(experts * f.blocks):
                    slot, at = m // f.blocks, m % f.blocks
                    dve.wait_ge(c_high.sem, c_high.at(st, it, m + 1))
                    dve.tensor_tensor(hidden[:, m % 4, 1, :], whole[:, m % 2, :],
                                      hidden[:, m % 4, 0, :].bitcast(F32), ALU.subtract).then_inc(c_low.sem, 1)
                    if experts > 1 and at in SPLIT:
                        split(it, 1 - slot, SPLIT[at] + (slot + 1) * f.chunks)
                    i = m - f.ahead + 1
                    if i >= f.hb and i % f.hb == 0:
                        add(it, i // f.hb - 1, experts)
                add(it, experts * QT - 1, experts)

            def choose():
                flat = [gex[:, n, :] for n in range(4)]
                dve.wait_ge(c_logits, 1)
                both = OUTS[3][:, 0:NT * 2 * E].rearrange("p (n a e) -> p n a e", n=NT, a=2)
                dve.tensor_copy(lg[:, :, :], both[:, :, 0, :])
                dve.drain()
                dve.tensor_tensor(lg[:, :, :], lg[:, :, :], both[:, :, 1, :], ALU.add)
                dve.drain()
                for n in range(NT):
                    dve.max(top[:, n, :], lg[:, n, :])
                dve.drain()
                dve.tensor_tensor(flat[0], top[:, :, 1], top[:, :, 0], ALU.subtract).then_inc(c_gex, 1)
                for n in range(NT):
                    dve.max_index(topi[:, n, :], top[:, n, :], lg[:, n, :])
                dve.drain()
                dve.tensor_copy(topf[:, :, :], topi[:, :, 0:2])
                dve.wait_ge(c_gate, 1)
                dve.tensor_scalar(flat[2], flat[1], 1.0, None, ALU.add)
                dve.drain()
                dve.reciprocal(flat[2], flat[2])
                dve.drain()
                dve.tensor_tensor(flat[3], flat[1], flat[2], ALU.mult)
                for c in range(2):
                    dve.tensor_tensor(gpart[:, c, :, :], iota8[:, :].unsqueeze(1).to_broadcast([P, NT, E]),
                                      topf[:, :, c:c + 1].to_broadcast([P, NT, E]), ALU.is_equal)
                dve.drain()
                for c in range(2):
                    dve.tensor_tensor(gpart[:, c, :, :], gpart[:, c, :, :],
                                      flat[2 + c].unsqueeze(2).to_broadcast([P, NT, E]), ALU.mult)
                dve.drain()
                dve.tensor_tensor(gates[:, 0:E, :].rearrange("p e n -> p n e"), gpart[:, 0, :, :],
                                  gpart[:, 1, :, :], ALU.add)
                dve.drain()

            if moe:
                dve.wait_ge(c_gwsplit, 1)
                dve.tensor_tensor(gwp[:, :, 1, :], gw[:, :, :], gwp[:, :, 0, :].bitcast(F32),
                                  ALU.subtract).then_inc(c_gwsplit, 1)
            else:
                dve.wait_ge(c_rawb, 32 if st == "f0" else 64)

            def mean_square(b):
                dve.drain()
                dve.wait_ge(c_sq.sem, c_sq.at(st, 0, b + 1))
                dve.tensor_reduce(ss[:, :], xs[:, b % 2, :, :], AX.X, ALU.add)
                dve.drain()
                if b >= 1:
                    dve.wait_ge(c_xs.sem, c_xs.at(st, 0, b))
                dve.tensor_scalar(ms[:, :], ss[:, :], 1.0 / D, 1e-5, ALU.mult, ALU.add).then_inc(c_ss.sem, 1)

            wait_x(dve, st, B - 1)
            if moe:
                mean_square(0)
            for j in range(QT * KB):
                b, kb = j // KB, j % KB
                if moe and kb == 0 and b + 1 < B:
                    mean_square(b + 1)
                dve.wait_ge(c_thigh.sem, c_thigh.at(st, 0, j + 1))
                dve.scalar_tensor_tensor(
                    out=tokens[:, 1, kb, b * S:(b + 1) * S], in0=RING[j % 4],
                    scalar=norm3[:, kb:kb + 1] if moe else 1.0, in1=tokens[:, 0, kb, b * S:(b + 1) * S].bitcast(F32),
                    op0=ALU.mult, op1=ALU.subtract).then_inc(c_tlow.sem, 1)
                if j < f.chunks:
                    split(0, 0, j)
            if moe:
                choose()
                with dve.Fori(0, TURNS) as it:
                    turn(it, PER_TURN)
                turn(TURNS, 1)
            else:
                turn(0, 1)


    for stages in BLOCKS:
        with ExitStack() as mem:
            (feed_block if stages[0] in FEED else attention_block)(mem, stages)


def kernel(**inputs):
    import ml_dtypes
    import numpy as np
    import concourse.bacc as bacc
    from concourse.bass_utils import run_bass_kernel_spmd

    v = {name: np.asarray(a) for name, a in inputs.items()}

    def rows(w):
        return w.reshape(-1, P, w.shape[-1]).transpose(1, 0, 2)

    def expert(w1, w2):
        return np.concatenate([rows(w1).reshape(P, -1), rows(w2).reshape(P, -1)], 1)

    zero = np.zeros(D, np.float32)
    zeros = np.zeros((D, D), np.float32)

    def heads(w):
        return w.transpose(1, 0, 2).reshape(D, D)

    L0, L1, L2, L3 = "L0_xattn_", "L1_xattn_", "L2_xattn_", "L3_xattn_"
    ws = []
    for n in (1, 2):
        ws.append([heads(v[f"{L0}W{c}{n}"]) for c in "qkv"] + [zeros, zero, zero, zero, zero,
                  v[f"{L0}ln{n}_g"], v[f"{L0}ln{n}_b"], zero])
    for n, p in ((1, "sa"), (2, "ca")):
        ws.append([v[f"{L1}{p}_w{c}"].T for c in "qkvo"] + [zero] * 6 + [v[f"{L1}norm{n}_w"]])
    for n, p in ((1, "sa"), (2, "ca")):
        ws.append([v[f"{L2}{p}_w{c}"] for c in "qkvo"] + [v[f"{L2}{p}_b{c}"] for c in "qkvo"]
                  + [v[f"{L2}ln{n}_g"], v[f"{L2}ln{n}_b"], zero])
    ws.append([v[f"{L3}W{c}"] for c in "qkv"] + [zeros] + [v[f"{L3}b{c}"] for c in "qkv"]
              + [zero, v[f"{L3}gamma"], v[f"{L3}beta"], zero])

    def spread(*vectors):
        return np.broadcast_to(np.stack(vectors)[None], (P, len(vectors), D))

    arrays = {"x": v["x"], "ctx": v["ctx_1024"],
              "ctxT": v["ctx_1024"].transpose(0, 2, 1).reshape(B, KB, P, S).transpose(0, 2, 1, 3),
              "mask0": v["mask_BxSxS_ik0"], "mask1": v["mask_BxSxS2_if1"], "mask2": v["mask_BxSxS2_ik0"]}
    for n, (wq, wk, wv, wo, bq, bk, bv, bo, g, be, nw) in enumerate(ws):
        arrays[f"w{n}"] = rows(np.concatenate([wq, wk, wv, wo], 1))
        arrays[f"col{n}"] = np.concatenate([bq.reshape(KB, P), bk.reshape(KB, P), nw.reshape(KB, P)]).T
        arrays[f"row{n}"] = spread(bv, bo, g, be)
    for st, w1, b1, w2, b2, g, be in (
            ("f0", v[L0 + "fc1_w"].T, v[L0 + "fc1_b"], v[L0 + "fc2_w"].T, v[L0 + "fc2_b"],
             v[L0 + "ln3_g"], v[L0 + "ln3_b"]),
            ("f2", v[L2 + "ff_w1"], v[L2 + "ff_b1"], v[L2 + "ff_w2"], v[L2 + "ff_b2"],
             v[L2 + "ln3_g"], v[L2 + "ln3_b"])):
        arrays[f"{st}w"] = expert(w1, w2)
        arrays[f"{st}col"], arrays[f"{st}row"] = b1.reshape(-1, P).T, spread(b2, g, be)
    arrays["moew"] = np.stack([expert(v[L1 + "exp_w1"][e].T, v[L1 + "exp_w2"][e].T) for e in range(E)]
                              + [expert(v[L1 + "sh_w1"].T, v[L1 + "sh_w2"].T)])
    arrays["gw"] = rows(v[L1 + "gate_w"].T)
    arrays["norm3"] = v[L1 + "norm3_w"].reshape(KB, P).T

    bf16 = ml_dtypes.bfloat16
    p = np.arange(P)
    arrays["identf"] = np.eye(P, dtype=np.float32)
    arrays["identb"] = np.eye(P).astype(bf16)
    arrays["causal"] = np.where(p[None, :] > p[:, None], BIG, 0.0).astype(bf16)
    arrays["selq"] = (np.arange(32)[None, None, :] == (2 * np.arange(GS)[None, :, None] + p[:, None, None] // 64))\
        .astype(np.float32)
    arrays["iota"] = np.broadcast_to(np.arange(S, dtype=np.float32), (16, S))
    arrays["iota8"] = np.broadcast_to(np.arange(E, dtype=np.float32), (P, E))
    column = np.arange(SELW)[None, :] - 64
    for dk in (16, 32):
        own = (column >= 0) & (column // (4 * dk) == p[:, None] // dk) & (column % dk == p[:, None] % dk)
        which = column // dk % 4
        arrays[f"select{dk}"] = np.stack([own & (which % 2 == 0), own & (which < 2)], 1).astype(np.float32)

    nc = bacc.Bacc("TRN2", target_bir_lowering=False, num_devices=1)
    arrays = {name: np.ascontiguousarray(a) for name, a in arrays.items()}
    io = {name: nc.dram_tensor(f"in_{name}", a.shape, mybir.dt.from_np(a.dtype), kind="ExternalInput").ap()
          for name, a in arrays.items()}
    io["out"] = nc.dram_tensor("out", (B, S, D), F32, kind="ExternalOutput").ap()
    with ExitStack() as ctx:
        build(nc, io, ctx)
    r = run_bass_kernel_spmd(nc, [{f"in_{name}": a for name, a in arrays.items()}], core_ids=[0])
    return r.results[0]["out"]
```
